# Optimizing a Trainium2 kernel written in Bass

```python
import numpy as np
import jax
import jax.numpy as jnp

def _softmax(x, axis=-1):
    return jax.nn.softmax(x, axis=axis)

def _gelu(x):
    return jax.nn.gelu(x, approximate=True)

def _silu(x):
    return jax.nn.silu(x)

def _sigmoid(x):
    return jax.nn.sigmoid(x)

def _layernorm(x, axis=-1, eps=1e-05):
    m = jnp.mean(x, axis=axis, keepdims=True)
    v = jnp.var(x, axis=axis, keepdims=True)
    return (x - m) / jnp.sqrt(v + eps)

def _scatter_add(tgt, idx, src, axis=0):
    return tgt.at[idx].add(src)

def _segment_sum(src, seg, n):
    return jax.ops.segment_sum(src, seg, n)
kernel_name = 'mk_gnn_preln_d2_gnn_r8_f8f118'

def setup_inputs(seed: int=0):
    np.random.seed(seed)
    _w = jnp.asarray

    def _rec_inputs():
        import jax
        import jax.numpy as jnp
        _gk = jax.random.key(seed)
        x = -0.0002221 + 1 * jax.random.normal(jax.random.fold_in(_gk, 1), (1250, 768), jnp.float32)
        src = jax.random.randint(jax.random.fold_in(_gk, 2), (20000,), 0, 1250, jnp.int32)
        dst = jnp.minimum((1250 * jax.random.uniform(jax.random.fold_in(_gk, 3), (20000,)) ** 2.0).astype(jnp.int32), 9999)
        _o = jnp.argsort(dst, stable=True)
        src = src[_o]
        dst = dst[_o]
        edge_type_3 = jax.random.randint(jax.random.fold_in(_gk, 13), (20000,), 0, 3, jnp.int32)
        return (x, src, dst, edge_type_3)
    x, src, dst, edge_type_3 = _rec_inputs()

    def _L0_gnn_setup():
        import jax, jax.numpy as jnp
        import numpy as np
        NEG_SLOPE = 0.2
        EPS = 1e-16
        N_NODES = 4096
        N_EDGES = 20000
        DIM = 768
        HEADS1 = 4
        OUT1 = DIM // HEADS1
        HEADS2 = 1
        OUT2 = DIM
        N_REL = 3

        def rgat_conv(x, W, q, k, b, src, dst, etype, heads, out_ch, n_nodes):
            xr = jnp.einsum('nd,rdf->rnf', x, W)
            oi = xr[etype, dst]
            oj = xr[etype, src]
            qi = oi @ q
            kj = oj @ k
            alpha = jax.nn.leaky_relu(qi + kj, NEG_SLOPE)
            m = jax.ops.segment_max(alpha, dst, num_segments=n_nodes)
            e = jnp.exp(alpha - m[dst])
            z = jax.ops.segment_sum(e, dst, num_segments=n_nodes)
            a = e / (z[dst] + EPS)
            msg = (a[:, :, None] * oj.reshape(-1, heads, out_ch)).reshape(-1, heads * out_ch)
            out = jax.ops.segment_sum(msg, dst, num_segments=n_nodes)
            return out + b
        key = jax.random.key(seed)
        ks = jax.random.split(key, 12)
        s = 0.02
        return {'x': jax.random.normal(ks[0], (N_NODES, DIM), dtype=jnp.float32), 'edge_index': jax.random.randint(ks[1], (2, N_EDGES), 0, N_NODES, dtype=jnp.int64), 'edge_type': jax.random.randint(ks[2], (N_EDGES,), 0, N_REL, dtype=jnp.int64), 'W1': jax.random.normal(ks[3], (N_REL, DIM, HEADS1 * OUT1), dtype=jnp.float32) * s, 'q1': jax.random.normal(ks[4], (HEADS1 * OUT1, HEADS1), dtype=jnp.float32) * s, 'k1': jax.random.normal(ks[5], (HEADS1 * OUT1, HEADS1), dtype=jnp.float32) * s, 'b1': jnp.zeros((HEADS1 * OUT1,), dtype=jnp.float32), 'W2': jax.random.normal(ks[6], (N_REL, DIM, HEADS2 * OUT2), dtype=jnp.float32) * s, 'q2': jax.random.normal(ks[7], (HEADS2 * OUT2, HEADS2), dtype=jnp.float32) * s, 'k2': jax.random.normal(ks[8], (HEADS2 * OUT2, HEADS2), dtype=jnp.float32) * s, 'b2': jnp.zeros((HEADS2 * OUT2,), dtype=jnp.float32)}
    _L0_gnn_all = _L0_gnn_setup()
    _L0_gnn_in = {k: v for k, v in _L0_gnn_all.items() if k in ('W1', 'q1', 'k1', 'b1', 'W2', 'q2', 'k2', 'b2')}
    del _L0_gnn_all

    def _L1_gnn_setup():
        import jax, jax.numpy as jnp
        import numpy as np
        N = 2500
        DEG = 16
        E = N * DEG
        H = 12
        DIN = 64
        DOUT = 64
        NEG_SLOPE = 0.2
        key = jax.random.key(seed)
        k_h, k_src, k_w, k_al, k_ar, k_wr = jax.random.split(key, 6)
        std = 1.414 * np.sqrt(2.0 / (DIN + DOUT))
        h = jax.random.normal(k_h, (N, H * DIN), dtype=jnp.float32)
        src = jax.random.randint(k_src, (E,), 0, N, dtype=jnp.int64)
        dst = jnp.repeat(jnp.arange(N, dtype=jnp.int64), DEG)
        W = jax.random.normal(k_w, (DOUT, DIN), dtype=jnp.float32) * std
        attn_l = jax.random.normal(k_al, (1, H, DOUT), dtype=jnp.float32) * std
        attn_r = jax.random.normal(k_ar, (1, H, DOUT), dtype=jnp.float32) * std
        W_res = jax.random.normal(k_wr, (DOUT, DIN), dtype=jnp.float32) * std
        return {'h': h, 'src': src, 'dst': dst, 'W': W, 'attn_l': attn_l, 'attn_r': attn_r, 'W_res': W_res}
    _L1_gnn_all = _L1_gnn_setup()
    _L1_gnn_in = {k: v for k, v in _L1_gnn_all.items() if k in ('W', 'attn_l', 'attn_r', 'W_res')}
    del _L1_gnn_all
    return {'x': x, 'src': src, 'dst': dst, 'edge_type_3': edge_type_3, 'L0_gnn_W1': _L0_gnn_in['W1'], 'L0_gnn_q1': _L0_gnn_in['q1'], 'L0_gnn_k1': _L0_gnn_in['k1'], 'L0_gnn_b1': _L0_gnn_in['b1'], 'L0_gnn_W2': _L0_gnn_in['W2'], 'L0_gnn_q2': _L0_gnn_in['q2'], 'L0_gnn_k2': _L0_gnn_in['k2'], 'L0_gnn_b2': _L0_gnn_in['b2'], 'L1_gnn_W': _L1_gnn_in['W'], 'L1_gnn_attn_l': _L1_gnn_in['attn_l'], 'L1_gnn_attn_r': _L1_gnn_in['attn_r'], 'L1_gnn_W_res': _L1_gnn_in['W_res']}

def reference(x, src, dst, edge_type_3, L0_gnn_W1, L0_gnn_q1, L0_gnn_k1, L0_gnn_b1, L0_gnn_W2, L0_gnn_q2, L0_gnn_k2, L0_gnn_b2, L1_gnn_W, L1_gnn_attn_l, L1_gnn_attn_r, L1_gnn_W_res):
    import jax
    import jax.numpy as jnp

    def _L0_gnn_ref(x, edge_index, edge_type, W1, q1, k1, b1, W2, q2, k2, b2):
        import jax, jax.numpy as jnp
        import numpy as np
        NEG_SLOPE = 0.2
        EPS = 1e-16
        N_NODES = 4096
        N_EDGES = 20000
        DIM = 768
        HEADS1 = 4
        OUT1 = DIM // HEADS1
        HEADS2 = 1
        OUT2 = DIM
        N_REL = 3

        def rgat_conv(x, W, q, k, b, src, dst, etype, heads, out_ch, n_nodes):
            xr = jnp.einsum('nd,rdf->rnf', x, W)
            oi = xr[etype, dst]
            oj = xr[etype, src]
            qi = oi @ q
            kj = oj @ k
            alpha = jax.nn.leaky_relu(qi + kj, NEG_SLOPE)
            m = jax.ops.segment_max(alpha, dst, num_segments=n_nodes)
            e = jnp.exp(alpha - m[dst])
            z = jax.ops.segment_sum(e, dst, num_segments=n_nodes)
            a = e / (z[dst] + EPS)
            msg = (a[:, :, None] * oj.reshape(-1, heads, out_ch)).reshape(-1, heads * out_ch)
            out = jax.ops.segment_sum(msg, dst, num_segments=n_nodes)
            return out + b
        src, dst = (edge_index[0], edge_index[1])
        n = x.shape[0]
        h = rgat_conv(x, W1, q1, k1, b1, src, dst, edge_type, HEADS1, OUT1, n)
        h = jax.nn.elu(h)
        out = rgat_conv(h, W2, q2, k2, b2, src, dst, edge_type, HEADS2, OUT2, n)
        return out

    def _L1_gnn_ref(h, src, dst, W, attn_l, attn_r, W_res):
        import jax, jax.numpy as jnp
        import numpy as np
        N = 2500
        DEG = 16
        E = N * DEG
        H = 12
        DIN = 64
        DOUT = 64
        NEG_SLOPE = 0.2
        n = h.shape[0]
        hv = h.reshape(n, H, DIN)
        ft = jnp.einsum('nhd,od->nho', hv, W)
        a1 = jnp.sum(ft * attn_l, axis=-1)
        a2 = jnp.sum(ft * attn_r, axis=-1)
        e = jax.nn.leaky_relu(a1[src] + a2[dst], negative_slope=NEG_SLOPE)
        m = jax.ops.segment_max(e, dst, num_segments=n)
        m = jnp.where(jnp.isfinite(m), m, 0.0)
        w = jnp.exp(e - m[dst])
        denom = jax.ops.segment_sum(w, dst, num_segments=n)
        alpha = w / jnp.maximum(denom[dst], 1e-16)
        msg = alpha[:, :, None] * ft[src]
        agg = jax.ops.segment_sum(msg, dst, num_segments=n)
        res = jnp.einsum('nhd,od->nho', hv, W_res)
        out = jax.nn.relu((agg + res).reshape(n, H * DOUT))
        return out
    edge_index = jnp.stack([src, dst])
    h = jnp.maximum(_layernorm(x, axis=-1), 0.0)
    x = x + _L0_gnn_ref(h, edge_index, edge_type_3, L0_gnn_W1, L0_gnn_q1, L0_gnn_k1, L0_gnn_b1, L0_gnn_W2, L0_gnn_q2, L0_gnn_k2, L0_gnn_b2)
    h = jnp.maximum(_layernorm(x, axis=-1), 0.0)
    x = x + _L1_gnn_ref(h, src, dst, L1_gnn_W, L1_gnn_attn_l, L1_gnn_attn_r, L1_gnn_W_res)
    return x

_drawn_inputs = setup_inputs


def setup_inputs(seed=0):
    import zlib

    import numpy as np

    out = dict(_drawn_inputs(seed))
    spreads = {'L0_gnn_b1': (0.0, 0.1), 'L0_gnn_b2': (0.0, 0.1)}
    factors = {'L0_gnn_q1': 8.0, 'L0_gnn_k1': 8.0, 'L0_gnn_q2': 29.177, 'L0_gnn_k2': 27.416}
    for name, (base, spread) in spreads.items():
        noise = np.random.default_rng([zlib.crc32(name.encode()), seed]).standard_normal(out[name].shape)
        drawn = base * np.exp(spread * noise) if base else spread * noise
        out[name] = jnp.asarray(drawn.astype(out[name].dtype))
    for name, factor in factors.items():
        out[name] = (out[name] * factor).astype(out[name].dtype)
    return out
```

```python
from contextlib import ExitStack

import numpy as np
import concourse.bass as bass
from concourse import mybir

ALU = mybir.AluOpType
ACT = mybir.ActivationFunctionType
F32 = mybir.dt.float32
I32 = mybir.dt.int32
U16 = mybir.dt.uint16
BF16 = mybir.dt.bfloat16
AX = mybir.AxisListType.X

P = 128
BIG = 1.0e30
SLOPE = 0.2
Z_EPS = 1.0e-16
LN_EPS = 1.0e-5
SLOTS = 5
GROUPS = [(0, 4), (4, 4), (8, 2)]


class Graph:

    def __init__(self, x, src):
        self.N, self.D = x.shape
        self.E = src.shape[0]
        self.NT = -(-self.N // P)
        self.NP = self.NT * P
        self.LAST = self.N - (self.NT - 1) * P
        self.KD = self.D // P
        self.R = 3
        assert self.NT == sum(w for _, w in GROUPS)


def load_nodes(eng, g, sbuf, dram, sem):
    full = (g.NT - 1) * P
    eng.dma_start(sbuf[:, 0:g.NT - 1, :], dram[0:full, :].rearrange("(t p) d -> p t d", p=P)).then_inc(sem, 16)
    eng.dma_start(sbuf[0:g.LAST, g.NT - 1, :], dram[full:g.N, :]).then_inc(sem, 16)


def layernorm_stats(dve, g, x, stats, mv, sem):
    half = g.D // 2
    for t in range(g.NT):
        for i in range(2):
            dve.bn_stats(stats[:, t, i, :], x[:, t, i * half:(i + 1) * half]).then_inc(sem, 1)
    for t in range(g.NT):
        dve.wait_ge(sem, 2 * (t + 1))
        dve.bn_aggr(mv[:, t, :], stats[:, t]).then_inc(sem, 1)


def tables_and_counts(nc, g, x, src, dst, etype, W1, q1, k1, W2, q2, k2, ident, kq1, wqk2, feat1, counts):
    N, D, NT, NP, KD, R = g.N, g.D, g.NT, g.NP, g.KD, g.R
    H, F = 4, D // 4
    CELLS = R * NP * NP
    EC_FULL = g.E // P
    EC_USED = -(-g.E // P)
    EC = -(-EC_USED // 8) * 8
    TAIL = g.E - EC_FULL * P
    ZC = CELLS // P // 10
    NW = 2 * R
    with ExitStack() as ctx:
        sb = lambda n, s, d=F32: ctx.enter_context(nc.sbuf_tensor(n, s, d))
        sem = lambda n: ctx.enter_context(nc.semaphore(n))
        edges_i = sb("edges_i", [P, 3, EC], I32)
        edges_f = sb("edges_f", [P, 3, EC])
        key = sb("key", [P, EC])
        key_i = sb("key_i", [P, EC], I32)
        packed = sb("packed", [P, EC])
        zero = sb("zero", [P, ZC])
        ones = sb("ones", [P, P])
        earlier = sb("earlier", [P, P])
        diag = sb("diag", [P, 2, 4, P])
        same = sb("same", [P, 8, P])
        h = sb("h", [P, NT, D])
        hT = sb("hT", [P, KD, NP])
        stats = sb("stats", [P, NT, 2, 6])
        mv = sb("mv", [P, NT, 2])
        std = sb("std", [P, NT])
        rstd = sb("rstd", [P, NT])
        shift = sb("shift", [P, NT])
        eps = sb("eps", [P, 1])
        w = sb("w", [P, 2, KD, D])
        wT = sb("wT", [P, KD, D])
        qk1 = sb("qk1", [P, KD, 2 * H])
        qk2 = sb("qk2", [P, 2, KD])
        wqk1 = sb("wqk1", [P, KD, R, 2 * H])
        stage = sb("stage", [P, 2, H, F + 1])
        ps_turn = ctx.enter_context(nc.psum_tensor("ps_turn", [P, 2, 512], F32))
        ps_feat = ctx.enter_context(nc.psum_tensor("ps_feat", [P, 2, 2, 512], F32))
        ps_small = ctx.enter_context(nc.psum_tensor("ps_small", [P, 512], F32))
        ps_key = ctx.enter_context(nc.psum_tensor("ps_key", [P, 512], F32))

        s_clean = sem("a_clean")
        s_const = sem("a_const")
        s_zero = sem("a_zero")
        s_edges = sem("a_edges")
        s_x = sem("a_x")
        s_qk = sem("a_qk")
        s_cleared = sem("a_cleared")
        s_w = [sem("a_w0"), sem("a_w1")]
        s_wused = sem("a_wused")
        s_stat = sem("a_stat")
        s_norm = sem("a_norm")
        s_h = sem("a_h")
        s_turn = sem("a_turn")
        s_turned = sem("a_turned")
        s_wqk = sem("a_wqk")
        s_wqk_out = sem("a_wqk_out")
        s_feat = sem("a_feat")
        s_feat_out = sem("a_feat_out")
        s_spill = [sem("a_spill0"), sem("a_spill1")]
        s_key = sem("a_keys")
        s_diag = sem("a_diag")
        s_bcast = sem("a_bcast")
        s_same = sem("a_same")
        s_index = sem("a_index")
        s_scat = [sem("a_scat0"), sem("a_scat1")]
        block = ctx.enter_context(nc.Block())

        @block.sync
        def _(sp):
            sp.wait_ge(s_clean, 2)
            for i, a in enumerate((src, dst, etype)):
                sp.dma_start(edges_i[:, i, 0:EC_FULL],
                             a[0:EC_FULL * P].rearrange("(p c) -> p c", p=P)).then_inc(s_edges, 16)
                sp.dma_start(edges_i[0:TAIL, i, EC_FULL:EC_FULL + 1],
                             a[EC_FULL * P:g.E].rearrange("(p c) -> p c", c=1)).then_inc(s_edges, 16)
            load_nodes(sp, g, h, x, s_x)
            for vec, sl in ((q1, qk1[:, :, 0:H]), (k1, qk1[:, :, H:2 * H])):
                sp.dma_start(sl, vec.rearrange("(k p) h -> p k h", p=P)).then_inc(s_qk, 16)
            for c, vec in enumerate((q2, k2)):
                sp.dma_start(qk2[:, c, :], vec.rearrange("(k p) h -> p (k h)", p=P),
                             allow_slow_non_contiguous=True).then_inc(s_qk, 16)

            def load_w(i):
                big = (W1 if i < R else W2)[i % R]
                sp.dma_start(w[:, i % 2], big.rearrange("(k p) f -> p k f", p=P)).then_inc(s_w[i % 2], 16)

            load_w(0)
            load_w(1)
            sp.wait_ge(s_zero, 1)
            for table in counts:
                flat = table.rearrange("(k p c) o -> k p (c o)", p=P, k=10)
                for k in range(10):
                    sp.dma_start(flat[k], zero[:]).then_inc(s_cleared, 16)
            for i in range(2, NW):
                sp.wait_ge(s_wused, i - 1)
                load_w(i)
            for q in (0, 1):
                sp.wait_ge(s_spill[q], 16 * R * NT // 2)
                sp.wait_ge(s_scat[q], 16 * len(range(q, EC_USED, 2)))

        @block.gpsimd
        def _(pool):
            pool.memset(edges_i[:], R).then_inc(s_clean, 1)
            pool.memset(h[:, NT - 1, :], 0.0).then_inc(s_clean, 1)
            pool.memset(ident[:], 0.0).then_inc(s_const, 1)
            pool.memset(earlier[:], float(2 * P + 1)).then_inc(s_const, 1)
            pool.memset(ones[:], 1.0).then_inc(s_const, 1)
            pool.memset(eps[:], LN_EPS).then_inc(s_const, 1)
            pool.memset(stage[:], 1.0).then_inc(s_const, 1)
            pool.wait_ge(s_const, 2)
            pool.affine_select(out=ident[:], in_=ident[:], compare_op=ALU.not_equal, fill=1.0, base=0,
                               pattern=[[-1, P]], channel_multiplier=1).then_inc(s_const, 1)
            pool.affine_select(out=earlier[:], in_=earlier[:], compare_op=ALU.is_gt, fill=1.0, base=0,
                               pattern=[[-1, P]], channel_multiplier=1).then_inc(s_const, 1)
            pool.wait_ge(s_const, 7)
            pool.wait_ge(s_key, 3)
            for d in range(2):
                pool.sem_inc(s_bcast, 1)
            with pool.Fori(0, EC // 8) as i:
                for b in range(2):
                    pool.wait_ge(s_bcast, i * 2 + b + 1)
                    pool.tensor_tensor(diag[:, b], ident[:].rearrange("p (a e) -> p a e", a=1).broadcast_to([P, 4, P]),
                                       key[:, bass.ds(i * 8 + b * 4, 4)].rearrange("p (a e) -> p a e", e=1)
                                       .broadcast_to([P, 4, P]), ALU.mult).then_inc(s_diag, 1)
            pool.wait_ge(s_index, 1)
            pool.wait_ge(s_cleared, 16 * 20)
            for c in range(EC_USED):
                if c >= 2:
                    pool.wait_ge(s_scat[c % 2], 16 * (c // 2))
                pool.indirect_dma_start(out=counts[c % 2],
                                        out_offset=bass.IndirectOffsetOnAxis(ap=key_i[:, c:c + 1], axis=0),
                                        in_=packed[:, c:c + 1], in_offset=None, bounds_check=CELLS - 1,
                                        oob_is_err=False, compute_op=ALU.add).then_inc(s_scat[c % 2], 16)

        @block.tensor
        def _(pe):
            turns = [0]

            def turn(blocks):
                n = turns[0]
                turns[0] += 1
                if n >= 2:
                    pe.wait_ge(s_turned, n - 1)
                for j, blk in enumerate(blocks):
                    last = pe.transpose(ps_turn[:, n % 2, j * P:(j + 1) * P], blk, ident[:])
                last.then_inc(s_turn, 1)

            def weights_turned(i):
                pe.wait_ge(s_w[i % 2], 16 * (i // 2 + 1))
                for f in range(KD):
                    for half in range(2):
                        turn([w[:, i % 2, 3 * half + j, f * P:(f + 1) * P] for j in range(3)])

            def logit_weights(i):
                c = 2 * H if i < R else 2
                pe.wait_ge(s_turned, turns[0])
                if i >= 1:
                    pe.wait_ge(s_wqk_out, 2 * i if i <= R else R + i)
                for kd in range(KD):
                    for f in range(KD):
                        last = pe.matmul(ps_small[:, kd * c:(kd + 1) * c], wT[:, f, kd * P:(kd + 1) * P],
                                         qk1[:, f, :] if i < R else qk2[:, :, f],
                                         start=(f == 0), stop=(f == KD - 1), skip_group_check=True)
                last.then_inc(s_wqk, 1)

            pe.wait_ge(s_const, 7)
            pe.wait_ge(s_qk, 64)
            weights_turned(0)
            logit_weights(0)
            for t in range(NT):
                pe.wait_ge(s_h, t + 1)
                for half in range(2):
                    turn([h[:, t, (3 * half + j) * P:(3 * half + j + 1) * P] for j in range(3)])
            for i in range(NW):
                if i > 0:
                    weights_turned(i)
                    logit_weights(i)
                if i < R:
                    pe.wait_ge(s_wqk_out, 2 * i + 1)
                    pe.wait_ge(s_turned, turns[0])
                    for t in range(NT):
                        for kd in range(KD):
                            last = pe.matmul(ps_small[:, t * 2 * H:(t + 1) * 2 * H], hT[:, kd, t * P:(t + 1) * P],
                                             wqk1[:, kd, i, :], start=(kd == 0), stop=(kd == KD - 1),
                                             skip_group_check=True)
                    last.then_inc(s_wqk, 1)
                    for t in range(NT):
                        n = i * NT + t
                        if n >= 2:
                            pe.wait_ge(s_feat_out, 2 * (n - 1))
                        for half in range(2):
                            for kd in range(KD):
                                last = pe.matmul(ps_feat[:, n % 2, half, 0:D // 2], hT[:, kd, t * P:(t + 1) * P],
                                                 w[:, i % 2, kd, half * D // 2:(half + 1) * D // 2],
                                                 start=(kd == 0), stop=(kd == KD - 1))
                        last.then_inc(s_feat, 1)
                        if n < EC // 32:
                            for b in range(8):
                                m = n * 8 + b
                                pe.wait_ge(s_diag, m + 1)
                                pe.wait_ge(s_same, 4 * m + 8)
                                pe.matmul(ps_key[:], ones[:], diag[:, m % 2].rearrange("p a e -> p (a e)"),
                                          start=True, stop=True).then_inc(s_bcast, 1)
                pe.wait_ge(s_feat if i < R else s_wqk, (i + 1) * NT if i < R else 2 * R + (i - R) + 1)
                pe.sem_inc(s_wused, 1)

        @block.scalar
        def _(act):
            act.wait_ge(s_const, 7)
            act.wait_ge(s_stat, 3 * NT)
            act.activation(std[:], mv[:, :, 1], ACT.Sqrt, bias=eps[:]).then_inc(s_norm, 1)
            act.wait_ge(s_norm, 3)
            for t in range(NT):
                act.activation(h[:, t, :], h[:, t, :], ACT.Relu, bias=shift[:, t:t + 1],
                               scale=rstd[:, t:t + 1]).then_inc(s_h, 1)
            for t in range(NT):
                for half in range(2):
                    n = 2 * KD + 2 * t + half
                    act.wait_ge(s_turn, n + 1)
                    act.copy(hT[:, 3 * half:3 * half + 3, t * P:(t + 1) * P],
                             ps_turn[:, n % 2, 0:3 * P].rearrange("p (k n) -> p k n", k=3)).then_inc(s_turned, 1)
            for q in range(2):
                act.sem_inc(s_spill[q], 16)
            with act.Fori(0, R * NT // 2) as i:
                for q in range(2):
                    act.wait_ge(s_feat, i * 2 + q + 1)
                    act.wait_ge(s_spill[q], i * 16 + 16)
                    for half in range(2):
                        act.copy(stage[:, q, 2 * half:2 * half + 2, 0:F],
                                 ps_feat[:, q, half, 0:2 * F].rearrange("p (a f) -> p a f", a=2)).then_inc(s_feat_out, 1)
                    act.wait_ge(s_feat_out, i * 4 + 2 * q + 2)
                    act.dma_start(feat1[:, bass.ds(i * 2 + q, 1)].rearrange("h n p f -> p (n h) f"),
                                  stage[:, q]).then_inc(s_spill[q], 16)
            for q in range(2):
                act.wait_ge(s_spill[q], 16 * (R * NT // 2) + 16)

        @block.vector
        def _(dve):
            dve.memset(zero[:], 0.0).then_inc(s_zero, 1)
            dve.wait_ge(s_edges, 96)
            dve.tensor_copy(edges_f[:], edges_i[:]).then_inc(s_key, 1)
            dve.wait_ge(s_key, 1)
            dve.scalar_tensor_tensor(out=packed[:], in0=edges_f[:, 2, :], scalar=float(NP), in1=edges_f[:, 0, :],
                                     op0=ALU.mult, op1=ALU.add).then_inc(s_key, 1)
            dve.wait_ge(s_key, 2)
            dve.scalar_tensor_tensor(out=key[:], in0=packed[:], scalar=float(NP), in1=edges_f[:, 1, :],
                                     op0=ALU.mult, op1=ALU.add).then_inc(s_key, 1)
            dve.wait_ge(s_key, 3)
            dve.wait_ge(s_x, 32)
            layernorm_stats(dve, g, h, stats, mv, s_stat)
            dve.wait_ge(s_norm, 1)
            dve.reciprocal(rstd[:], std[:]).then_inc(s_norm, 1)
            dve.wait_ge(s_norm, 2)
            dve.scalar_tensor_tensor(out=shift[:], in0=mv[:, :, 0], scalar=-1.0, in1=rstd[:],
                                     op0=ALU.mult, op1=ALU.mult).then_inc(s_norm, 1)

            def weights_out(i):
                if i > 0:
                    dve.wait_ge(s_wqk, 2 * i - 1 if i <= R else R + i)
                for f in range(KD):
                    for half in range(2):
                        n = 12 * i + 2 * f + half + (2 * NT if i > 0 else 0)
                        dve.wait_ge(s_turn, n + 1)
                        dve.tensor_copy(wT[:, f, half * 3 * P:(half + 1) * 3 * P],
                                        ps_turn[:, n % 2, 0:3 * P]).then_inc(s_turned, 1)
                dve.wait_ge(s_wqk, 2 * i + 1 if i < R else R + i + 1)
                c, out = (2 * H, wqk1[:, :, i, :]) if i < R else (2, wqk2[:, :, i - R, :])
                dve.tensor_copy(out, ps_small[:, 0:KD * c].rearrange("p (k c) -> p k c", c=c)).then_inc(s_wqk_out, 1)

            for i in range(NW):
                weights_out(i)
                if i < R:
                    dve.wait_ge(s_wqk, 2 * i + 2)
                    dve.tensor_copy(kq1[:, :, i, :], ps_small[:, 0:NT * 2 * H].rearrange("p (t c) -> p t c", c=2 * H)
                                    ).then_inc(s_wqk_out, 1)
                if i == 0:
                    dve.sem_inc(s_same, 8)
                    with dve.Fori(0, EC // 8) as j:
                        for b in range(2):
                            dve.wait_ge(s_bcast, j * 2 + b + 3)
                            for a in range(4):
                                c = j * 8 + b * 4 + a
                                dve.wait_ge(s_same, c + 1)
                                dve.scalar_tensor_tensor(out=same[:, 4 * b + a], in0=ps_key[:, a * P:(a + 1) * P],
                                                         scalar=key[:, bass.ds(c, 1)], in1=earlier[:],
                                                         op0=ALU.is_equal, op1=ALU.mult,
                                                         accum_out=packed[:, bass.ds(c, 1)]).then_inc(s_same, 1)
                    dve.wait_ge(s_same, EC + 8)
                    dve.tensor_scalar(edges_f[:, 0, :], packed[:], float(2 * P), float(2 ** 23), ALU.is_ge,
                                      ALU.mult).then_inc(s_key, 1)
                    dve.wait_ge(s_key, 4)
                    dve.tensor_tensor(edges_f[:, 1, :], key[:], edges_f[:, 0, :], ALU.add).then_inc(s_key, 1)
                    dve.wait_ge(s_key, 5)
                    dve.tensor_copy(key_i[:], edges_f[:, 1, :]).then_inc(s_index, 1)


def gather_counts(nc, g, counts, ct):
    NT, NP, R = g.NT, g.NP, g.R
    with ExitStack() as ctx:
        part = ctx.enter_context(nc.sbuf_tensor("part", [P, 2, 2, NP], F32))
        s_in = [ctx.enter_context(nc.semaphore(f"c_in{q}")) for q in range(2)]
        s_sum = ctx.enter_context(nc.semaphore("c_sum"))
        block = ctx.enter_context(nc.Block())
        tiles = [c.rearrange("(r s p n) o -> (r s) p (n o)", r=R, s=NT, p=P) for c in counts]

        @block.sync
        def _(sp):
            for n in range(R * NT):
                if n >= 2:
                    sp.wait_ge(s_sum, n - 1)
                for k in range(2):
                    sp.dma_start(part[:, n % 2, k, :], tiles[k][n]).then_inc(s_in[n % 2], 16)

        @block.vector
        def _(dve):
            for n in range(R * NT):
                dve.wait_ge(s_in[n % 2], 32 * (n // 2 + 1))
                dve.tensor_tensor(ct[n // NT][:, n % NT, :], part[:, n % 2, 0, :], part[:, n % 2, 1, :],
                                  ALU.add).then_inc(s_sum, 1)


class Heads:

    def __init__(self, nc, ctx, g, tag, H, R, ct, kq, ident, rows):
        self.g, self.H, self.R, self.ct, self.kq, self.ident = g, H, R, ct, kq, ident
        NT, NP = g.NT, g.NP
        sb = lambda n, s, d=F32: ctx.enter_context(nc.sbuf_tensor(tag + n, s, d))
        sem = lambda n: ctx.enter_context(nc.semaphore(tag + n))
        self.rows = rows
        self.miss = sb("miss", [P, 2, NP], BF16)
        self.acc = sb("acc", [P, NP])
        self.km = sb("km", [P, NT, R])
        self.lg = sb("lg", [P, NT, R])
        self.m0 = sb("m0", [P, NT])
        self.m = sb("m", [P, NT])
        self.none = sb("none", [P, NT])
        self.ab = sb("ab", [P, NT, R, 2])
        self.rows_sb = sb("rows_sb", [2 * R, NP])
        self.ps_turn = ctx.enter_context(nc.psum_tensor(tag + "ps_turn", [P, 2, 512], F32))
        self.ps_rows = ctx.enter_context(nc.psum_tensor(tag + "ps_rows", [P, 512], F32))
        self.s_miss = sem("miss_made")
        self.s_acc = sem("acc_step")
        self.s_turn = sem("acc_turned")
        self.s_km = sem("km_made")
        self.s_ab = sem("ab_made")
        self.s_abT = sem("ab_turned")
        self.s_rows = sem("rows_copied")
        self.s_rows_out = sem("rows_out")

    def start_vector(self, dve):
        dve.sem_inc(self.s_km, 2)

    def max_step(self, dve, h, r, s):
        NT = self.g.NT
        n = (h * self.R + r) * NT + s
        dve.tensor_scalar(self.miss[:, s % 2], self.ct[r][:, s, :], 0.0, -BIG, ALU.is_equal,
                          ALU.mult).then_inc(self.s_miss, 1)
        dve.wait_ge(self.s_miss, n + 1)
        k = self.kq[:, s, r, bass.ds(self.H + h, 1)]
        if s == 0:
            dve.tensor_scalar(self.acc[:], self.miss[:, 0], k, None, ALU.add).then_inc(self.s_acc, 1)
        else:
            dve.wait_ge(self.s_acc, n)
            dve.scalar_tensor_tensor(out=self.acc[:], in0=self.miss[:, s % 2], scalar=k, in1=self.acc[:],
                                     op0=ALU.add, op1=ALU.max).then_inc(self.s_acc, 1)

    def reduce_unit(self, dve, h, r):
        for i, (t0, nt) in enumerate(GROUPS):
            dve.wait_ge(self.s_turn, (h * self.R + r) * 3 + i + 1)
            dve.tensor_reduce(self.km[:, t0:t0 + nt, r],
                              self.ps_turn[:, i % 2, 0:nt * P].rearrange("p (t s) -> p t s", s=P),
                              AX, ALU.max).then_inc(self.s_km, 1)

    def rows_of_head(self, dve, h):
        R, NT = self.R, self.g.NT
        q = self.kq[:, :, :, bass.ds(h, 1)].rearrange("p t r o -> p t (r o)")
        dve.wait_ge(self.s_km, (h + 1) * 3 * R + 2)
        dve.tensor_tensor(self.lg[:], self.km[:], q, ALU.add).then_inc(self.s_ab, 1)
        dve.wait_ge(self.s_ab, h * 7 + 1)
        dve.tensor_reduce(self.m0[:], self.lg[:], AX, ALU.max).then_inc(self.s_ab, 1)
        dve.wait_ge(self.s_ab, h * 7 + 2)
        dve.scalar_tensor_tensor(out=self.m[:], in0=self.m0[:], scalar=SLOPE, in1=self.m0[:], op0=ALU.mult,
                                 op1=ALU.max).then_inc(self.s_ab, 1)
        dve.tensor_scalar(self.none[:], self.m0[:], -0.5 * BIG, BIG, ALU.is_lt, ALU.mult).then_inc(self.s_ab, 1)
        dve.wait_ge(self.s_ab, h * 7 + 4)
        dve.tensor_tensor(self.m[:], self.m[:], self.none[:], ALU.add).then_inc(self.s_ab, 1)
        dve.wait_ge(self.s_ab, h * 7 + 5)
        dve.wait_ge(self.s_abT, h * 3 + 3)
        m = self.m[:].rearrange("p (t o) -> p t o", o=1).broadcast_to([P, NT, R])
        dve.tensor_tensor(self.ab[:, :, :, 0], q, m, ALU.subtract).then_inc(self.s_ab, 1)
        dve.scalar_tensor_tensor(out=self.ab[:, :, :, 1], in0=q, scalar=SLOPE, in1=m, op0=ALU.mult,
                                 op1=ALU.subtract).then_inc(self.s_ab, 1)

    def start_tensor(self, pe):
        pe.sem_inc(self.s_abT, 3)

    def turn_unit(self, pe, h, r):
        u = h * self.R + r
        pe.wait_ge(self.s_acc, (u + 1) * self.g.NT)
        for i, (t0, nt) in enumerate(GROUPS):
            pe.wait_ge(self.s_km, u * 3 + (2, 1, 3)[i])
            for j in range(nt):
                last = pe.transpose(self.ps_turn[:, i % 2, j * P:(j + 1) * P],
                                    self.acc[:, (t0 + j) * P:(t0 + j + 1) * P], self.ident[:])
            last.then_inc(self.s_turn, 1)

    def turn_rows(self, pe, h):
        pe.wait_ge(self.s_ab, h * 7 + 7)
        for i, (t0, nt) in enumerate(GROUPS):
            pe.wait_ge(self.s_rows, h * 3 + i + 1)
            for j in range(nt):
                last = pe.transpose(self.ps_rows[0:2 * self.R, j * P:(j + 1) * P],
                                    self.ab[:, t0 + j].rearrange("p r c -> p (r c)"), self.ident[:])
            last.then_inc(self.s_abT, 1)

    def start_scalar(self, act):
        act.sem_inc(self.s_rows, 1)
        act.sem_inc(self.s_rows_out, 16)

    def rows_to_dram(self, act, h):
        act.wait_ge(self.s_rows_out, h * 16 + 16)
        for i, (t0, nt) in enumerate(GROUPS):
            act.wait_ge(self.s_abT, h * 3 + i + 4)
            act.copy(self.rows_sb[:, t0 * P:(t0 + nt) * P], self.ps_rows[0:2 * self.R, 0:nt * P]
                     ).then_inc(self.s_rows, 1)
        act.wait_ge(self.s_rows, h * 3 + 4)
        R = self.R
        act.dma_start(self.rows[bass.ds(h * R, R)].rearrange("r (c n) -> (r c) n", c=2),
                      self.rows_sb[:]).then_inc(self.s_rows_out, 16)


def scaled_k(dve, kq, H, k08, k02, sem):
    dve.tensor_scalar(k08[:], kq[:, :, :, H:2 * H], 1.0 - SLOPE, None, ALU.mult).then_inc(sem, 1)
    dve.tensor_scalar(k02[:], kq[:, :, :, H:2 * H], SLOPE, None, ALU.mult).then_inc(sem, 1)


def multi_head(nc, g, tag, H, R, F, ct, kq, ident, feat, rows, post_setup):
    NT, NP = g.NT, g.NP
    per_bank = 512 // (F + 1)
    banks = -(-NT // per_bank)
    UNIT = NT
    PE0 = 2 * UNIT
    T0 = 2 * UNIT
    with ExitStack() as ctx:
        sb = lambda n, s, d=F32: ctx.enter_context(nc.sbuf_tensor(tag + n, s, d))
        sem = lambda n: ctx.enter_context(nc.semaphore(tag + n))
        hd = Heads(nc, ctx, g, tag, H, R, ct, kq, ident, rows)
        wt = sb("wt", [P, SLOTS, NP])
        row = sb("row", [P, 2, 2, NP])
        ft = sb("ft", [P, 2, NT, F + 1])
        raw = sb("raw", [P, NT, F + 1])
        k08 = sb("k08", [P, NT, R, H])
        k02 = sb("k02", [P, NT, R, H])
        ps_out = ctx.enter_context(nc.psum_tensor(tag + "ps_out", [P, banks, 512], F32))
        s_k = sem("k_scaled")
        s_row = sem("row_in")
        s_ft = sem("ft_in")
        s_lg = sem("logit_made")
        s_exp = sem("exp_made")
        s_wt = sem("weight_made")
        s_pe = sem("step_summed")
        s_raw = sem("raw_copied")
        post = post_setup(ctx, raw, s_raw, banks)
        block = ctx.enter_context(nc.Block())

        def over_heads(eng, body):
            body(0, False, False, True)
            if H > 3:
                with eng.Fori(1, H - 2) as h:
                    body(h, True, True, True)
            body(H - 2, True, True, False)
            body(H - 1, True, False, False)

        @block.sync
        def _(sp):
            post.sync(sp, H)
            for u in range(H * R):
                h, r = divmod(u, R)
                if u >= 2:
                    sp.wait_ge(s_pe, (u + 1) * UNIT)
                sp.dma_start(ft[:, u % 2], feat[h, r * NT:(r + 1) * NT].rearrange("s p f -> p s f")
                             ).then_inc(s_ft, 16)
                if r == 0:
                    sp.wait_ge(hd.s_rows_out, h * 16 + 32)
                if u >= 2:
                    sp.wait_ge(s_lg, (u + 1) * UNIT)
                sp.dma_start(row[:, u % 2].rearrange("p c n -> p (c n)"),
                             rows[u:u + 1].broadcast_to([P, 2 * NP])).then_inc(s_row, 16)
                sp.wait_ge(s_ft, u * 16 + 16)
                sp.wait_ge(s_row, u * 16 + 16)

        @block.vector
        def _(dve):
            hd.start_vector(dve)
            dve.sem_inc(s_lg, T0)
            scaled_k(dve, kq, H, k08, k02, s_k)
            dve.wait_ge(s_k, 2)
            for h in range(2):
                for r in range(R):
                    for s in range(NT):
                        hd.max_step(dve, h, r, s)
                    hd.reduce_unit(dve, h, r)
                hd.rows_of_head(dve, h)

            def body(h, pending_sums, pending_rows, maximum):
                for r in range(R):
                    u = h * R + r

                    def logits(s):
                        n = u * UNIT + s
                        dve.wait_ge(s_pe, n + 1 + PE0 - SLOTS)
                        if s == 0:
                            dve.wait_ge(s_row, u * 16 + 16)
                        slot = u % 2
                        a = row[:, bass.ds(slot, 1), 0, :].rearrange("p o n -> p (o n)")
                        b = row[:, bass.ds(slot, 1), 1, :].rearrange("p o n -> p (o n)")
                        dve.scalar_tensor_tensor(out=wt[:, s % SLOTS], in0=a, scalar=k08[:, s, r, bass.ds(h, 1)],
                                                 in1=b, op0=ALU.add, op1=ALU.max).then_inc(s_lg, 1)

                    logits(0)
                    for s in range(NT):
                        if s + 1 < NT:
                            logits(s + 1)
                        if maximum:
                            hd.max_step(dve, h + 2, r, s)
                        dve.wait_ge(s_exp, u * UNIT + s + 1)
                        dve.scalar_tensor_tensor(out=wt[:, s % SLOTS], in0=wt[:, s % SLOTS], scalar=1.0,
                                                 in1=ct[r][:, s, :], op0=ALU.min, op1=ALU.mult).then_inc(s_wt, 1)
                        if r == 0 and s == 3 and pending_sums:
                            post.vector(dve, h - 1)
                    if maximum:
                        hd.reduce_unit(dve, h + 2, r)
                if maximum:
                    hd.rows_of_head(dve, h + 2)

            over_heads(dve, body)
            post.vector(dve, H - 1)

        @block.scalar
        def _(act):
            hd.start_scalar(act)
            act.sem_inc(s_raw, banks)
            act.wait_ge(s_k, 2)
            for h in range(2):
                hd.rows_to_dram(act, h)

            def sums_out(h):
                act.wait_ge(s_pe, (h + 1) * R * UNIT + PE0)
                post.before_raw(act, h)
                for b in range(banks):
                    nt = min(per_bank, NT - b * per_bank)
                    act.copy(raw[:, b * per_bank:b * per_bank + nt, :],
                             ps_out[:, b, 0:nt * (F + 1)].rearrange("p (t f) -> p t f", t=nt)).then_inc(s_raw, 1)

            def body(h, pending_sums, pending_rows, maximum):
                for r in range(R):
                    for s in range(NT):
                        n = (h * R + r) * UNIT + s
                        act.wait_ge(s_lg, n + 1 + T0)
                        act.activation(wt[:, s % SLOTS], wt[:, s % SLOTS], ACT.Exp,
                                       bias=k02[:, s, r, bass.ds(h, 1)]).then_inc(s_exp, 1)
                        if r == 0 and s == 0 and pending_sums:
                            sums_out(h - 1)
                        if r == 0 and s == 2 and pending_rows:
                            hd.rows_to_dram(act, h + 1)
                        if r == R - 1 and s == NT - 2 and pending_sums:
                            post.scalar(act, h - 1)

            over_heads(act, body)
            sums_out(H - 1)
            post.scalar(act, H - 1)
            act.wait_ge(hd.s_rows_out, 16 * H + 16)

        @block.tensor
        def _(pe):
            hd.start_tensor(pe)
            pe.sem_inc(s_pe, PE0)
            for h in range(2):
                for r in range(R):
                    hd.turn_unit(pe, h, r)
                hd.turn_rows(pe, h)

            def body(h, pending_sums, pending_rows, maximum):
                for r in range(R):
                    u = h * R + r
                    for s in range(NT):
                        if s == NT - 1 and maximum:
                            hd.turn_unit(pe, h + 2, r)
                        pe.wait_ge(s_wt, u * UNIT + s + 1)
                        if s == 0:
                            pe.wait_ge(s_ft, u * 16 + 16)
                            if r == 0:
                                pe.wait_ge(s_raw, h * banks + banks)
                        for t in range(NT):
                            b, j = divmod(t, per_bank)
                            last = pe.matmul(ps_out[:, b, j * (F + 1):(j + 1) * (F + 1)],
                                             wt[:, s % SLOTS, t * P:(t + 1) * P],
                                             ft[:, bass.ds(u % 2, 1), s, :].rearrange("p o f -> p (o f)"),
                                             start=(r == 0 and s == 0 and j == 0),
                                             stop=(r == R - 1 and s == NT - 1), skip_group_check=True)
                        last.then_inc(s_pe, 1)
                        if r == 0 and s == 0 and pending_rows:
                            hd.turn_rows(pe, h + 1)

            over_heads(pe, body)

        @block.gpsimd
        def _(pool):
            post.start_pool(pool)
            for h in range(H):
                post.pool(pool, h)


def relational_post(nc, g, b1, h2):
    H, F, NT = 4, g.D // 4, g.NT

    def setup(ctx, raw, s_raw, banks):
        sb = lambda n, s, d=F32: ctx.enter_context(nc.sbuf_tensor("r1" + n, s, d))
        sem = lambda n: ctx.enter_context(nc.semaphore("r1" + n))
        bias = sb("bias", [P, g.D])
        rz = sb("rz", [P, NT])
        e = sb("e", [P, NT, F])
        s_b = sem("bias_in")
        s_rz = sem("rz")
        s_y = sem("y")
        s_e = sem("elu_exp")
        s_out = sem("h2_out")
        s_free = sem("raw_free")
        y = raw[:, :, 0:F]

        class Post:
            def sync(self, sp, H):
                sp.dma_start(bias[:], b1.rearrange("(o d) -> o d", o=1).broadcast_to([P, g.D])).then_inc(s_b, 16)
                sp.wait_ge(s_b, 16)

            def vector(self, dve, h):
                dve.wait_ge(s_raw, h * banks + 2 * banks)
                dve.wait_ge(s_y, h * 7 + 7)
                dve.tensor_scalar(rz[:], raw[:, :, F], Z_EPS, None, ALU.add).then_inc(s_rz, 1)
                dve.wait_ge(s_rz, h * 2 + 1)
                dve.reciprocal(rz[:], rz[:]).then_inc(s_rz, 1)

            def before_raw(self, act, h):
                act.wait_ge(s_free, h + 1)

            def scalar(self, act, h):
                act.wait_ge(s_y, h * 7 + 7 + 3)
                act.activation(e[:], e[:], ACT.Exp).then_inc(s_e, 1)

            def start_pool(self, pool):
                pool.sem_inc(s_y, 7)
                pool.sem_inc(s_free, 1)
                pool.wait_ge(s_b, 16)

            def pool(self, pool, h):
                bh = bias[:, bass.ds(h * F, F)].rearrange("p (o f) -> p o f", o=1).broadcast_to([P, NT, F])
                pool.wait_ge(s_rz, h * 2 + 2)
                pool.wait_ge(s_raw, h * banks + 2 * banks)
                pool.tensor_tensor(y, y, rz[:].rearrange("p (t o) -> p t o", o=1).broadcast_to([P, NT, F]),
                                   ALU.mult).then_inc(s_y, 1)
                pool.wait_ge(s_y, h * 7 + 8)
                pool.tensor_tensor(y, y, bh, ALU.add).then_inc(s_y, 1)
                pool.wait_ge(s_y, h * 7 + 9)
                pool.tensor_scalar(e[:], y, 0.0, None, ALU.min).then_inc(s_y, 1)
                pool.wait_ge(s_y, h * 7 + 10)
                pool.tensor_scalar(y, y, 0.0, None, ALU.max).then_inc(s_y, 1)
                pool.wait_ge(s_e, h + 1)
                pool.tensor_scalar(e[:], e[:], -1.0, None, ALU.add).then_inc(s_y, 1)
                pool.wait_ge(s_y, h * 7 + 12)
                pool.tensor_tensor(y, y, e[:], ALU.add).then_inc(s_y, 2)
                pool.wait_ge(s_y, h * 7 + 14)
                pool.dma_start(h2[:, :, h * F:(h + 1) * F], y).then_inc(s_out, 16)
                pool.wait_ge(s_out, 16 * (h + 1))
                pool.sem_inc(s_free, 1)

        return Post()

    return setup


def final_post(nc, g, x1, res, out):
    H, F, NT = 12, g.D // 12, g.NT

    def setup(ctx, raw, s_raw, banks):
        sb = lambda n, s, d=F32: ctx.enter_context(nc.sbuf_tensor("g1" + n, s, d))
        sem = lambda n: ctx.enter_context(nc.semaphore("g1" + n))
        rz = sb("rz", [P, NT])
        s_rz = sem("rz")
        s_y = sem("y")
        s_out = sem("out")
        s_free = sem("raw_free")
        y = raw[:, :, 0:F]
        full = (NT - 1) * P

        class Post:
            def sync(self, sp, H):
                pass

            def vector(self, dve, h):
                dve.wait_ge(s_raw, h * banks + 2 * banks)
                dve.wait_ge(s_y, h * 4 + 4)
                dve.tensor_scalar(rz[:], raw[:, :, F], Z_EPS, None, ALU.max).then_inc(s_rz, 1)
                dve.wait_ge(s_rz, h * 2 + 1)
                dve.reciprocal(rz[:], rz[:]).then_inc(s_rz, 1)

            def before_raw(self, act, h):
                act.wait_ge(s_free, h + 1)

            def scalar(self, act, h):
                pass

            def start_pool(self, pool):
                pool.sem_inc(s_y, 4)
                pool.sem_inc(s_free, 1)

            def pool(self, pool, h):
                pool.wait_ge(s_rz, h * 2 + 2)
                pool.wait_ge(s_raw, h * banks + 2 * banks)
                pool.tensor_tensor(y, y, rz[:].rearrange("p (t o) -> p t o", o=1).broadcast_to([P, NT, F]),
                                   ALU.mult).then_inc(s_y, 1)
                pool.wait_ge(s_y, h * 4 + 5)
                pool.tensor_tensor(y, y, res[:, :, bass.ds(h * F, F)], ALU.add).then_inc(s_y, 1)
                pool.wait_ge(s_y, h * 4 + 6)
                pool.tensor_scalar(y, y, 0.0, None, ALU.max).then_inc(s_y, 1)
                pool.wait_ge(s_y, h * 4 + 7)
                pool.tensor_tensor(y, y, x1[:, :, bass.ds(h * F, F)], ALU.add).then_inc(s_y, 1)
                pool.wait_ge(s_y, h * 4 + 8)
                pool.dma_start(out[0:full, bass.ds(h * F, F)].rearrange("(t p) d -> p t d", p=P),
                               raw[:, 0:NT - 1, 0:F]).then_inc(s_out, 16)
                pool.dma_start(out[full:g.N, bass.ds(h * F, F)], raw[0:g.LAST, NT - 1, 0:F]).then_inc(s_out, 16)
                pool.wait_ge(s_out, 32 * (h + 1))
                pool.sem_inc(s_free, 1)

        return Post()

    return setup


def second_logits(nc, g, ct, h2d, h2, kq2, wqk2, ident, rows):
    NT, NP, KD, R, D = g.NT, g.NP, g.KD, g.R, g.D
    with ExitStack() as ctx:
        sb = lambda n, s, d=F32: ctx.enter_context(nc.sbuf_tensor("l2" + n, s, d))
        sem = lambda n: ctx.enter_context(nc.semaphore("l2" + n))
        hd = Heads(nc, ctx, g, "l2", 1, R, ct, kq2, ident, rows)
        h2T = sb("h2T", [P, KD, NP])
        ps_h = ctx.enter_context(nc.psum_tensor("l2ps_h", [P, 2, 512], F32))
        ps_kq = ctx.enter_context(nc.psum_tensor("l2ps_kq", [P, 512], F32))
        s_in = sem("in")
        s_hT = sem("hT")
        s_hT_out = sem("hT_out")
        s_kq = sem("kq")
        s_kq_out = sem("kq_out")
        block = ctx.enter_context(nc.Block())

        @block.sync
        def _(sp):
            sp.dma_start(h2[:], h2d).then_inc(s_in, 16)

        @block.tensor
        def _(pe):
            hd.start_tensor(pe)
            pe.wait_ge(s_in, 16)
            for n in range(2 * NT):
                t, half = divmod(n, 2)
                if n >= 2:
                    pe.wait_ge(s_hT_out, n - 1)
                for j in range(3):
                    kd = 3 * half + j
                    last = pe.transpose(ps_h[:, n % 2, j * P:(j + 1) * P], h2[:, t, kd * P:(kd + 1) * P], ident[:])
                last.then_inc(s_hT, 1)
            pe.wait_ge(s_hT_out, 2 * NT)
            for t in range(NT):
                for kd in range(KD):
                    last = pe.matmul(ps_kq[:, t * 2 * R:(t + 1) * 2 * R], h2T[:, kd, t * P:(t + 1) * P],
                                     wqk2[:, kd].rearrange("p r c -> p (r c)"), start=(kd == 0), stop=(kd == KD - 1),
                                     skip_group_check=True)
            last.then_inc(s_kq, 1)
            for r in range(R):
                hd.turn_unit(pe, 0, r)
            hd.turn_rows(pe, 0)

        @block.scalar
        def _(act):
            hd.start_scalar(act)
            for n in range(2 * NT):
                t, half = divmod(n, 2)
                act.wait_ge(s_hT, n + 1)
                act.copy(h2T[:, 3 * half:3 * half + 3, t * P:(t + 1) * P],
                         ps_h[:, n % 2, 0:3 * P].rearrange("p (k n) -> p k n", k=3)).then_inc(s_hT_out, 1)
            hd.rows_to_dram(act, 0)
            act.wait_ge(hd.s_rows_out, 32)

        @block.vector
        def _(dve):
            hd.start_vector(dve)
            dve.wait_ge(s_kq, 1)
            dve.tensor_copy(kq2[:], ps_kq[:, 0:NT * 2 * R].rearrange("p (t r c) -> p t r c", t=NT, r=R)
                            ).then_inc(s_kq_out, 1)
            dve.wait_ge(s_kq_out, 1)
            for r in range(R):
                for s in range(NT):
                    hd.max_step(dve, 0, r, s)
                hd.reduce_unit(dve, 0, r)
            hd.rows_of_head(dve, 0)


def second_layer(nc, g, ct, h2, kq2, rows, W2, b2, x, x1):
    NT, NP, KD, R, D = g.NT, g.NP, g.KD, g.R, g.D
    TG = 2
    W = TG * P
    NG = NT // TG
    RING = NT
    full = (NT - 1) * P
    with ExitStack() as ctx:
        sb = lambda n, s, d=F32: ctx.enter_context(nc.sbuf_tensor("m2" + n, s, d))
        sem = lambda n: ctx.enter_context(nc.semaphore("m2" + n))
        w = sb("w", [P, R, KD, D])
        row = sb("row", [P, 2 * R, W])
        wt = sb("wt", [P, RING, W])
        k08 = sb("k08", [P, NT, R, 1])
        k02 = sb("k02", [P, NT, R, 1])
        gT = sb("gT", [P, R, KD, W])
        zsum = sb("zsum", [P, W])
        ones = sb("ones", [P, 1])
        none = sb("none", [P, 1])
        rz = sb("rz", [P, 2])
        bias = sb("bias", [P, D])
        xt = sb("xt", [P, 2, D])
        ps_g = ctx.enter_context(nc.psum_tensor("m2ps_g", [P, 2, 3, 512], F32))
        ps_o = ctx.enter_context(nc.psum_tensor("m2ps_o", [P, 2, 512], F32))
        s_k = sem("k")
        s_one = sem("one")
        s_w = sem("w")
        s_b = sem("b")
        s_row = sem("row")
        s_x = [sem("x0"), sem("x1")]
        s_lg = sem("lg")
        s_exp = sem("exp")
        s_wt = sem("wt")
        s_pe = sem("pe")
        s_z = sem("z")
        s_g = sem("g")
        s_o = sem("o")
        s_rz = sem("rz")
        s_o_out = sem("o_out")
        s_st = [sem("st0"), sem("st1")]
        block = ctx.enter_context(nc.Block())
        U = R * NT

        @block.sync
        def _(sp):
            sp.dma_start(bias[:], b2.rearrange("(o d) -> o d", o=1).broadcast_to([P, D])).then_inc(s_b, 16)
            rv = rows.rearrange("r (c n) -> (r c) n", c=2)

            def load_rows(gr):
                sp.wait_ge(s_lg, (gr + 1) * U)
                sp.dma_start(row[:],
                             rv[:, bass.ds(gr * W, W)].rearrange("(o c) n -> o c n", o=1)
                             .broadcast_to([P, 2 * R, W])).then_inc(s_row, 16)
                sp.wait_ge(s_row, (gr + 1) * 16)

            load_rows(0)
            for r in range(R):
                sp.dma_start(w[:, r], W2[r].rearrange("(k p) f -> p k f", p=P)).then_inc(s_w, 16)
            sp.wait_ge(s_one, 3)
            for gr in range(NG):
                if gr + 1 < NG:
                    load_rows(gr + 1)
                for j in range(TG):
                    t = gr * TG + j
                    if gr >= 1:
                        sp.wait_ge(s_st[j], 16 * gr)
                    if t < NT - 1:
                        sp.dma_start(xt[:, j, :], x[t * P:(t + 1) * P, :]).then_inc(s_x[j], 16)
                    else:
                        sp.wait_ge(s_o_out, 3)
                        sp.dma_start(xt[0:g.LAST, j, :], x[full:g.N, :]).then_inc(s_x[j], 16)
                if gr >= 0:
                    for j in range(TG):
                        t = gr * TG + j
                        sp.wait_ge(s_o_out, 3 * (t + 1))
                        sp.dma_start(x1[:, t, :], xt[:, j, :]).then_inc(s_st[j], 16)
            for j in range(TG):
                sp.wait_ge(s_st[j], 16 * NG)

        @block.gpsimd
        def _(pool):
            pool.memset(ones[:], 1.0).then_inc(s_one, 1)
            pool.memset(none[:], 0.0).then_inc(s_one, 1)
            pool.memset(xt[:], 0.0).then_inc(s_one, 1)
            pool.sem_inc(s_z, RING)
            pool.wait_ge(s_one, 3)
            with pool.Fori(0, NG) as gr:
                for r in range(R):
                    for s in range(NT):
                        n = gr * U + r * NT + s
                        pool.wait_ge(s_wt, n + 1)
                        if r == 0 and s == 0:
                            pool.wait_ge(s_o, gr * TG + 1)
                            pool.tensor_tensor(zsum[:], wt[:, s], none[:].broadcast_to([P, W]), ALU.add).then_inc(s_z, 1)
                        else:
                            pool.wait_ge(s_z, n + RING)
                            pool.tensor_tensor(zsum[:], zsum[:], wt[:, s], ALU.add).then_inc(s_z, 1)

        @block.vector
        def _(dve):
            dve.sem_inc(s_lg, U)
            scaled_k(dve, kq2, 1, k08, k02, s_k)
            dve.wait_ge(s_k, 2)
            dve.wait_ge(s_b, 16)

            def steps(gr):
                dve.wait_ge(s_row, gr * 16 + 16)

                def logits(r, s):
                    n = gr * U + r * NT + s
                    dve.wait_ge(s_pe, n + 1)
                    dve.wait_ge(s_z, n + 1)
                    dve.scalar_tensor_tensor(out=wt[:, s], in0=row[:, 2 * r, :], scalar=k08[:, s, r, :],
                                             in1=row[:, 2 * r + 1, :], op0=ALU.add,
                                             op1=ALU.max).then_inc(s_lg, 1)

                def weights(r, s):
                    n = gr * U + r * NT + s
                    dve.wait_ge(s_exp, n + 1)
                    dve.scalar_tensor_tensor(out=wt[:, s], in0=wt[:, s], scalar=1.0,
                                             in1=ct[r][:, s, bass.ds(gr * W, W)], op0=ALU.min,
                                             op1=ALU.mult).then_inc(s_wt, 1)

                for r in range(R):
                    for s in range(NT + 2):
                        if s < NT:
                            logits(r, s)
                        if s >= 2:
                            weights(r, s - 2)

            def outputs(gr):
                for j in range(TG):
                    t = gr * TG + j
                    dve.wait_ge(s_o, t + 2)
                    dve.tensor_scalar(rz[:, 0:1], ps_o[:, 1, D // 2:D // 2 + 1], Z_EPS, None, ALU.add).then_inc(s_rz, 1)
                    dve.wait_ge(s_rz, 2 * t + 1)
                    dve.reciprocal(rz[:, 1:2], rz[:, 0:1]).then_inc(s_rz, 1)
                    dve.wait_ge(s_x[j], 16 * (gr + 1))
                    dve.tensor_tensor(xt[:, j, :], xt[:, j, :], bias[:], ALU.add).then_inc(s_o_out, 1)
                    dve.wait_ge(s_rz, 2 * t + 2)
                    dve.wait_ge(s_o_out, 3 * t + 1)
                    for half in range(2):
                        c = slice(half * D // 2, (half + 1) * D // 2)
                        dve.scalar_tensor_tensor(out=xt[:, j, c], in0=ps_o[:, half, 0:D // 2], scalar=rz[:, 1:2],
                                                 in1=xt[:, j, c], op0=ALU.mult, op1=ALU.add).then_inc(s_o_out, 1)

            steps(0)
            for gr in range(1, NG):
                steps_first = gr
                outputs(gr - 1)
                steps(steps_first)
            outputs(NG - 1)

        @block.scalar
        def _(act):
            act.wait_ge(s_k, 2)

            def evac(gr, r):
                act.wait_ge(s_pe, RING + gr * U + (r + 1) * NT)
                for b in range(3):
                    act.copy(gT[:, r, 2 * b:2 * b + 2, :],
                             ps_g[:, r % 2, b, 0:2 * W].rearrange("p (k n) -> p k n", k=2)).then_inc(s_g, 1)

            for gr in range(NG):
                for r in range(R):
                    for s in range(NT):
                        n = gr * U + r * NT + s
                        act.wait_ge(s_lg, n + 1 + U)
                        act.activation(wt[:, s], wt[:, s], ACT.Exp, bias=k02[:, s, r, :]).then_inc(s_exp, 1)
                        if s == 3 and r > 0:
                            evac(gr, r - 1)
                evac(gr, R - 1)

        @block.tensor
        def _(pe):
            pe.sem_inc(s_pe, RING)
            pe.sem_inc(s_o, 1)
            for gr in range(NG):
                for r in range(R):
                    u = gr * R + r
                    for s in range(NT):
                        pe.wait_ge(s_wt, gr * U + r * NT + s + 1)
                        if s == 0 and u >= 1:
                            pe.wait_ge(s_g, 3 * u if r == 0 else max(3 * (u - 1), 0) or 1) if (r == 0 or u >= 2) else None
                        for f in range(KD):
                            last = pe.matmul(ps_g[:, r % 2, f // 2, (f % 2) * W:(f % 2 + 1) * W],
                                             h2[:, s, f * P:(f + 1) * P], wt[:, s],
                                             start=(s == 0 and f % 2 == 0), stop=(s == NT - 1), skip_group_check=True)
                        last.then_inc(s_pe, 1)
                pe.wait_ge(s_g, 3 * R * (gr + 1))
                pe.wait_ge(s_z, RING + (gr + 1) * U)
                pe.wait_ge(s_w, 16 * R)
                pe.wait_ge(s_one, 3)
                for j in range(TG):
                    t = gr * TG + j
                    if t >= 1:
                        pe.wait_ge(s_o_out, 3 * t)
                    for half in range(2):
                        for i in range(R * KD):
                            r, kd = divmod(i, KD)
                            last = pe.matmul(ps_o[:, half, 0:D // 2], gT[:, r, kd, j * P:(j + 1) * P],
                                             w[:, r, kd, half * D // 2:(half + 1) * D // 2], start=(i == 0),
                                             stop=(i == R * KD - 1), skip_group_check=True)
                    pe.matmul(ps_o[:, 1, D // 2:D // 2 + 1], zsum[:, j * P:(j + 1) * P], ones[:], start=False,
                              stop=True, skip_group_check=True).then_inc(s_o, 1)


def sum_relations(nc, g, ct):
    with ExitStack() as ctx:
        s = ctx.enter_context(nc.semaphore("sum_rel"))
        block = ctx.enter_context(nc.Block())

        @block.vector
        def _(dve):
            for r in (1, 2):
                for t in range(g.NT):
                    if r == 2:
                        dve.wait_ge(s, t + 1)
                    dve.tensor_tensor(ct[0][:, t, :], ct[0][:, t, :], ct[r][:, t, :], ALU.add).then_inc(s, 1)


def third_tables(nc, g, x1d, x1, res, kq3, feat3, Wg, al, ar, Wres, ident):
    NT, NP, KD, D = g.NT, g.NP, g.KD, g.D
    H, F = 12, D // 12
    with ExitStack() as ctx:
        sb = lambda n, s, d=F32: ctx.enter_context(nc.sbuf_tensor("t3" + n, s, d))
        sem = lambda n: ctx.enter_context(nc.semaphore("t3" + n))
        h = sb("h", [P, NT, D])
        hT = sb("hT", [P, KD, NP])
        stats = sb("stats", [P, NT, 2, 6])
        mv = sb("mv", [P, NT, 2])
        std = sb("std", [P, NT])
        rstd = sb("rstd", [P, NT])
        shift = sb("shift", [P, NT])
        eps = sb("eps", [P, 1])
        wd = sb("wd", [F, 2, 2, F])
        att = sb("att", [2 * H, F])
        attT = sb("attT", [F, 2 * H])
        wbd = sb("wbd", [P, 2, P])
        wa = sb("wa", [P, 2 * H])
        wabd = sb("wabd", [P, KD, 2 * H])
        stage = sb("stage", [P, 2, H, F + 1])
        ps_turn = ctx.enter_context(nc.psum_tensor("t3ps_turn", [P, 2, 512], F32))
        ps_f = ctx.enter_context(nc.psum_tensor("t3ps_f", [P, 2, 2, 512], F32))
        ps_s = ctx.enter_context(nc.psum_tensor("t3ps_s", [P, 512], F32))
        s_const = sem("const")
        s_x = sem("x")
        s_wd = sem("wd")
        s_stat = sem("stat")
        s_norm = sem("norm")
        s_h = sem("h_made")
        s_turn = sem("turn")
        s_turned = sem("turned")
        s_prep = sem("prep")
        s_prep_out = sem("prep_out")
        s_f = sem("f")
        s_f_out = sem("f_out")
        s_kq = sem("kq")
        s_spill = [sem("spill0"), sem("spill1")]
        block = ctx.enter_context(nc.Block())

        @block.sync
        def _(sp):
            sp.dma_start(x1[:], x1d).then_inc(s_x, 16)
            for i, m in enumerate((Wg, Wres)):
                for c in range(2):
                    sp.dma_start(wd[:, i, c, :], m).then_inc(s_wd, 16)
            for i, m in enumerate((al, ar)):
                sp.dma_start(att[i * H:(i + 1) * H, :], m.rearrange("o h f -> (o h) f")).then_inc(s_wd, 16)

        @block.gpsimd
        def _(pool):
            pool.memset(eps[:], LN_EPS).then_inc(s_const, 1)
            pool.memset(wbd[:], 0.0).then_inc(s_const, 1)
            pool.memset(wabd[:], 0.0).then_inc(s_const, 1)
            pool.memset(stage[:], 1.0).then_inc(s_const, 1)

        @block.tensor
        def _(pe):
            pe.wait_ge(s_wd, 96)
            for i in range(2):
                last = pe.transpose(ps_s[:, i * F:(i + 1) * F], wd[:, i].rearrange("o c d -> o (c d)"), ident[0:F, 0:F])
            last = pe.transpose(ps_s[0:F, P:P + 2 * H], att[:], ident[0:2 * H, 0:2 * H])
            last.then_inc(s_prep, 1)
            pe.wait_ge(s_prep_out, 5)
            pe.matmul(ps_s[:, 0:2 * H], wd[:, 0].rearrange("o c d -> o (c d)"), attT[:], start=True,
                      stop=True).then_inc(s_prep, 1)
            for n in range(2 * NT):
                t, half = divmod(n, 2)
                pe.wait_ge(s_h, t + 1)
                if n >= 2:
                    pe.wait_ge(s_turned, n - 1)
                for j in range(3):
                    kd = 3 * half + j
                    last = pe.transpose(ps_turn[:, n % 2, j * P:(j + 1) * P], h[:, t, kd * P:(kd + 1) * P], ident[:])
                last.then_inc(s_turn, 1)
            pe.wait_ge(s_turned, 2 * NT)
            pe.wait_ge(s_prep_out, 6 + 2 * KD)
            for t in range(NT):
                for kd in range(KD):
                    last = pe.matmul(ps_s[:, t * 2 * H:(t + 1) * 2 * H], hT[:, kd, t * P:(t + 1) * P], wabd[:, kd, :],
                                     start=(kd == 0), stop=(kd == KD - 1), skip_group_check=True)
            last.then_inc(s_kq, 1)
            for n in range(2 * NT):
                i, t = divmod(n, NT)
                if n >= 2:
                    pe.wait_ge(s_f_out, 2 * (n - 1))
                for kd in range(KD):
                    b, j = divmod(kd, 3)
                    last = pe.matmul(ps_f[:, n % 2, b, j * P:(j + 1) * P], hT[:, kd, t * P:(t + 1) * P], wbd[:, i, :],
                                     start=(j == 0), stop=True, skip_group_check=True)
                last.then_inc(s_f, 1)

        @block.vector
        def _(dve):
            dve.wait_ge(s_prep, 1)
            dve.wait_ge(s_const, 4)
            for i in range(2):
                for c in range(2):
                    dve.tensor_copy(wbd[c * F:(c + 1) * F, i, c * F:(c + 1) * F],
                                    ps_s[c * F:(c + 1) * F, i * F:(i + 1) * F]).then_inc(s_prep_out, 1)
            dve.tensor_copy(attT[:], ps_s[0:F, P:P + 2 * H]).then_inc(s_prep_out, 1)
            dve.wait_ge(s_prep, 2)
            dve.tensor_copy(wa[:], ps_s[:, 0:2 * H]).then_inc(s_prep_out, 1)
            dve.wait_ge(s_prep_out, 6)
            for kd in range(KD):
                for c in range(2):
                    hh = 2 * kd + c
                    p = slice(c * F, (c + 1) * F)
                    dve.tensor_copy(wabd[p, kd, hh:hh + H + 1:H], wa[p, hh:hh + H + 1:H]).then_inc(s_prep_out, 1)
            dve.wait_ge(s_x, 16)
            layernorm_stats(dve, g, x1, stats, mv, s_stat)
            dve.wait_ge(s_norm, 1)
            dve.reciprocal(rstd[:], std[:]).then_inc(s_norm, 1)
            dve.wait_ge(s_norm, 2)
            dve.scalar_tensor_tensor(out=shift[:], in0=mv[:, :, 0], scalar=-1.0, in1=rstd[:],
                                     op0=ALU.mult, op1=ALU.mult).then_inc(s_norm, 1)
            dve.wait_ge(s_kq, 1)
            v = ps_s[:, 0:NT * 2 * H].rearrange("p (t c) -> p t c", t=NT)
            dve.tensor_copy(kq3[:, :, 0, H:2 * H], v[:, :, 0:H])
            dve.tensor_copy(kq3[:, :, 0, 0:H], v[:, :, H:2 * H])

        @block.scalar
        def _(act):
            act.wait_ge(s_const, 4)
            act.wait_ge(s_stat, 3 * NT)
            act.activation(std[:], mv[:, :, 1], ACT.Sqrt, bias=eps[:]).then_inc(s_norm, 1)
            act.wait_ge(s_norm, 3)
            for t in range(NT):
                act.activation(h[:, t, :], x1[:, t, :], ACT.Relu, bias=shift[:, t:t + 1],
                               scale=rstd[:, t:t + 1]).then_inc(s_h, 1)
            for n in range(2 * NT):
                t, half = divmod(n, 2)
                act.wait_ge(s_turn, n + 1)
                act.copy(hT[:, 3 * half:3 * half + 3, t * P:(t + 1) * P],
                         ps_turn[:, n % 2, 0:3 * P].rearrange("p (k n) -> p k n", k=3)).then_inc(s_turned, 1)
            for n in range(2 * NT):
                i, t = divmod(n, NT)
                act.wait_ge(s_f, n + 1)
                if i == 0 and t >= 2:
                    act.wait_ge(s_spill[t % 2], 16 * (t // 2))
                for b in range(2):
                    v = ps_f[:, n % 2, b, 0:3 * P]
                    if i == 0:
                        act.copy(stage[:, t % 2, 6 * b:6 * b + 6, 0:F],
                                 v.rearrange("p (a f) -> p a f", f=F)).then_inc(s_f_out, 1)
                    else:
                        act.copy(res[:, t, b * 3 * P:(b + 1) * 3 * P], v).then_inc(s_f_out, 1)
                if i == 0:
                    act.wait_ge(s_f_out, 2 * (n + 1))
                    act.dma_start(feat3[:, t].rearrange("h p f -> p h f"), stage[:, t % 2]).then_inc(s_spill[t % 2], 16)
            for q in range(2):
                act.wait_ge(s_spill[q], 16 * NT // 2)


def gnn_kernel(nc, x, src, dst, etype, W1, q1, k1, b1, W2, q2, k2, b2, Wg, al, ar, Wres, out):
    g = Graph(x, src)
    NT, NP, R, D = g.NT, g.NP, g.R, g.D
    H1, F1, H3, F3 = 4, D // 4, 12, D // 12
    dram = lambda n, s: nc.dram_tensor(n, s, F32, kind="Internal").ap()
    counts = [dram(f"counts{i}", [R * NP * NP, 1]) for i in range(2)]
    feat1 = dram("feat1", [H1, R * NT, P, F1 + 1])
    feat3 = dram("feat3", [H3, NT, P, F3 + 1])
    rows1 = dram("rows1", [H1 * R, 2 * NP])
    rows2 = dram("rows2", [R, 2 * NP])
    rows3 = dram("rows3", [H3, 2 * NP])
    h2d = dram("h2d", [P, NT, D])
    x1d = dram("x1d", [P, NT, D])
    with ExitStack() as ctx:
        sb = lambda c, n, s, d=F32: c.enter_context(nc.sbuf_tensor(n, s, d))
        ident = sb(ctx, "ident", [P, P])
        kq1 = sb(ctx, "kq1", [P, NT, R, 2 * H1])
        wqk2 = sb(ctx, "wqk2", [P, g.KD, R, 2])
        kq2 = sb(ctx, "kq2", [P, NT, R, 2])
        kq3 = sb(ctx, "kq3", [P, NT, 1, 2 * H3])
        tables_and_counts(nc, g, x, src, dst, etype, W1, q1, k1, W2, q2, k2, ident, kq1, wqk2, feat1, counts)
        ct0 = sb(ctx, "ct0", [P, NT, NP], U16)
        with ExitStack() as inner:
            ct = [ct0] + [sb(inner, f"ct{r}", [P, NT, NP], U16) for r in (1, 2)]
            gather_counts(nc, g, counts, ct)
            multi_head(nc, g, "h1", H1, R, F1, ct, kq1, ident, feat1, rows1, relational_post(nc, g, b1, h2d))
            h2 = sb(inner, "h2", [P, NT, D])
            second_logits(nc, g, ct, h2d, h2, kq2, wqk2, ident, rows2)
            second_layer(nc, g, ct, h2, kq2, rows2, W2, b2, x, x1d)
            sum_relations(nc, g, ct)
        x1 = sb(ctx, "x1", [P, NT, D])
        res = sb(ctx, "res", [P, NT, D])
        third_tables(nc, g, x1d, x1, res, kq3, feat3, Wg, al, ar, Wres, ident)
        multi_head(nc, g, "h3", H3, 1, F3, [ct0], kq3, ident, feat3, rows3, final_post(nc, g, x1, res, out))


_INS = ['x', 'src', 'dst', 'edge_type_3', 'L0_gnn_W1', 'L0_gnn_q1', 'L0_gnn_k1', 'L0_gnn_b1', 'L0_gnn_W2', 'L0_gnn_q2',
        'L0_gnn_k2', 'L0_gnn_b2', 'L1_gnn_W', 'L1_gnn_attn_l', 'L1_gnn_attn_r', 'L1_gnn_W_res']


def kernel(**inputs):
    import numpy as _np
    import concourse.bacc as _bacc
    from concourse import mybir as _mybir
    from concourse.bass_utils import run_bass_kernel_spmd as _run

    nc = _bacc.Bacc("TRN2", target_bir_lowering=False, num_devices=1)
    arrays, args = {}, []
    for name in _INS:
        a = _np.ascontiguousarray(inputs[name])
        arrays[f"in_{name}_dram"] = a
        args.append(nc.dram_tensor(f"in_{name}_dram", a.shape, _mybir.dt.from_np(a.dtype), kind="ExternalInput").ap())
    out = nc.dram_tensor("out_0_dram", tuple(inputs['x'].shape), _mybir.dt.float32, kind="ExternalOutput").ap()
    gnn_kernel(nc, *args, out)
    r = _run(nc, [arrays], core_ids=[0])
    return r.results[0]["out_0_dram"]
```

```python
from contextlib import ExitStack

import numpy as np
import concourse.bass as bass
from concourse import mybir

ALU = mybir.AluOpType
ACT = mybir.ActivationFunctionType
F32 = mybir.dt.float32
I32 = mybir.dt.int32
U16 = mybir.dt.uint16
BF16 = mybir.dt.bfloat16
AX = mybir.AxisListType.X

P = 128
BIG = 1.0e30
SLOPE = 0.2
Z_EPS = 1.0e-16
LN_EPS = 1.0e-5
TURN_STEP = 8
SLOTS = 5
GROUPS = [(0, 4), (4, 4), (8, 2)]


class Graph:

    def __init__(self, x, src):
        self.N, self.D = x.shape
        self.E = src.shape[0]
        self.NT = -(-self.N // P)
        self.NP = self.NT * P
        self.LAST = self.N - (self.NT - 1) * P
        self.KD = self.D // P
        self.R = 3
        assert self.NT == sum(w for _, w in GROUPS)


def load_nodes(eng, g, sbuf, dram, sem):
    full = (g.NT - 1) * P
    eng.dma_start(sbuf[:, 0:g.NT - 1, :], dram[0:full, :].rearrange("(t p) d -> p t d", p=P)).then_inc(sem, 16)
    eng.dma_start(sbuf[0:g.LAST, g.NT - 1, :], dram[full:g.N, :]).then_inc(sem, 16)


def layernorm_stats(dve, g, x, stats, mv, sem):
    half = g.D // 2
    for t in range(g.NT):
        for i in range(2):
            dve.bn_stats(stats[:, t, i, :], x[:, t, i * half:(i + 1) * half]).then_inc(sem, 1)
    for t in range(g.NT):
        dve.wait_ge(sem, 2 * (t + 1))
        dve.bn_aggr(mv[:, t, :], stats[:, t]).then_inc(sem, 1)


class Heads:

    def __init__(self, nc, ctx, g, tag, H, R, ct, kq, ident, rows, space=None):
        self.g, self.H, self.R, self.ct, self.kq, self.ident = g, H, R, ct, kq, ident
        NT, NP = g.NT, g.NP
        sb = lambda n, s, d=F32: ctx.enter_context(nc.sbuf_tensor(tag + n, s, d))
        sem = lambda n: ctx.enter_context(nc.semaphore(tag + n))
        self.rows = rows
        self.all_miss = R == 1
        self.miss = sb("miss", [P, NT if self.all_miss else 2, NP], BF16)
        if space is None:
            space = sb("space", [P, 2 + (H > 1), NP])
        self.acc = [space[:, 0], space[:, 2 - (H == 1)]]
        self.km = sb("km", [P, 2, NT, R])
        self.lg = sb("lg", [P, NT, R])
        self.m0 = sb("m0", [P, NT])
        self.m = sb("m", [P, NT])
        self.none = sb("none", [P, NT])
        self.ab = sb("ab", [P, NT, R, 2])
        self.rows_sb = space[0:2 * R, 1]
        self.s_miss = sem("miss_made")
        self.s_first = [sem("first0"), sem("first1")]
        self.s_later = sem("later")
        self.s_turn = sem("acc_turned")
        self.s_km = sem("km_made")
        self.s_ab = sem("ab_made")
        self.s_abT = sem("ab_turned")
        self.s_rows = sem("rows_copied")
        self.s_rows_out = sem("rows_out")

    def later_unit(self, h, r):
        return (h - 2) * self.R + r

    def unit(self, h, r):
        return 2 * r + h if isinstance(h, int) and h < 2 and self.H > 1 else h * self.R + r

    def start_vector(self, dve):
        dve.sem_inc(self.s_km, 3)

    def mask(self, dve, r, s):
        dve.tensor_scalar(self.miss[:, s if self.all_miss else s % 2], self.ct[r][:, s, :], 0.0, -BIG, ALU.is_equal,
                          ALU.mult).then_inc(self.s_miss, 1)

    def first_step(self, dve, h, r, s):
        n = r * self.g.NT + s
        mask = self.miss[:, s if self.all_miss else s % 2]
        k = self.kq[:, s, r, self.H + h:self.H + h + 1]
        acc, sem = self.acc[h], self.s_first[h]
        if s == 0:
            dve.tensor_scalar(acc, mask, k, None, ALU.add).then_inc(sem, 1)
        else:
            dve.wait_ge(sem, n)
            dve.scalar_tensor_tensor(out=acc, in0=mask, scalar=k, in1=acc, op0=ALU.add,
                                     op1=ALU.max).then_inc(sem, 1)

    def later_step(self, dve, h, r, s):
        n = self.later_unit(h, r) * self.g.NT + s
        mask = self.miss[:, s if self.all_miss else s % 2]
        k = self.kq[:, s, r, bass.ds(self.H + h, 1)]
        if s == 0:
            dve.tensor_scalar(self.acc[0], mask, k, None, ALU.add).then_inc(self.s_later, 1)
        else:
            dve.wait_ge(self.s_later, n)
            dve.scalar_tensor_tensor(out=self.acc[0], in0=mask, scalar=k, in1=self.acc[0], op0=ALU.add,
                                     op1=ALU.max).then_inc(self.s_later, 1)

    def reduce_unit(self, dve, h, r):
        for i, (t0, nt) in enumerate(GROUPS):
            dve.wait_ge(self.s_turn, self.unit(h, r) * 3 + i + 1)
            dve.tensor_reduce(self.km[:, bass.ds(h % 2, 1), t0:t0 + nt, r].rearrange("p o t -> p (o t)"),
                              self.ps_turn[:, i, 0:nt * P].rearrange("p (t s) -> p t s", s=P),
                              AX, ALU.max).then_inc(self.s_km, 1)

    def rows_of_head(self, dve, h):
        R, NT = self.R, self.g.NT
        q = self.kq[:, :, :, bass.ds(h, 1)].rearrange("p t r o -> p t (r o)")
        groups = self.unit(h, R - 1) * 3 + 3
        dve.wait_ge(self.s_km, groups + 3)
        dve.tensor_tensor(self.lg[:], self.km[:, bass.ds(h % 2, 1)].rearrange("p o t r -> p (o t) r"), q,
                          ALU.add).then_inc(self.s_ab, 1)
        dve.wait_ge(self.s_ab, h * 7 + 1)
        dve.tensor_reduce(self.m0[:], self.lg[:], AX, ALU.max).then_inc(self.s_ab, 1)
        dve.wait_ge(self.s_ab, h * 7 + 2)
        dve.scalar_tensor_tensor(out=self.m[:], in0=self.m0[:], scalar=SLOPE, in1=self.m0[:], op0=ALU.mult,
                                 op1=ALU.max).then_inc(self.s_ab, 1)
        dve.tensor_scalar(self.none[:], self.m0[:], -0.5 * BIG, BIG, ALU.is_lt, ALU.mult).then_inc(self.s_ab, 1)
        dve.wait_ge(self.s_ab, h * 7 + 4)
        dve.tensor_tensor(self.m[:], self.m[:], self.none[:], ALU.add).then_inc(self.s_ab, 1)
        dve.wait_ge(self.s_ab, h * 7 + 5)
        dve.wait_ge(self.s_abT, h * 3 + 3)
        m = self.m[:].rearrange("p (t o) -> p t o", o=1).broadcast_to([P, NT, R])
        dve.tensor_tensor(self.ab[:, :, :, 0], q, m, ALU.subtract).then_inc(self.s_ab, 1)
        dve.scalar_tensor_tensor(out=self.ab[:, :, :, 1], in0=q, scalar=SLOPE, in1=m, op0=ALU.mult,
                                 op1=ALU.subtract).then_inc(self.s_ab, 1)

    def start_tensor(self, pe):
        pe.sem_inc(self.s_abT, 3)

    def turn_unit(self, pe, h, r):
        first = isinstance(h, int) and h < 2
        if first:
            pe.wait_ge(self.s_first[h], (r + 1) * self.g.NT)
        else:
            pe.wait_ge(self.s_later, (self.later_unit(h, r) + 1) * self.g.NT)
            pe.wait_ge(self.s_rows, h * 3 + 3)
        acc = self.acc[h] if first else self.acc[0]
        for i, (t0, nt) in enumerate(GROUPS):
            pe.wait_ge(self.s_km, self.unit(h, r) * 3 + i + 1)
            for j in range(nt):
                last = pe.transpose(self.ps_turn[:, i, j * P:(j + 1) * P],
                                    acc[:, (t0 + j) * P:(t0 + j + 1) * P], self.ident[:])
            last.then_inc(self.s_turn, 1)

    def turn_rows(self, pe, h):
        pe.wait_ge(self.s_ab, h * 7 + 7)
        pe.wait_ge(self.s_rows, h * 3 + 3)
        for i, (t0, nt) in enumerate(GROUPS):
            for j in range(nt):
                last = pe.transpose(self.ps_turn[0:2 * self.R, i, j * P:(j + 1) * P],
                                    self.ab[:, t0 + j].rearrange("p r c -> p (r c)"), self.ident[:])
            last.then_inc(self.s_abT, 1)

    def start_scalar(self, act):
        act.sem_inc(self.s_rows, 3)
        act.sem_inc(self.s_rows_out, 16)

    def rows_to_dram(self, act, h):
        act.wait_ge(self.s_rows_out, h * 16 + 16)
        for i, (t0, nt) in enumerate(GROUPS):
            act.wait_ge(self.s_abT, h * 3 + i + 4)
            act.copy(self.rows_sb[:, t0 * P:(t0 + nt) * P], self.ps_turn[0:2 * self.R, i, 0:nt * P]
                     ).then_inc(self.s_rows, 1)
        act.wait_ge(self.s_rows, h * 3 + 6)
        R = self.R
        act.dma_start(self.rows[bass.ds(h * R, R)].rearrange("r (c n) -> (r c) n", c=2),
                      self.rows_sb).then_inc(self.s_rows_out, 16)


def scaled_k(dve, kq, H, k08, k02, sem, slope=SLOPE):
    dve.tensor_scalar(k08[:], kq[:, :, :, H:2 * H], 1.0 - SLOPE, None, ALU.mult).then_inc(sem, 1)
    dve.tensor_scalar(k02[:], kq[:, :, :, H:2 * H], slope, None, ALU.mult).then_inc(sem, 1)


def tables_and_counts(nc, g, x, src, dst, etype, W1, q1, k1, W2, q2, k2, ident, hd, kq1, wqk2, feat1, counts, ct_all):
    N, D, NT, NP, KD, R = g.N, g.D, g.NT, g.NP, g.KD, g.R
    H, F = 4, D // 4
    CELLS = R * NP * NP
    EC_FULL = g.E // P
    EC_USED = -(-g.E // P)
    EC = -(-EC_USED // 8) * 8
    TAIL = g.E - EC_FULL * P
    PIECES = 20
    ZC = CELLS // P // PIECES
    NW = 3 * R
    TURNS_W = 2 * KD
    with ExitStack() as ctx:
        sb = lambda n, s, d=F32: ctx.enter_context(nc.sbuf_tensor(n, s, d))
        sem = lambda n: ctx.enter_context(nc.semaphore(n))
        edges_i = sb("edges_i", [P, 3, EC], I32)
        edges_f = sb("edges_f", [P, 3, EC])
        key = sb("key", [P, EC])
        key_i = sb("key_i", [P, EC], I32)
        packed = sb("packed", [P, EC])
        ones = sb("ones", [P, P])
        earlier = sb("earlier", [P, P])
        diag = sb("diag", [P, 2, 4, P])
        same = sb("same", [P, 8, P])
        part = sb("part", [P, 2, 2, NP])
        zero = part[:].rearrange("p a b n -> p (a b n)")[:, 0:ZC]
        spare = ct_all[:].bitcast(F32)
        h = spare[:, 0:NT * D].rearrange("p (t d) -> p t d", t=NT)
        wT = spare[:, NT * D:NT * D + KD * D].rearrange("p (k d) -> p k d", k=KD)
        hT = sb("hT", [P, KD, NP])
        stats = sb("stats", [P, NT, 2, 6])
        mv = sb("mv", [P, NT, 2])
        std = sb("std", [P, NT])
        rstd = sb("rstd", [P, NT])
        shift = sb("shift", [P, NT])
        eps = sb("eps", [P, 1])
        w = sb("w", [P, 2, KD, D])
        qk1 = sb("qk1", [P, KD, 2 * H])
        qk2 = sb("qk2", [P, 2, KD])
        wqk1 = sb("wqk1", [P, KD, R, 2 * H])
        stage = sb("stage", [P, 2, H, F + 1])
        ps_turn = ctx.enter_context(nc.psum_tensor("ps_turn", [P, 3, 512], F32))
        ps_feat = ctx.enter_context(nc.psum_tensor("ps_feat", [P, 2, 2, 512], F32))
        ps_small = ctx.enter_context(nc.psum_tensor("ps_small", [P, 512], F32))
        ps_key = ps_turn[:, 2, :]
        hd.ps_turn = ps_turn

        s_clean = sem("a_clean")
        s_const = sem("a_const")
        s_zero = sem("a_zero")
        s_edges = sem("a_edges")
        s_x = sem("a_x")
        s_qk = sem("a_qk")
        s_cleared = sem("a_cleared")
        s_w = [sem("a_w0"), sem("a_w1")]
        s_wused = sem("a_wused")
        s_stat = sem("a_stat")
        s_norm = sem("a_norm")
        s_h = sem("a_h")
        s_turn = sem("a_turn")
        s_turned = sem("a_turned")
        s_wqk = sem("a_wqk")
        s_wqk_out = sem("a_wqk_out")
        s_feat = sem("a_feat")
        s_feat_out = sem("a_feat_out")
        s_spill = [sem("a_spill0"), sem("a_spill1")]
        s_key = sem("a_keys")
        s_diag = sem("a_diag")
        s_bcast = sem("a_bcast")
        s_same = sem("a_same")
        s_index = sem("a_index")
        s_scat = [sem("a_scat0"), sem("a_scat1")]
        s_part = [sem("a_part0"), sem("a_part1")]
        s_ct = sem("a_ct")
        block = ctx.enter_context(nc.Block())

        @block.sync
        def _(sp):
            sp.wait_ge(s_clean, 2)
            for i, a in enumerate((src, dst, etype)):
                sp.dma_start(edges_i[:, i, 0:EC_FULL],
                             a[0:EC_FULL * P].rearrange("(p c) -> p c", p=P)).then_inc(s_edges, 16)
                sp.dma_start(edges_i[0:TAIL, i, EC_FULL:EC_FULL + 1],
                             a[EC_FULL * P:g.E].rearrange("(p c) -> p c", c=1)).then_inc(s_edges, 16)
            for vec, sl in ((q1, qk1[:, :, 0:H]), (k1, qk1[:, :, H:2 * H])):
                sp.dma_start(sl, vec.rearrange("(k p) h -> p k h", p=P)).then_inc(s_qk, 16)
            for c, vec in enumerate((q2, k2)):
                sp.dma_start(qk2[:, c, :], vec.rearrange("(k p) h -> p (k h)", p=P),
                             allow_slow_non_contiguous=True).then_inc(s_qk, 16)

            def load_w(i):
                big = (W1, W2, W1)[i // R][i % R]
                sp.dma_start(w[:, i % 2], big.rearrange("(k p) f -> p k f", p=P)).then_inc(s_w[i % 2], 16)

            load_w(0)
            load_nodes(sp, g, h, x, s_x)
            load_w(1)
            sp.wait_ge(s_zero, 1)
            for table in counts:
                flat = table.rearrange("(k p c) o -> k p (c o)", p=P, k=PIECES)
                for k in range(PIECES):
                    sp.dma_start(flat[k], zero).then_inc(s_cleared, 16)
            for i in range(2, NW):
                sp.wait_ge(s_wused, i - 1)
                load_w(i)
            for q in (0, 1):
                sp.wait_ge(s_scat[q], 16 * len(range(q, EC_USED, 2)))
            tiles = [c.rearrange("(r s p n) o -> (r s) p (n o)", r=R, s=NT, p=P) for c in counts]
            for n in range(R * NT):
                if n >= 2:
                    sp.wait_ge(s_ct, n - 1)
                for k in range(2):
                    sp.dma_start(part[:, n % 2, k, :], tiles[k][n]).then_inc(s_part[n % 2], 16)

        @block.gpsimd
        def _(pool):
            pool.memset(edges_i[:], R).then_inc(s_clean, 1)
            pool.memset(h[:, NT - 1, :], 0.0).then_inc(s_clean, 1)
            pool.memset(ident[:], 0.0).then_inc(s_const, 1)
            pool.memset(earlier[:], float(2 * P + 1)).then_inc(s_const, 1)
            pool.memset(ones[:], 1.0).then_inc(s_const, 1)
            pool.memset(eps[:], LN_EPS).then_inc(s_const, 1)
            pool.memset(stage[:], 1.0).then_inc(s_const, 1)
            pool.wait_ge(s_const, 2)
            pool.affine_select(out=ident[:], in_=ident[:], compare_op=ALU.not_equal, fill=1.0, base=0,
                               pattern=[[-1, P]], channel_multiplier=1).then_inc(s_const, 1)
            pool.affine_select(out=earlier[:], in_=earlier[:], compare_op=ALU.is_gt, fill=1.0, base=0,
                               pattern=[[-1, P]], channel_multiplier=1).then_inc(s_const, 1)
            pool.wait_ge(s_const, 7)
            pool.wait_ge(s_key, 3)
            pool.sem_inc(s_bcast, 2)
            with pool.Fori(0, EC // 8) as i:
                for b in range(2):
                    pool.wait_ge(s_bcast, i * 2 + b + 1)
                    pool.tensor_tensor(diag[:, b], ident[:].rearrange("p (a e) -> p a e", a=1).broadcast_to([P, 4, P]),
                                       key[:, bass.ds(i * 8 + b * 4, 4)].rearrange("p (a e) -> p a e", e=1)
                                       .broadcast_to([P, 4, P]), ALU.mult).then_inc(s_diag, 1)
            pool.wait_ge(s_index, 1)
            pool.wait_ge(s_cleared, 16 * 2 * PIECES)
            for c in range(EC_USED):
                if c >= 2:
                    pool.wait_ge(s_scat[c % 2], 16 * (c // 2))
                pool.indirect_dma_start(out=counts[c % 2],
                                        out_offset=bass.IndirectOffsetOnAxis(ap=key_i[:, c:c + 1], axis=0),
                                        in_=packed[:, c:c + 1], in_offset=None, bounds_check=CELLS - 1,
                                        oob_is_err=False, compute_op=ALU.add).then_inc(s_scat[c % 2], 16)

        @block.tensor
        def _(pe):
            hd.start_tensor(pe)
            turns = [0]

            def turn(blocks):
                n = turns[0]
                turns[0] += 1
                if n >= 2:
                    pe.wait_ge(s_turned, n - 1)
                for j, blk in enumerate(blocks):
                    last = pe.transpose(ps_turn[:, n % 2, j * P:(j + 1) * P], blk, ident[:])
                last.then_inc(s_turn, 1)

            def turn_weights(i, group):
                f, half = divmod(group, 2)
                turn([w[:, i % 2, 3 * half + j, f * P:(f + 1) * P] for j in range(3)])

            def logit_weights(i):
                c = 2 * H if i < R else 2
                pe.wait_ge(s_turned, turns[0])
                if i >= 1:
                    pe.wait_ge(s_wqk_out, i)
                for kd in range(KD):
                    for f in range(KD):
                        last = pe.matmul(ps_small[:, kd * c:(kd + 1) * c], wT[:, f, kd * P:(kd + 1) * P],
                                         qk1[:, f, :] if i < R else qk2[:, :, f],
                                         start=(f == 0), stop=(f == KD - 1), skip_group_check=True)
                last.then_inc(s_wqk, 1)

            def compare(m):
                pe.wait_ge(s_diag, m + 1)
                pe.wait_ge(s_same, 4 * m + 8)
                pe.matmul(ps_key, ones[:], diag[:, m % 2].rearrange("p a e -> p (a e)"),
                          start=True, stop=True).then_inc(s_bcast, 1)

            pe.wait_ge(s_const, 7)
            pe.wait_ge(s_qk, 64)
            for m in range(EC // 4):
                compare(m)
                i, group = divmod(m, TURNS_W)
                if i < 2:
                    if group == 0:
                        pe.wait_ge(s_w[i % 2], 16 * (i // 2 + 1))
                    turn_weights(i, group)
                    if group == TURNS_W - 1:
                        logit_weights(i)
                        pe.wait_ge(s_wqk, i + 1)
                        pe.sem_inc(s_wused, 1)
            for i in range(2, 2 * R):
                pe.wait_ge(s_w[i % 2], 16 * (i // 2 + 1))
                for group in range(TURNS_W):
                    turn_weights(i, group)
                logit_weights(i)
                pe.wait_ge(s_wqk, i + 1)
                pe.sem_inc(s_wused, 1)
            for t in range(NT):
                pe.wait_ge(s_h, t + 1)
                for half in range(2):
                    turn([h[:, t, (3 * half + j) * P:(3 * half + j + 1) * P] for j in range(3)])
            pe.wait_ge(s_turned, turns[0])
            pe.wait_ge(s_wqk_out, 2 * R)
            for t in range(NT):
                for kd in range(KD):
                    last = pe.matmul(ps_small[:, t * 2 * H * R:(t + 1) * 2 * H * R], hT[:, kd, t * P:(t + 1) * P],
                                     wqk1[:, kd].rearrange("p r c -> p (r c)"), start=(kd == 0), stop=(kd == KD - 1),
                                     skip_group_check=True)
            last.then_inc(s_wqk, 1)
            for n in range(R * NT):
                r, t = divmod(n, NT)
                i = 2 * R + r
                if t == 0:
                    pe.wait_ge(s_w[i % 2], 16 * (i // 2 + 1))
                if n >= 2:
                    pe.wait_ge(s_feat_out, 2 * (n - 1))
                for half in range(2):
                    for kd in range(KD):
                        last = pe.matmul(ps_feat[:, n % 2, half, 0:D // 2], hT[:, kd, t * P:(t + 1) * P],
                                         w[:, i % 2, kd, half * D // 2:(half + 1) * D // 2],
                                         start=(kd == 0), stop=(kd == KD - 1))
                last.then_inc(s_feat, 1)
                if t == NT - 1:
                    pe.wait_ge(s_feat, n + 1)
                    pe.sem_inc(s_wused, 1)
            pe.wait_ge(s_same, EC + 8)
            for r in range(R):
                for j in range(2):
                    hd.turn_unit(pe, j, r)
            for j in range(2):
                hd.turn_rows(pe, j)

        @block.scalar
        def _(act):
            hd.start_scalar(act)
            act.wait_ge(s_const, 7)

            def turned(n, out):
                act.wait_ge(s_turn, n + 1)
                act.copy(out, ps_turn[:, n % 2, 0:3 * P].rearrange("p (k n) -> p k n", k=3)).then_inc(s_turned, 1)

            for i in range(2 * R):
                if i >= 1:
                    act.wait_ge(s_wqk, i)
                for group in range(TURNS_W):
                    f, half = divmod(group, 2)
                    turned(TURNS_W * i + group, wT[:, f, half * 3 * P:(half + 1) * 3 * P].rearrange(
                        "p (k n) -> p k n", k=3))
            act.wait_ge(s_stat, 3 * NT)
            act.activation(std[:], mv[:, :, 1], ACT.Sqrt, bias=eps[:]).then_inc(s_norm, 1)
            act.wait_ge(s_norm, 3)
            for t in range(NT):
                act.activation(h[:, t, :], h[:, t, :], ACT.Relu, bias=shift[:, t:t + 1],
                               scale=rstd[:, t:t + 1]).then_inc(s_h, 1)
            for t in range(NT):
                for half in range(2):
                    turned(2 * R * TURNS_W + 2 * t + half, hT[:, 3 * half:3 * half + 3, t * P:(t + 1) * P])
            for q in range(2):
                act.sem_inc(s_spill[q], 16)
            with act.Fori(0, R * NT // 2) as i:
                for q in range(2):
                    act.wait_ge(s_feat, i * 2 + q + 1)
                    act.wait_ge(s_spill[q], i * 16 + 16)
                    for half in range(2):
                        act.copy(stage[:, q, 2 * half:2 * half + 2, 0:F],
                                 ps_feat[:, q, half, 0:2 * F].rearrange("p (a f) -> p a f", a=2)).then_inc(s_feat_out, 1)
                    act.wait_ge(s_feat_out, i * 4 + 2 * q + 2)
                    act.dma_start(feat1[:, bass.ds(i * 2 + q, 1)].rearrange("h n p f -> p (n h) f"),
                                  stage[:, q]).then_inc(s_spill[q], 16)
            for j in range(2):
                hd.rows_to_dram(act, j)
            for q in range(2):
                act.wait_ge(s_spill[q], 16 * (R * NT // 2) + 16)

        @block.vector
        def _(dve):
            hd.start_vector(dve)
            dve.memset(zero, 0.0).then_inc(s_zero, 1)
            dve.wait_ge(s_edges, 96)
            dve.tensor_copy(edges_f[:], edges_i[:]).then_inc(s_key, 1)
            dve.wait_ge(s_key, 1)
            dve.scalar_tensor_tensor(out=packed[:], in0=edges_f[:, 2, :], scalar=float(NP), in1=edges_f[:, 0, :],
                                     op0=ALU.mult, op1=ALU.add).then_inc(s_key, 1)
            dve.wait_ge(s_key, 2)
            dve.scalar_tensor_tensor(out=key[:], in0=packed[:], scalar=float(NP), in1=edges_f[:, 1, :],
                                     op0=ALU.mult, op1=ALU.add).then_inc(s_key, 1)
            dve.wait_ge(s_key, 3)
            dve.sem_inc(s_same, 8)
            logit_weights_out = [0]

            def small_out(i):
                dve.wait_ge(s_wqk, i + 1)
                c, out = (2 * H, wqk1[:, :, i, :]) if i < R else (2, wqk2[:, :, i - R, :])
                dve.tensor_copy(out, ps_small[:, 0:KD * c].rearrange("p (k c) -> p k c", c=c)).then_inc(s_wqk_out, 1)

            for m in range(EC // 4):
                dve.wait_ge(s_bcast, m + 3)
                for a in range(4):
                    c = 4 * m + a
                    dve.wait_ge(s_same, c + 1)
                    dve.scalar_tensor_tensor(out=same[:, c % 8], in0=ps_key[:, a * P:(a + 1) * P],
                                             scalar=key[:, c:c + 1], in1=earlier[:],
                                             op0=ALU.is_equal, op1=ALU.mult,
                                             accum_out=packed[:, c:c + 1]).then_inc(s_same, 1)
                if m in (TURNS_W + 1, 2 * TURNS_W + 1):
                    small_out(m // TURNS_W - 1)
            dve.wait_ge(s_same, EC + 8)
            dve.tensor_scalar(edges_f[:, 0, :], packed[:], float(2 * P), float(2 ** 23), ALU.is_ge,
                              ALU.mult).then_inc(s_key, 1)
            dve.wait_ge(s_key, 4)
            dve.tensor_tensor(edges_f[:, 1, :], key[:], edges_f[:, 0, :], ALU.add).then_inc(s_key, 1)
            dve.wait_ge(s_key, 5)
            dve.tensor_copy(key_i[:], edges_f[:, 1, :]).then_inc(s_index, 1)
            dve.wait_ge(s_x, 32)
            layernorm_stats(dve, g, h, stats, mv, s_stat)
            for i in range(2, 2 * R):
                small_out(i)
            dve.wait_ge(s_norm, 1)
            dve.reciprocal(rstd[:], std[:]).then_inc(s_norm, 1)
            dve.wait_ge(s_norm, 2)
            dve.scalar_tensor_tensor(out=shift[:], in0=mv[:, :, 0], scalar=-1.0, in1=rstd[:],
                                     op0=ALU.mult, op1=ALU.mult).then_inc(s_norm, 1)
            dve.wait_ge(s_wqk, 2 * R + 1)
            dve.tensor_copy(kq1[:], ps_small[:, 0:NT * R * 2 * H].rearrange("p (t r c) -> p t r c", t=NT, r=R)
                            ).then_inc(s_wqk_out, 1)
            dve.wait_ge(s_wqk_out, 2 * R + 1)
            for r in range(R):
                for s in range(NT):
                    n = r * NT + s
                    dve.wait_ge(s_part[n % 2], 32 * (n // 2 + 1))
                    dve.tensor_tensor(hd.ct[r][:, s, :], part[:, n % 2, 0, :], part[:, n % 2, 1, :],
                                      ALU.add).then_inc(s_ct, 1)
                    dve.wait_ge(s_ct, n + 1)
                    if n >= 2:
                        dve.wait_ge(hd.s_first[1], n - 1)
                    hd.mask(dve, r, s)
                    dve.wait_ge(hd.s_miss, n + 1)
                    for j in range(2):
                        hd.first_step(dve, j, r, s)
                for j in range(2):
                    hd.reduce_unit(dve, j, r)
            for j in range(2):
                hd.rows_of_head(dve, j)


def multi_head(nc, g, tag, hd, F, feat, post_setup):
    NT, NP, H, R, ct, kq = g.NT, g.NP, hd.H, hd.R, hd.ct, hd.kq
    rows = hd.rows
    per_bank = 512 // (F + 1)
    banks = -(-NT // per_bank)
    UNIT = NT
    PE0 = 2 * UNIT
    T0 = 2 * UNIT
    direct = [s for s in range(NT) if R > 1 and s % SLOTS == SLOTS - 1]
    ON_POOL = NT - len(direct)
    exps_before = [sum(1 if t in direct else 2 for t in range(s)) for s in range(NT + 1)]
    pool_before = [sum(t not in direct for t in range(s)) for s in range(NT)]
    with ExitStack() as ctx:
        sb = lambda n, s, d=F32: ctx.enter_context(nc.sbuf_tensor(tag + n, s, d))
        sem = lambda n: ctx.enter_context(nc.semaphore(tag + n))
        cf = sb("cf", [P, 2, NP]) if direct else None
        hd.ps_turn = ctx.enter_context(nc.psum_tensor(tag + "ps_turn", [P, 3, 512], F32))
        wt = sb("wt", [P, SLOTS, NP])
        row = sb("row", [P, 2, 2, NP])
        ft = sb("ft", [P, 2, NT, F + 1])
        k08 = sb("k08", [P, NT, R, H])
        k02 = sb("k02", [P, NT, R, H])
        k02n = sb("k02n", [P, NT, R, H])
        rz = sb("rz", [P, 2, banks, per_bank])
        ps_out = ctx.enter_context(nc.psum_tensor(tag + "ps_out", [P, banks, 512], F32))
        s_k = sem("k_scaled")
        s_row = sem("row_in")
        s_ft = sem("ft_in")
        s_lg = sem("logit_made")
        s_exp = sem("exp_made")
        s_wt = sem("weight_made")
        s_wtd = sem("weight_direct")
        s_cf = sem("counts_float")
        s_pe = sem("step_summed")
        s_rz = sem("rz_made")
        s_raw = sem("sums_out")
        post = post_setup(ctx, s_raw, banks)
        block = ctx.enter_context(nc.Block())

        def over_heads(eng, body):
            body(0, False, False, True)
            if H > 3:
                with eng.Fori(1, H - 2) as h:
                    body(h, True, True, True)
            body(H - 2, True, True, False)
            body(H - 1, True, False, False)

        @block.sync
        def _(sp):
            post.sync(sp, H)
            for u in range(H * R):
                h, r = divmod(u, R)
                if u >= 2:
                    sp.wait_ge(s_pe, (u + 1) * UNIT)
                sp.dma_start(ft[:, u % 2], feat[h, r * NT:(r + 1) * NT].rearrange("s p f -> p s f")
                             ).then_inc(s_ft, 16)
                if r == 0:
                    sp.wait_ge(hd.s_rows_out, h * 16 + 32)
                if u >= 2:
                    sp.wait_ge(s_lg, (u + 1) * UNIT)
                sp.dma_start(row[:, u % 2].rearrange("p c n -> p (c n)"),
                             rows[u:u + 1].broadcast_to([P, 2 * NP])).then_inc(s_row, 16)
                sp.wait_ge(s_ft, u * 16 + 16)
                sp.wait_ge(s_row, u * 16 + 16)

        @block.vector
        def _(dve):
            dve.sem_inc(s_lg, T0)
            dve.sem_inc(s_raw, banks)
            scaled_k(dve, kq, H, k08, k02, s_k)
            dve.tensor_scalar(k02n[:], kq[:, :, :, H:2 * H], -SLOPE, None, ALU.mult).then_inc(s_k, 1)
            dve.wait_ge(s_k, 3)
            if hd.all_miss:
                hd.start_vector(dve)
                for r in range(R):
                    for s in range(NT):
                        hd.mask(dve, r, s)
                        dve.wait_ge(hd.s_miss, s + 1)
                        for j in range(2):
                            hd.first_step(dve, j, r, s)
                    for j in range(2):
                        hd.reduce_unit(dve, j, r)
                for j in range(2):
                    hd.rows_of_head(dve, j)

            def sums_out(h):
                dve.wait_ge(s_pe, (h + 1) * R * UNIT + PE0)
                for b in range(banks):
                    nt = min(per_bank, NT - b * per_bank)
                    v = ps_out[:, b, 0:nt * (F + 1)].rearrange("p (t f) -> p t f", t=nt)
                    dve.tensor_scalar(rz[:, 0, b, 0:nt], v[:, :, F], Z_EPS, None, post.guard).then_inc(s_rz, 1)
                    dve.wait_ge(s_rz, h * 2 * banks + 2 * b + 1)
                    dve.reciprocal(rz[:, 1, b, 0:nt], rz[:, 0, b, 0:nt]).then_inc(s_rz, 1)
                post.before_sums(dve, h)
                for b in range(banks):
                    nt = min(per_bank, NT - b * per_bank)
                    v = ps_out[:, b, 0:nt * (F + 1)].rearrange("p (t f) -> p t f", t=nt)
                    dve.wait_ge(s_rz, h * 2 * banks + 2 * b + 2)
                    dve.tensor_tensor(post.y[:, b * per_bank:b * per_bank + nt, :], v[:, :, 0:F],
                                      rz[:, 1, b, 0:nt].rearrange("p (t o) -> p t o", o=1).broadcast_to([P, nt, F]),
                                      ALU.mult).then_inc(s_raw, 1)

            def body(h, pending_sums, pending_rows, maximum):
                for r in range(R):
                    u = h * R + r

                    def logits(s):
                        n = u * UNIT + s
                        dve.wait_ge(s_pe, n + 1 + PE0 - SLOTS)
                        if s == 0:
                            dve.wait_ge(s_row, u * 16 + 16)
                        slot = u % 2
                        a = row[:, bass.ds(slot, 1), 0, :].rearrange("p o n -> p (o n)")
                        b = row[:, bass.ds(slot, 1), 1, :].rearrange("p o n -> p (o n)")
                        dve.scalar_tensor_tensor(out=wt[:, s % SLOTS], in0=a, scalar=k08[:, s, r, bass.ds(h, 1)],
                                                 in1=b, op0=ALU.add, op1=ALU.max).then_inc(s_lg, 1)

                    logits(0)
                    for s in range(NT):
                        if s + 1 < NT:
                            logits(s + 1)
                        if s == 0 and (r > 0 and maximum or r == 0 and pending_rows):
                            hd.reduce_unit(dve, h + 2 if r > 0 else h + 1, (r - 1) % R)
                            if r == 0:
                                hd.rows_of_head(dve, h + 1)
                        if maximum:
                            n = hd.later_unit(h + 2, r) * NT + s
                            if not hd.all_miss:
                                dve.wait_ge(hd.s_later, n - 1) if s >= 2 or r > 0 else None
                                hd.mask(dve, r, s)
                                dve.wait_ge(hd.s_miss, (R + r) * NT + h * UNIT * R + s + 1)
                            if s == 0:
                                dve.wait_ge(hd.s_turn, hd.unit(h + 2, r) * 3)
                            hd.later_step(dve, h + 2, r, s)
                        if s in direct:
                            dve.wait_ge(s_exp, u * exps_before[NT] + exps_before[s + 1])
                            dve.scalar_tensor_tensor(out=wt[:, s % SLOTS], in0=wt[:, s % SLOTS], scalar=1.0,
                                                     in1=ct[r][:, s, :], op0=ALU.min, op1=ALU.mult).then_inc(s_wtd, 1)
                        if r == 0 and s == 2 and pending_sums:
                            sums_out(h - 1)
                        if r == R - 1 and s == NT - 2 and pending_sums:
                            post.vector(dve, h - 1)

            over_heads(dve, body)
            sums_out(H - 1)
            post.vector(dve, H - 1)

        @block.scalar
        def _(act):
            act.wait_ge(s_k, 3)
            if hd.all_miss:
                hd.start_scalar(act)
                for h in range(2):
                    hd.rows_to_dram(act, h)

            def body(h, pending_sums, pending_rows, maximum):
                for r in range(R):
                    for s in range(NT):
                        n = (h * R + r) * UNIT + s
                        if s in direct:
                            act.wait_ge(s_lg, n + 1 + T0)
                            act.activation(wt[:, s % SLOTS], wt[:, s % SLOTS], ACT.Exp,
                                           bias=k02[:, s, r, bass.ds(h, 1)]).then_inc(s_exp, 1)
                        else:
                            if cf is not None:
                                j = pool_before[s]
                                act.wait_ge(s_wt, (h * R + r) * ON_POOL + j - 1 + ON_POOL)
                                act.copy(cf[:, j % 2], ct[r][:, s, :]).then_inc(s_cf, 1)
                            act.wait_ge(s_lg, n + 1 + T0)
                            act.activation(wt[:, s % SLOTS], wt[:, s % SLOTS], ACT.Relu, scale=-1.0,
                                           bias=k02n[:, s, r, bass.ds(h, 1)]).then_inc(s_exp, 1)
                            act.wait_ge(s_exp, (h * R + r) * exps_before[NT] + exps_before[s] + 1)
                            act.activation(wt[:, s % SLOTS], wt[:, s % SLOTS], ACT.Exp, scale=-1.0).then_inc(s_exp, 1)
                        if r == 0 and s == 3 and pending_rows:
                            hd.rows_to_dram(act, h + 1)
                        if r == R - 1 and s == NT // 2 and pending_sums:
                            post.scalar(act, h - 1)

            over_heads(act, body)
            post.scalar(act, H - 1)
            act.wait_ge(hd.s_rows_out, 16 * H + 16)

        @block.tensor
        def _(pe):
            pe.sem_inc(s_pe, PE0)
            if hd.all_miss:
                hd.start_tensor(pe)
                for r in range(R):
                    for h in range(2):
                        hd.turn_unit(pe, h, r)
                for h in range(2):
                    hd.turn_rows(pe, h)

            def body(h, pending_sums, pending_rows, maximum):
                for r in range(R):
                    u = h * R + r
                    for s in range(NT):
                        if s == TURN_STEP and maximum:
                            hd.turn_unit(pe, h + 2, r)
                        if s in direct:
                            pe.wait_ge(s_wtd, u * len(direct) + s // SLOTS + 1)
                        else:
                            pe.wait_ge(s_wt, u * ON_POOL + pool_before[s] + 1 + ON_POOL)
                        if s == 0:
                            pe.wait_ge(s_ft, u * 16 + 16)
                            if r == 0:
                                pe.wait_ge(s_raw, h * banks + banks)
                        for t in range(NT):
                            b, j = divmod(t, per_bank)
                            last = pe.matmul(ps_out[:, b, j * (F + 1):(j + 1) * (F + 1)],
                                             wt[:, s % SLOTS, t * P:(t + 1) * P],
                                             ft[:, bass.ds(u % 2, 1), s, :].rearrange("p o f -> p (o f)"),
                                             start=(r == 0 and s == 0 and j == 0),
                                             stop=(r == R - 1 and s == NT - 1), skip_group_check=True)
                        last.then_inc(s_pe, 1)
                        if r == 0 and s == 1 and pending_rows:
                            hd.turn_rows(pe, h + 1)

            over_heads(pe, body)

        @block.gpsimd
        def _(pool):
            post.start_pool(pool)
            pool.sem_inc(s_wt, ON_POOL)
            for h in range(H):
                for r in range(R):
                    u = h * R + r
                    for s in range(NT):
                        if s not in direct:
                            counts = ct[r][:, s, :]
                            if cf is not None:
                                counts = cf[:, pool_before[s] % 2]
                                pool.wait_ge(s_cf, u * ON_POOL + pool_before[s] + 1)
                            pool.wait_ge(s_exp, u * exps_before[NT] + exps_before[s + 1])
                            pool.tensor_tensor(wt[:, s % SLOTS], wt[:, s % SLOTS], counts, ALU.mult
                                               ).then_inc(s_wt, 1)
                        if r == 0 and s == NT // 2 and h >= 1:
                            post.pool(pool, h - 1)
                if h >= 1:
                    post.store(pool, h - 1)
            post.pool(pool, H - 1)
            post.store(pool, H - 1)


def relational_post(nc, g, b1, h2):
    H, F, NT = 4, g.D // 4, g.NT

    def setup(ctx, s_raw, banks):
        sb = lambda n, s, d=F32: ctx.enter_context(nc.sbuf_tensor("r1" + n, s, d))
        sem = lambda n: ctx.enter_context(nc.semaphore("r1" + n))
        bias = sb("bias", [P, g.D])
        y = sb("y", [P, NT, F])
        e = sb("e", [P, NT, F])
        s_b = sem("bias_in")
        s_y = sem("y")
        s_e = sem("elu_exp")
        s_h = sem("elu")
        s_out = sem("h2_out")
        s_free = sem("y_free")

        class Post:
            guard = ALU.add

            def sync(self, sp, H):
                sp.dma_start(bias[:], b1.rearrange("(o d) -> o d", o=1).broadcast_to([P, g.D])).then_inc(s_b, 16)
                sp.wait_ge(s_b, 16)

            def before_sums(self, dve, h):
                dve.wait_ge(s_free, h + 1)

            def scalar(self, act, h):
                act.wait_ge(s_y, h + 1)
                act.activation(e[:], y[:], ACT.Relu, scale=-1.0).then_inc(s_e, 1)
                act.wait_ge(s_e, h * 3 + 1)
                act.activation(e[:], e[:], ACT.Exp, scale=-1.0).then_inc(s_e, 1)
                act.activation(y[:], y[:], ACT.Relu).then_inc(s_e, 1)

            def vector(self, dve, h):
                dve.wait_ge(s_e, h * 3 + 3)
                dve.scalar_tensor_tensor(out=y[:], in0=e[:], scalar=-1.0, in1=y[:], op0=ALU.add,
                                         op1=ALU.add).then_inc(s_h, 1)

            def start_pool(self, pool):
                pool.sem_inc(s_free, 1)
                pool.wait_ge(s_b, 16)

            def pool(self, pool, h):
                bh = bias[:, h * F:(h + 1) * F].rearrange("p (o f) -> p o f", o=1).broadcast_to([P, NT, F])
                pool.wait_ge(s_raw, h * banks + 2 * banks)
                pool.tensor_tensor(y[:], y[:], bh, ALU.add).then_inc(s_y, 1)

            def store(self, pool, h):
                pool.wait_ge(s_h, h + 1)
                pool.dma_start(h2[:, :, h * F:(h + 1) * F], y[:]).then_inc(s_out, 16)
                pool.wait_ge(s_out, 16 * (h + 1))
                pool.sem_inc(s_free, 1)

        post = Post()
        post.y = y
        return post

    return setup


def final_post(nc, g, x1, res, out):
    H, F, NT = 12, g.D // 12, g.NT

    def setup(ctx, s_raw, banks):
        sb = lambda n, s, d=F32: ctx.enter_context(nc.sbuf_tensor("g1" + n, s, d))
        sem = lambda n: ctx.enter_context(nc.semaphore("g1" + n))
        y = sb("y", [P, NT, F])
        s_y = sem("y")
        s_h = sem("summed")
        s_out = sem("out")
        s_free = sem("y_free")
        full = (NT - 1) * P

        class Post:
            guard = ALU.max

            def sync(self, sp, H):
                pass

            def before_sums(self, dve, h):
                dve.wait_ge(s_free, h + 1)

            def scalar(self, act, h):
                pass

            def vector(self, dve, h):
                dve.wait_ge(s_y, h + 1)
                dve.scalar_tensor_tensor(out=y[:], in0=y[:], scalar=0.0, in1=x1[:, :, bass.ds(h * F, F)],
                                         op0=ALU.max, op1=ALU.add).then_inc(s_h, 1)

            def start_pool(self, pool):
                pool.sem_inc(s_free, 1)

            def pool(self, pool, h):
                pool.wait_ge(s_raw, h * banks + 2 * banks)
                pool.tensor_tensor(y[:], y[:], res[:, :, h * F:(h + 1) * F], ALU.add).then_inc(s_y, 1)

            def store(self, pool, h):
                pool.wait_ge(s_h, h + 1)
                pool.dma_start(out[0:full, h * F:(h + 1) * F].rearrange("(t p) d -> p t d", p=P),
                               y[:, 0:NT - 1, :]).then_inc(s_out, 16)
                pool.dma_start(out[full:g.N, h * F:(h + 1) * F], y[0:g.LAST, NT - 1, :]).then_inc(s_out, 16)
                pool.wait_ge(s_out, 32 * (h + 1))
                pool.sem_inc(s_free, 1)

        post = Post()
        post.y = y
        return post

    return setup


def second_logits(nc, g, ct, h2d, h2, kq2, wqk2, ident, rows):
    NT, NP, KD, R, D = g.NT, g.NP, g.KD, g.R, g.D
    with ExitStack() as ctx:
        sb = lambda n, s, d=F32: ctx.enter_context(nc.sbuf_tensor("l2" + n, s, d))
        sem = lambda n: ctx.enter_context(nc.semaphore("l2" + n))
        hd = Heads(nc, ctx, g, "l2", 1, R, ct, kq2, ident, rows)
        hd.ps_turn = ctx.enter_context(nc.psum_tensor("l2ps_turn", [P, 3, 512], F32))
        h2T = sb("h2T", [P, KD, NP])
        ps_h = ctx.enter_context(nc.psum_tensor("l2ps_h", [P, 2, 512], F32))
        ps_kq = ctx.enter_context(nc.psum_tensor("l2ps_kq", [P, 512], F32))
        s_in = sem("in")
        s_hT = sem("hT")
        s_hT_out = sem("hT_out")
        s_kq = sem("kq")
        s_kq_out = sem("kq_out")
        block = ctx.enter_context(nc.Block())

        @block.sync
        def _(sp):
            sp.dma_start(h2[:], h2d).then_inc(s_in, 16)

        @block.tensor
        def _(pe):
            hd.start_tensor(pe)
            pe.wait_ge(s_in, 16)
            for n in range(2 * NT):
                t, half = divmod(n, 2)
                if n >= 2:
                    pe.wait_ge(s_hT_out, n - 1)
                for j in range(3):
                    kd = 3 * half + j
                    last = pe.transpose(ps_h[:, n % 2, j * P:(j + 1) * P], h2[:, t, kd * P:(kd + 1) * P], ident[:])
                last.then_inc(s_hT, 1)
            pe.wait_ge(s_hT_out, 2 * NT)
            for t in range(NT):
                for kd in range(KD):
                    last = pe.matmul(ps_kq[:, t * 2 * R:(t + 1) * 2 * R], h2T[:, kd, t * P:(t + 1) * P],
                                     wqk2[:, kd].rearrange("p r c -> p (r c)"), start=(kd == 0), stop=(kd == KD - 1),
                                     skip_group_check=True)
            last.then_inc(s_kq, 1)
            for r in range(R):
                hd.turn_unit(pe, 0, r)
            hd.turn_rows(pe, 0)

        @block.scalar
        def _(act):
            hd.start_scalar(act)
            for n in range(2 * NT):
                t, half = divmod(n, 2)
                act.wait_ge(s_hT, n + 1)
                act.copy(h2T[:, 3 * half:3 * half + 3, t * P:(t + 1) * P],
                         ps_h[:, n % 2, 0:3 * P].rearrange("p (k n) -> p k n", k=3)).then_inc(s_hT_out, 1)
            hd.rows_to_dram(act, 0)
            act.wait_ge(hd.s_rows_out, 32)

        @block.vector
        def _(dve):
            hd.start_vector(dve)
            dve.wait_ge(s_kq, 1)
            dve.tensor_copy(kq2[:], ps_kq[:, 0:NT * 2 * R].rearrange("p (t r c) -> p t r c", t=NT, r=R)
                            ).then_inc(s_kq_out, 1)
            dve.wait_ge(s_kq_out, 1)
            for r in range(R):
                for s in range(NT):
                    hd.mask(dve, r, s)
                    dve.wait_ge(hd.s_miss, r * NT + s + 1)
                    hd.first_step(dve, 0, r, s)
                hd.reduce_unit(dve, 0, r)
            hd.rows_of_head(dve, 0)


def second_layer(nc, g, ct, h2, kq2, rows, W2, b2, x, x1):
    NT, NP, KD, R, D = g.NT, g.NP, g.KD, g.R, g.D
    TG = 2
    W = TG * P
    NG = NT // TG
    RING = NT
    full = (NT - 1) * P
    with ExitStack() as ctx:
        sb = lambda n, s, d=F32: ctx.enter_context(nc.sbuf_tensor("m2" + n, s, d))
        sem = lambda n: ctx.enter_context(nc.semaphore("m2" + n))
        w = sb("w", [P, R, KD, D])
        row = sb("row", [P, 2 * R, W])
        wt = sb("wt", [P, RING, W])
        k08 = sb("k08", [P, NT, R, 1])
        k02 = sb("k02", [P, NT, R, 1])
        gT = sb("gT", [P, R, KD, W])
        zsum = sb("zsum", [P, W])
        ones = sb("ones", [P, 1])
        none = sb("none", [P, 1])
        rz = sb("rz", [P, 2])
        bias = sb("bias", [P, D])
        xt = sb("xt", [P, 2, D])
        ps_g = ctx.enter_context(nc.psum_tensor("m2ps_g", [P, 2, 3, 512], F32))
        ps_o = ctx.enter_context(nc.psum_tensor("m2ps_o", [P, 2, 512], F32))
        s_k = sem("k")
        s_one = sem("one")
        s_w = sem("w")
        s_b = sem("b")
        s_row = sem("row")
        s_x = [sem("x0"), sem("x1")]
        s_lg = sem("lg")
        s_exp = sem("exp")
        s_wt = sem("wt")
        s_pe = sem("pe")
        s_z = sem("z")
        s_g = sem("g")
        s_o = sem("o")
        s_rz = sem("rz")
        s_o_out = sem("o_out")
        s_st = [sem("st0"), sem("st1")]
        block = ctx.enter_context(nc.Block())
        U = R * NT

        @block.sync
        def _(sp):
            sp.dma_start(bias[:], b2.rearrange("(o d) -> o d", o=1).broadcast_to([P, D])).then_inc(s_b, 16)
            rv = rows.rearrange("r (c n) -> (r c) n", c=2)

            def load_rows(gr):
                sp.wait_ge(s_lg, (gr + 1) * U)
                sp.dma_start(row[:],
                             rv[:, bass.ds(gr * W, W)].rearrange("(o c) n -> o c n", o=1)
                             .broadcast_to([P, 2 * R, W])).then_inc(s_row, 16)
                sp.wait_ge(s_row, (gr + 1) * 16)

            load_rows(0)
            for r in range(R):
                sp.dma_start(w[:, r], W2[r].rearrange("(k p) f -> p k f", p=P)).then_inc(s_w, 16)
            sp.wait_ge(s_one, 3)
            for gr in range(NG):
                if gr + 1 < NG:
                    load_rows(gr + 1)
                for j in range(TG):
                    t = gr * TG + j
                    if gr >= 1:
                        sp.wait_ge(s_st[j], 16 * gr)
                    if t < NT - 1:
                        sp.dma_start(xt[:, j, :], x[t * P:(t + 1) * P, :]).then_inc(s_x[j], 16)
                    else:
                        sp.wait_ge(s_o_out, 3)
                        sp.dma_start(xt[0:g.LAST, j, :], x[full:g.N, :]).then_inc(s_x[j], 16)
                if gr >= 0:
                    for j in range(TG):
                        t = gr * TG + j
                        sp.wait_ge(s_o_out, 3 * (t + 1))
                        sp.dma_start(x1[:, t, :], xt[:, j, :]).then_inc(s_st[j], 16)
            for j in range(TG):
                sp.wait_ge(s_st[j], 16 * NG)

        @block.gpsimd
        def _(pool):
            pool.memset(ones[:], 1.0).then_inc(s_one, 1)
            pool.memset(none[:], 0.0).then_inc(s_one, 1)
            pool.memset(xt[:], 0.0).then_inc(s_one, 1)
            pool.sem_inc(s_z, RING)
            pool.wait_ge(s_one, 3)
            with pool.Fori(0, NG) as gr:
                for r in range(R):
                    for s in range(NT):
                        n = gr * U + r * NT + s
                        pool.wait_ge(s_wt, n + 1)
                        if r == 0 and s == 0:
                            pool.wait_ge(s_o, gr * TG + 1)
                            pool.tensor_tensor(zsum[:], wt[:, s], none[:].broadcast_to([P, W]), ALU.add).then_inc(s_z, 1)
                        else:
                            pool.wait_ge(s_z, n + RING)
                            pool.tensor_tensor(zsum[:], zsum[:], wt[:, s], ALU.add).then_inc(s_z, 1)

        @block.vector
        def _(dve):
            dve.sem_inc(s_lg, U)
            scaled_k(dve, kq2, 1, k08, k02, s_k)
            dve.wait_ge(s_k, 2)
            dve.wait_ge(s_b, 16)

            def steps(gr):
                dve.wait_ge(s_row, gr * 16 + 16)

                def logits(r, s):
                    n = gr * U + r * NT + s
                    dve.wait_ge(s_pe, n + 1)
                    dve.wait_ge(s_z, n + 1)
                    dve.scalar_tensor_tensor(out=wt[:, s], in0=row[:, 2 * r, :], scalar=k08[:, s, r, :],
                                             in1=row[:, 2 * r + 1, :], op0=ALU.add,
                                             op1=ALU.max).then_inc(s_lg, 1)

                def weights(r, s):
                    n = gr * U + r * NT + s
                    dve.wait_ge(s_exp, n + 1)
                    dve.scalar_tensor_tensor(out=wt[:, s], in0=wt[:, s], scalar=1.0,
                                             in1=ct[r][:, s, bass.ds(gr * W, W)], op0=ALU.min,
                                             op1=ALU.mult).then_inc(s_wt, 1)

                for r in range(R):
                    for s in range(NT + 2):
                        if s < NT:
                            logits(r, s)
                        if s >= 2:
                            weights(r, s - 2)

            def outputs(gr):
                for j in range(TG):
                    t = gr * TG + j
                    dve.wait_ge(s_o, t + 2)
                    dve.tensor_scalar(rz[:, 0:1], ps_o[:, 1, D // 2:D // 2 + 1], Z_EPS, None, ALU.add).then_inc(s_rz, 1)
                    dve.wait_ge(s_rz, 2 * t + 1)
                    dve.reciprocal(rz[:, 1:2], rz[:, 0:1]).then_inc(s_rz, 1)
                    dve.wait_ge(s_x[j], 16 * (gr + 1))
                    dve.tensor_tensor(xt[:, j, :], xt[:, j, :], bias[:], ALU.add).then_inc(s_o_out, 1)
                    dve.wait_ge(s_rz, 2 * t + 2)
                    dve.wait_ge(s_o_out, 3 * t + 1)
                    for half in range(2):
                        c = slice(half * D // 2, (half + 1) * D // 2)
                        dve.scalar_tensor_tensor(out=xt[:, j, c], in0=ps_o[:, half, 0:D // 2], scalar=rz[:, 1:2],
                                                 in1=xt[:, j, c], op0=ALU.mult, op1=ALU.add).then_inc(s_o_out, 1)

            steps(0)
            for gr in range(1, NG):
                steps_first = gr
                outputs(gr - 1)
                steps(steps_first)
            outputs(NG - 1)

        @block.scalar
        def _(act):
            act.wait_ge(s_k, 2)

            def evac(gr, r):
                act.wait_ge(s_pe, RING + gr * U + (r + 1) * NT)
                for b in range(3):
                    act.copy(gT[:, r, 2 * b:2 * b + 2, :],
                             ps_g[:, r % 2, b, 0:2 * W].rearrange("p (k n) -> p k n", k=2)).then_inc(s_g, 1)

            for gr in range(NG):
                for r in range(R):
                    for s in range(NT):
                        n = gr * U + r * NT + s
                        act.wait_ge(s_lg, n + 1 + U)
                        act.activation(wt[:, s], wt[:, s], ACT.Exp, bias=k02[:, s, r, :]).then_inc(s_exp, 1)
                        if s == 3 and r > 0:
                            evac(gr, r - 1)
                evac(gr, R - 1)

        @block.tensor
        def _(pe):
            pe.sem_inc(s_pe, RING)
            pe.sem_inc(s_o, 1)
            for gr in range(NG):
                for r in range(R):
                    u = gr * R + r
                    for s in range(NT):
                        pe.wait_ge(s_wt, gr * U + r * NT + s + 1)
                        if s == 0 and u >= 1:
                            pe.wait_ge(s_g, 3 * u if r == 0 else max(3 * (u - 1), 0) or 1) if (r == 0 or u >= 2) else None
                        for f in range(KD):
                            last = pe.matmul(ps_g[:, r % 2, f // 2, (f % 2) * W:(f % 2 + 1) * W],
                                             h2[:, s, f * P:(f + 1) * P], wt[:, s],
                                             start=(s == 0 and f % 2 == 0), stop=(s == NT - 1), skip_group_check=True)
                        last.then_inc(s_pe, 1)
                pe.wait_ge(s_g, 3 * R * (gr + 1))
                pe.wait_ge(s_z, RING + (gr + 1) * U)
                pe.wait_ge(s_w, 16 * R)
                pe.wait_ge(s_one, 3)
                for j in range(TG):
                    t = gr * TG + j
                    if t >= 1:
                        pe.wait_ge(s_o_out, 3 * t)
                    for half in range(2):
                        for i in range(R * KD):
                            r, kd = divmod(i, KD)
                            last = pe.matmul(ps_o[:, half, 0:D // 2], gT[:, r, kd, j * P:(j + 1) * P],
                                             w[:, r, kd, half * D // 2:(half + 1) * D // 2], start=(i == 0),
                                             stop=(i == R * KD - 1), skip_group_check=True)
                    pe.matmul(ps_o[:, 1, D // 2:D // 2 + 1], zsum[:, j * P:(j + 1) * P], ones[:], start=False,
                              stop=True, skip_group_check=True).then_inc(s_o, 1)


def sum_relations(nc, g, ct, total):
    with ExitStack() as ctx:
        s_sum = ctx.enter_context(nc.semaphore("sum_rel"))
        block = ctx.enter_context(nc.Block())

        @block.vector
        def _(dve):
            for t in range(g.NT):
                dve.tensor_tensor(total[:, t, :], ct[0][:, t, :], ct[1][:, t, :], ALU.add).then_inc(s_sum, 1)
            for t in range(g.NT):
                dve.wait_ge(s_sum, t + 1)
                dve.tensor_tensor(total[:, t, :], total[:, t, :], ct[2][:, t, :], ALU.add).then_inc(s_sum, 1)


def third_tables(nc, g, x1d, x1, res, kq3, feat3, Wg, al, ar, Wres, ident):
    NT, NP, KD, D = g.NT, g.NP, g.KD, g.D
    H, F = 12, D // 12
    with ExitStack() as ctx:
        sb = lambda n, s, d=F32: ctx.enter_context(nc.sbuf_tensor("t3" + n, s, d))
        sem = lambda n: ctx.enter_context(nc.semaphore("t3" + n))
        h = sb("h", [P, NT, D])
        hT = sb("hT", [P, KD, NP])
        stats = sb("stats", [P, NT, 2, 6])
        mv = sb("mv", [P, NT, 2])
        std = sb("std", [P, NT])
        rstd = sb("rstd", [P, NT])
        shift = sb("shift", [P, NT])
        eps = sb("eps", [P, 1])
        wd = sb("wd", [F, 2, 2, F])
        att = sb("att", [2 * H, F])
        attT = sb("attT", [F, 2 * H])
        wbd = sb("wbd", [P, 2, P])
        wa = sb("wa", [P, 2 * H])
        wabd = sb("wabd", [P, KD, 2 * H])
        stage = sb("stage", [P, 2, H, F + 1])
        ps_turn = ctx.enter_context(nc.psum_tensor("t3ps_turn", [P, 2, 512], F32))
        ps_f = ctx.enter_context(nc.psum_tensor("t3ps_f", [P, 2, 2, 512], F32))
        ps_s = ctx.enter_context(nc.psum_tensor("t3ps_s", [P, 512], F32))
        s_const = sem("const")
        s_x = sem("x")
        s_wd = sem("wd")
        s_stat = sem("stat")
        s_norm = sem("norm")
        s_h = sem("h_made")
        s_turn = sem("turn")
        s_turned = sem("turned")
        s_prep = sem("prep")
        s_prep_out = sem("prep_out")
        s_f = sem("f")
        s_f_out = sem("f_out")
        s_kq = sem("kq")
        s_spill = [sem("spill0"), sem("spill1")]
        block = ctx.enter_context(nc.Block())

        @block.sync
        def _(sp):
            sp.dma_start(x1[:], x1d).then_inc(s_x, 16)
            for i, m in enumerate((Wg, Wres)):
                for c in range(2):
                    sp.dma_start(wd[:, i, c, :], m).then_inc(s_wd, 16)
            for i, m in enumerate((al, ar)):
                sp.dma_start(att[i * H:(i + 1) * H, :], m.rearrange("o h f -> (o h) f")).then_inc(s_wd, 16)

        @block.gpsimd
        def _(pool):
            pool.memset(eps[:], LN_EPS).then_inc(s_const, 1)
            pool.memset(wbd[:], 0.0).then_inc(s_const, 1)
            pool.memset(wabd[:], 0.0).then_inc(s_const, 1)
            pool.memset(stage[:], 1.0).then_inc(s_const, 1)

        @block.tensor
        def _(pe):
            pe.wait_ge(s_wd, 96)
            for i in range(2):
                last = pe.transpose(ps_s[:, i * F:(i + 1) * F], wd[:, i].rearrange("o c d -> o (c d)"), ident[0:F, 0:F])
            last = pe.transpose(ps_s[0:F, P:P + 2 * H], att[:], ident[0:2 * H, 0:2 * H])
            last.then_inc(s_prep, 1)
            pe.wait_ge(s_prep_out, 5)
            pe.matmul(ps_s[:, 0:2 * H], wd[:, 0].rearrange("o c d -> o (c d)"), attT[:], start=True,
                      stop=True).then_inc(s_prep, 1)
            for n in range(2 * NT):
                t, half = divmod(n, 2)
                pe.wait_ge(s_h, t + 1)
                if n >= 2:
                    pe.wait_ge(s_turned, n - 1)
                for j in range(3):
                    kd = 3 * half + j
                    last = pe.transpose(ps_turn[:, n % 2, j * P:(j + 1) * P], h[:, t, kd * P:(kd + 1) * P], ident[:])
                last.then_inc(s_turn, 1)
            pe.wait_ge(s_turned, 2 * NT)
            pe.wait_ge(s_prep_out, 6 + 2 * KD)
            for t in range(NT):
                for kd in range(KD):
                    last = pe.matmul(ps_s[:, t * 2 * H:(t + 1) * 2 * H], hT[:, kd, t * P:(t + 1) * P], wabd[:, kd, :],
                                     start=(kd == 0), stop=(kd == KD - 1), skip_group_check=True)
            last.then_inc(s_kq, 1)
            for n in range(2 * NT):
                i, t = divmod(n, NT)
                if n >= 2:
                    pe.wait_ge(s_f_out, 2 * (n - 1))
                for kd in range(KD):
                    b, j = divmod(kd, 3)
                    last = pe.matmul(ps_f[:, n % 2, b, j * P:(j + 1) * P], hT[:, kd, t * P:(t + 1) * P], wbd[:, i, :],
                                     start=(j == 0), stop=True, skip_group_check=True)
                last.then_inc(s_f, 1)

        @block.vector
        def _(dve):
            dve.wait_ge(s_prep, 1)
            dve.wait_ge(s_const, 4)
            for i in range(2):
                for c in range(2):
                    dve.tensor_copy(wbd[c * F:(c + 1) * F, i, c * F:(c + 1) * F],
                                    ps_s[c * F:(c + 1) * F, i * F:(i + 1) * F]).then_inc(s_prep_out, 1)
            dve.tensor_copy(attT[:], ps_s[0:F, P:P + 2 * H]).then_inc(s_prep_out, 1)
            dve.wait_ge(s_prep, 2)
            dve.tensor_copy(wa[:], ps_s[:, 0:2 * H]).then_inc(s_prep_out, 1)
            dve.wait_ge(s_prep_out, 6)
            for kd in range(KD):
                for c in range(2):
                    hh = 2 * kd + c
                    p = slice(c * F, (c + 1) * F)
                    dve.tensor_copy(wabd[p, kd, hh:hh + H + 1:H], wa[p, hh:hh + H + 1:H]).then_inc(s_prep_out, 1)
            dve.wait_ge(s_x, 16)
            layernorm_stats(dve, g, x1, stats, mv, s_stat)
            dve.wait_ge(s_norm, 1)
            dve.reciprocal(rstd[:], std[:]).then_inc(s_norm, 1)
            dve.wait_ge(s_norm, 2)
            dve.scalar_tensor_tensor(out=shift[:], in0=mv[:, :, 0], scalar=-1.0, in1=rstd[:],
                                     op0=ALU.mult, op1=ALU.mult).then_inc(s_norm, 1)
            dve.wait_ge(s_kq, 1)
            v = ps_s[:, 0:NT * 2 * H].rearrange("p (t c) -> p t c", t=NT)
            dve.tensor_copy(kq3[:, :, 0, H:2 * H], v[:, :, 0:H])
            dve.tensor_copy(kq3[:, :, 0, 0:H], v[:, :, H:2 * H])

        @block.scalar
        def _(act):
            act.wait_ge(s_const, 4)
            act.wait_ge(s_stat, 3 * NT)
            act.activation(std[:], mv[:, :, 1], ACT.Sqrt, bias=eps[:]).then_inc(s_norm, 1)
            act.wait_ge(s_norm, 3)
            for t in range(NT):
                act.activation(h[:, t, :], x1[:, t, :], ACT.Relu, bias=shift[:, t:t + 1],
                               scale=rstd[:, t:t + 1]).then_inc(s_h, 1)
            for n in range(2 * NT):
                t, half = divmod(n, 2)
                act.wait_ge(s_turn, n + 1)
                act.copy(hT[:, 3 * half:3 * half + 3, t * P:(t + 1) * P],
                         ps_turn[:, n % 2, 0:3 * P].rearrange("p (k n) -> p k n", k=3)).then_inc(s_turned, 1)
            for n in range(2 * NT):
                i, t = divmod(n, NT)
                act.wait_ge(s_f, n + 1)
                if i == 0 and t >= 2:
                    act.wait_ge(s_spill[t % 2], 16 * (t // 2))
                for b in range(2):
                    v = ps_f[:, n % 2, b, 0:3 * P]
                    if i == 0:
                        act.copy(stage[:, t % 2, 6 * b:6 * b + 6, 0:F],
                                 v.rearrange("p (a f) -> p a f", f=F)).then_inc(s_f_out, 1)
                    else:
                        act.copy(res[:, t, b * 3 * P:(b + 1) * 3 * P], v).then_inc(s_f_out, 1)
                if i == 0:
                    act.wait_ge(s_f_out, 2 * (n + 1))
                    act.dma_start(feat3[:, t].rearrange("h p f -> p h f"), stage[:, t % 2]).then_inc(s_spill[t % 2], 16)
            for q in range(2):
                act.wait_ge(s_spill[q], 16 * NT // 2)


def gnn_kernel(nc, x, src, dst, etype, W1, q1, k1, b1, W2, q2, k2, b2, Wg, al, ar, Wres, out):
    g = Graph(x, src)
    NT, NP, R, D = g.NT, g.NP, g.R, g.D
    H1, F1, H3, F3 = 4, D // 4, 12, D // 12
    dram = lambda n, s, d=F32: nc.dram_tensor(n, s, d, kind="Internal").ap()
    counts = [dram(f"counts{i}", [R * NP * NP, 1]) for i in range(2)]
    feat1 = dram("feat1", [H1, R * NT, P, F1 + 1])
    feat3 = dram("feat3", [H3, NT, P, F3 + 1])
    rows1 = dram("rows1", [H1 * R, 2 * NP])
    rows2 = dram("rows2", [R, 2 * NP])
    rows3 = dram("rows3", [H3, 2 * NP])
    h2d = dram("h2d", [P, NT, D])
    x1d = dram("x1d", [P, NT, D])
    with ExitStack() as ctx:
        sb = lambda c, n, s, d=F32: c.enter_context(nc.sbuf_tensor(n, s, d))
        ident = sb(ctx, "ident", [P, P])
        ct_all = sb(ctx, "ct_all", [P, R * NT * NP], U16)
        ct = [ct_all[:, r * NT * NP:(r + 1) * NT * NP].rearrange("p (t n) -> p t n", t=NT) for r in range(R)]
        with ExitStack() as inner:
            wqk2 = sb(inner, "wqk2", [P, g.KD, R, 2])
            with ExitStack() as first:
                kq1 = sb(first, "kq1", [P, NT, R, 2 * H1])
                hd = Heads(nc, first, g, "h1", H1, R, ct, kq1, ident, rows1)
                tables_and_counts(nc, g, x, src, dst, etype, W1, q1, k1, W2, q2, k2, ident, hd, kq1, wqk2, feat1,
                                  counts, ct_all)
                multi_head(nc, g, "h1", hd, F1, feat1, relational_post(nc, g, b1, h2d))
            kq2 = sb(inner, "kq2", [P, NT, R, 2])
            h2 = sb(inner, "h2", [P, NT, D])
            second_logits(nc, g, ct, h2d, h2, kq2, wqk2, ident, rows2)
            second_layer(nc, g, ct, h2, kq2, rows2, W2, b2, x, x1d)
        total = sb(ctx, "total", [P, NT, NP])
        sum_relations(nc, g, ct, total)
        kq3 = sb(ctx, "kq3", [P, NT, 1, 2 * H3])
        spare = ct_all[:].bitcast(F32)
        x1 = spare[:, 0:NT * D].rearrange("p (t d) -> p t d", t=NT)
        res = spare[:, NT * D:2 * NT * D].rearrange("p (t d) -> p t d", t=NT)
        space = spare[:, 2 * NT * D:2 * NT * D + 3 * NP].rearrange("p (a n) -> p a n", a=3)
        third_tables(nc, g, x1d, x1, res, kq3, feat3, Wg, al, ar, Wres, ident)
        hd = Heads(nc, ctx, g, "h3", H3, 1, [total], kq3, ident, rows3, space)
        multi_head(nc, g, "h3", hd, F3, feat3, final_post(nc, g, x1, res, out))


_INS = ['x', 'src', 'dst', 'edge_type_3', 'L0_gnn_W1', 'L0_gnn_q1', 'L0_gnn_k1', 'L0_gnn_b1', 'L0_gnn_W2', 'L0_gnn_q2',
        'L0_gnn_k2', 'L0_gnn_b2', 'L1_gnn_W', 'L1_gnn_attn_l', 'L1_gnn_attn_r', 'L1_gnn_W_res']


def kernel(**inputs):
    import numpy as _np
    import concourse.bacc as _bacc
    from concourse import mybir as _mybir
    from concourse.bass_utils import run_bass_kernel_spmd as _run

    nc = _bacc.Bacc("TRN2", target_bir_lowering=False, num_devices=1)
    arrays, args = {}, []
    for name in _INS:
        a = _np.ascontiguousarray(inputs[name])
        arrays[f"in_{name}_dram"] = a
        args.append(nc.dram_tensor(f"in_{name}_dram", a.shape, _mybir.dt.from_np(a.dtype), kind="ExternalInput").ap())
    out = nc.dram_tensor("out_0_dram", tuple(inputs['x'].shape), _mybir.dt.float32, kind="ExternalOutput").ap()
    gnn_kernel(nc, *args, out)
    r = _run(nc, [arrays], core_ids=[0])
    return r.results[0]["out_0_dram"]
```

```python
from contextlib import ExitStack

import numpy as np
import concourse.bass as bass
from concourse import mybir

ALU = mybir.AluOpType
ACT = mybir.ActivationFunctionType
F32 = mybir.dt.float32
I32 = mybir.dt.int32
U16 = mybir.dt.uint16
BF16 = mybir.dt.bfloat16
F16 = mybir.dt.float16
AX = mybir.AxisListType.X

P = 128
BIG = 1.0e30
SLOPE = 0.2
Z_EPS = 1.0e-16
LN_EPS = 1.0e-5
TURN_STEP = 7
TABLES = 3
SLOTS = 5
GROUPS = [(0, 4), (4, 4), (8, 2)]


class Graph:

    def __init__(self, x, src):
        self.N, self.D = x.shape
        self.E = src.shape[0]
        self.NT = -(-self.N // P)
        self.NP = self.NT * P
        self.LAST = self.N - (self.NT - 1) * P
        self.KD = self.D // P
        self.R = 3
        assert self.NT == sum(w for _, w in GROUPS)


def load_nodes(eng, g, sbuf, dram, sem):
    full = (g.NT - 1) * P
    eng.dma_start(sbuf[:, 0:g.NT - 1, :], dram[0:full, :].rearrange("(t p) d -> p t d", p=P)).then_inc(sem, 16)
    eng.dma_start(sbuf[0:g.LAST, g.NT - 1, :], dram[full:g.N, :]).then_inc(sem, 16)


def layernorm_stats(dve, g, x, stats, mv, sem):
    half = g.D // 2
    for t in range(g.NT):
        for i in range(2):
            dve.bn_stats(stats[:, t, i, :], x[:, t, i * half:(i + 1) * half]).then_inc(sem, 1)
    for t in range(g.NT):
        dve.wait_ge(sem, 2 * (t + 1))
        dve.bn_aggr(mv[:, t, :], stats[:, t]).then_inc(sem, 1)


class Heads:

    def __init__(self, nc, ctx, g, tag, H, R, ct, kq, ident, rows, space=None):
        self.g, self.H, self.R, self.ct, self.kq, self.ident = g, H, R, ct, kq, ident
        NT, NP = g.NT, g.NP
        sb = lambda n, s, d=F32: ctx.enter_context(nc.sbuf_tensor(tag + n, s, d))
        sem = lambda n: ctx.enter_context(nc.semaphore(tag + n))
        self.rows = rows
        self.all_miss = R == 1
        self.miss = sb("miss", [P, NT if self.all_miss else 2, NP], BF16)
        if space is None:
            space = sb("space", [P, 3, NP])
        self.acc = [space[:, 0], space[:, 2]]
        self.km = sb("km", [P, 2, NT, R])
        self.lg = sb("lg", [P, NT, R])
        self.m0 = sb("m0", [P, NT])
        self.m = sb("m", [P, NT])
        self.none = sb("none", [P, NT])
        self.ab = sb("ab", [P, NT, R, 2])
        self.rows_sb = space[0:2 * R, 1]
        self.s_miss = sem("miss_made")
        self.s_first = [sem("first0"), sem("first1")]
        self.s_later = sem("later")
        self.s_turn = sem("acc_turned")
        self.s_km = sem("km_made")
        self.s_ab = sem("ab_made")
        self.s_abT = sem("ab_turned")
        self.s_rows = sem("rows_copied")
        self.s_rows_out = sem("rows_out")

    def later_unit(self, h, r):
        return (h - 2) * self.R + r

    def unit(self, h, r):
        return 2 * r + h if isinstance(h, int) and h < 2 and self.H > 1 else h * self.R + r

    def first_acc(self, h, r):
        return self.acc[h if self.H > 1 else r % 2]

    def start_vector(self, dve):
        dve.sem_inc(self.s_km, 3)

    def mask(self, dve, r, s):
        dve.tensor_scalar(self.miss[:, s if self.all_miss else s % 2], self.ct[r][:, s, :], 0.0, -BIG, ALU.is_equal,
                          ALU.mult).then_inc(self.s_miss, 1)

    def first_step(self, dve, h, r, s):
        n = r * self.g.NT + s
        mask = self.miss[:, s if self.all_miss else s % 2]
        k = self.kq[:, s, r, self.H + h:self.H + h + 1]
        acc, sem = self.first_acc(h, r), self.s_first[h]
        if s == 0:
            dve.tensor_scalar(acc, mask, k, None, ALU.add).then_inc(sem, 1)
        else:
            dve.wait_ge(sem, n)
            dve.scalar_tensor_tensor(out=acc, in0=mask, scalar=k, in1=acc, op0=ALU.add,
                                     op1=ALU.max).then_inc(sem, 1)

    def later_step(self, dve, h, r, s):
        n = self.later_unit(h, r) * self.g.NT + s
        mask = self.miss[:, s if self.all_miss else s % 2]
        k = self.kq[:, s, r, bass.ds(self.H + h, 1)]
        if s == 0:
            dve.tensor_scalar(self.acc[0], mask, k, None, ALU.add).then_inc(self.s_later, 1)
        else:
            dve.wait_ge(self.s_later, n)
            dve.scalar_tensor_tensor(out=self.acc[0], in0=mask, scalar=k, in1=self.acc[0], op0=ALU.add,
                                     op1=ALU.max).then_inc(self.s_later, 1)

    def reduce_unit(self, dve, h, r):
        for i, (t0, nt) in enumerate(GROUPS):
            dve.wait_ge(self.s_turn, self.unit(h, r) * 3 + i + 1)
            dve.tensor_reduce(self.km[:, bass.ds(h % 2, 1), t0:t0 + nt, r].rearrange("p o t -> p (o t)"),
                              self.ps_turn[:, i, 0:nt * P].rearrange("p (t s) -> p t s", s=P),
                              AX, ALU.max).then_inc(self.s_km, 1)

    ROW_PARTS = 5

    def rows_of_head(self, dve, h, parts=range(ROW_PARTS)):
        R, NT = self.R, self.g.NT
        q = self.kq[:, :, :, bass.ds(h, 1)].rearrange("p t r o -> p t (r o)")
        if 0 in parts:
            dve.wait_ge(self.s_km, self.unit(h, R - 1) * 3 + 6)
            dve.tensor_tensor(self.lg[:], self.km[:, bass.ds(h % 2, 1)].rearrange("p o t r -> p (o t) r"), q,
                              ALU.add).then_inc(self.s_ab, 1)
        if 1 in parts:
            dve.wait_ge(self.s_ab, h * 7 + 1)
            dve.tensor_reduce(self.m0[:], self.lg[:], AX, ALU.max).then_inc(self.s_ab, 1)
        if 2 in parts:
            dve.wait_ge(self.s_ab, h * 7 + 2)
            dve.scalar_tensor_tensor(out=self.m[:], in0=self.m0[:], scalar=SLOPE, in1=self.m0[:], op0=ALU.mult,
                                     op1=ALU.max).then_inc(self.s_ab, 1)
            dve.tensor_scalar(self.none[:], self.m0[:], -0.5 * BIG, BIG, ALU.is_lt, ALU.mult).then_inc(self.s_ab, 1)
        if 3 in parts:
            dve.wait_ge(self.s_ab, h * 7 + 4)
            dve.tensor_tensor(self.m[:], self.m[:], self.none[:], ALU.add).then_inc(self.s_ab, 1)
        if 4 in parts:
            dve.wait_ge(self.s_ab, h * 7 + 5)
            dve.wait_ge(self.s_abT, h * 3 + 3)
            m = self.m[:].rearrange("p (t o) -> p t o", o=1).broadcast_to([P, NT, R])
            dve.tensor_tensor(self.ab[:, :, :, 0], q, m, ALU.subtract).then_inc(self.s_ab, 1)
            dve.scalar_tensor_tensor(out=self.ab[:, :, :, 1], in0=q, scalar=SLOPE, in1=m, op0=ALU.mult,
                                     op1=ALU.subtract).then_inc(self.s_ab, 1)

    def start_tensor(self, pe):
        pe.sem_inc(self.s_abT, 3)

    def turn_unit(self, pe, h, r):
        first = isinstance(h, int) and h < 2
        if first:
            pe.wait_ge(self.s_first[h], (r + 1) * self.g.NT)
        else:
            pe.wait_ge(self.s_later, (self.later_unit(h, r) + 1) * self.g.NT)
            pe.wait_ge(self.s_rows, h * 3 + 3)
        acc = self.first_acc(h, r) if first else self.acc[0]
        for i, (t0, nt) in enumerate(GROUPS):
            pe.wait_ge(self.s_km, self.unit(h, r) * 3 + i + 1)
            for j in range(nt):
                last = pe.transpose(self.ps_turn[:, i, j * P:(j + 1) * P],
                                    acc[:, (t0 + j) * P:(t0 + j + 1) * P], self.ident[:])
            last.then_inc(self.s_turn, 1)

    def turn_rows(self, pe, h):
        pe.wait_ge(self.s_ab, h * 7 + 7)
        pe.wait_ge(self.s_rows, h * 3 + 3)
        for i, (t0, nt) in enumerate(GROUPS):
            for j in range(nt):
                last = pe.transpose(self.ps_turn[0:2 * self.R, i, j * P:(j + 1) * P],
                                    self.ab[:, t0 + j].rearrange("p r c -> p (r c)"), self.ident[:])
            last.then_inc(self.s_abT, 1)

    def start_scalar(self, act):
        act.sem_inc(self.s_rows, 3)
        act.sem_inc(self.s_rows_out, 16)

    def rows_to_dram(self, act, h):
        act.wait_ge(self.s_rows_out, h * 16 + 16)
        for i, (t0, nt) in enumerate(GROUPS):
            act.wait_ge(self.s_abT, h * 3 + i + 4)
            act.copy(self.rows_sb[:, t0 * P:(t0 + nt) * P], self.ps_turn[0:2 * self.R, i, 0:nt * P]
                     ).then_inc(self.s_rows, 1)
        act.wait_ge(self.s_rows, h * 3 + 6)
        R = self.R
        act.dma_start(self.rows[bass.ds(h * R, R)].rearrange("r (c n) -> (r c) n", c=2),
                      self.rows_sb).then_inc(self.s_rows_out, 16)


def logits_by_chunk(pe, wa, hT, banks, i, C, sem):
    t0, nt = GROUPS[i]
    KD = hT.shape[1]
    for kd in range(KD):
        last = pe.matmul(banks[i][0:C, 0:nt * P], wa(kd), hT[:, kd, t0 * P:(t0 + nt) * P],
                         start=(kd == 0), stop=(kd == KD - 1))
    last.then_inc(sem, 1)


def logits_back(pe, hd, kT, out, C, done, sem):
    for i, (t0, nt) in enumerate(GROUPS):
        pe.wait_ge(done, i + 1)
        for t in range(t0, t0 + nt):
            last = pe.transpose(out[:, t * C:(t + 1) * C], kT[0:C, t * P:(t + 1) * P], hd.ident[0:C, 0:C])
        last.then_inc(sem, 1)


def scaled_k(dve, kq, H, k08, k02, sem, slope=SLOPE):
    dve.tensor_scalar(k08[:], kq[:, :, :, H:2 * H], 1.0 - SLOPE, None, ALU.mult).then_inc(sem, 1)
    dve.tensor_scalar(k02[:], kq[:, :, :, H:2 * H], slope, None, ALU.mult).then_inc(sem, 1)


def tables_and_counts(nc, g, x, src, dst, etype, W1, q1, k1, W2, q2, k2, ident, hd, kq1, wqk2, feat1, counts, ct_all):
    N, D, NT, NP, KD, R = g.N, g.D, g.NT, g.NP, g.KD, g.R
    H, F = 4, D // 4
    CELLS = R * NP * NP
    EC_FULL = g.E // P
    EC_USED = -(-g.E // P)
    EC = -(-EC_USED // 8) * 8
    TAIL = g.E - EC_FULL * P
    PIECES = 10
    ZC = CELLS // P // PIECES
    NW = 2 * R
    tables = [c % TABLES for c in range(EC_USED)]
    TURNS_W = 2 * KD
    with ExitStack() as ctx:
        sb = lambda n, s, d=F32: ctx.enter_context(nc.sbuf_tensor(n, s, d))
        sem = lambda n: ctx.enter_context(nc.semaphore(n))
        edges_i = sb("edges_i", [P, 3, EC], I32)
        edges_f = sb("edges_f", [P, 3, EC])
        key = sb("key", [P, EC])
        key_i = sb("key_i", [P, EC], I32)
        packed = sb("packed", [P, EC])
        ones = sb("ones", [P, P])
        earlier = sb("earlier", [P, P])
        diag = sb("diag", [P, 2, 4, P])
        same = sb("same", [P, 8, P])
        part = sb("part", [P, 2, TABLES, NP], U16)
        zero = part[:].rearrange("p a b n -> p (a b n)")[:, 0:ZC]
        packed_i = sb("packed_i", [P, EC], U16)
        spare = ct_all[:].bitcast(F32)
        h = spare[:, 0:NT * D].rearrange("p (t d) -> p t d", t=NT)
        wT = spare[:, NT * D:NT * D + KD * D].rearrange("p (k d) -> p k d", k=KD)
        hT = sb("hT", [P, KD, NP])
        wT2 = hT[:].rearrange("p k n -> p (k n)")[:, 0:KD * D].rearrange("p (k d) -> p k d", k=KD)
        stats = sb("stats", [P, NT, 2, 6])
        mv = sb("mv", [P, NT, 2])
        std = sb("std", [P, NT])
        rstd = sb("rstd", [P, NT])
        shift = sb("shift", [P, NT])
        eps = sb("eps", [P, 1])
        w = sb("w", [P, 2, KD, D])
        qk1 = sb("qk1", [P, KD, 2 * H])
        qk2 = sb("qk2", [P, 2, KD])
        wqk1 = sb("wqk1", [P, KD, R, 2 * H])
        stage = sb("stage", [P, 2, H, F + 1])
        ps_turn = ctx.enter_context(nc.psum_tensor("ps_turn", [P, 3, 512], F32))
        ps_feat = ctx.enter_context(nc.psum_tensor("ps_feat", [P, 2, 2, 512], F32))
        ps_small = ctx.enter_context(nc.psum_tensor("ps_small", [P, 512], F32))
        ps_key = ps_feat[:, 0]
        hd.ps_turn = ps_turn
        wq_banks = [ps_turn[:, 2], ps_small]
        wqT = sb("wqT", [2 * H, D])

        s_clean = sem("a_clean")
        s_const = sem("a_const")
        s_zero = sem("a_zero")
        s_edges = sem("a_edges")
        s_x = sem("a_x")
        s_qk = sem("a_qk")
        s_cleared = [sem(f"a_cleared{i}") for i in range(TABLES)]
        s_w = [sem("a_w0"), sem("a_w1")]
        s_wused = sem("a_wused")
        s_stat = sem("a_stat")
        s_norm = sem("a_norm")
        s_h = sem("a_h")
        s_turn = sem("a_turn")
        s_turned = sem("a_turned")
        s_wqT = sem("a_wqT")
        s_wqT_out = sem("a_wqT_out")
        s_wqk = sem("a_wqk")
        s_wqk_out = sem("a_wqk_out")
        s_feat = sem("a_feat")
        s_feat_out = sem("a_feat_out")
        s_spill = [sem("a_spill0"), sem("a_spill1")]
        s_key = sem("a_keys")
        s_diag = sem("a_diag")
        s_bcast = sem("a_bcast")
        s_same = sem("a_same")
        s_index = sem("a_index")
        s_scat = [sem(f"a_scat{i}") for i in range(TABLES)]
        s_part = [sem("a_part0"), sem("a_part1")]
        s_ct = sem("a_ct")
        block = ctx.enter_context(nc.Block())

        @block.sync
        def _(sp):
            sp.wait_ge(s_clean, 2)
            for i, a in enumerate((src, dst, etype)):
                sp.dma_start(edges_i[:, i, 0:EC_FULL],
                             a[0:EC_FULL * P].rearrange("(p c) -> p c", p=P)).then_inc(s_edges, 16)
                sp.dma_start(edges_i[0:TAIL, i, EC_FULL:EC_FULL + 1],
                             a[EC_FULL * P:g.E].rearrange("(p c) -> p c", c=1)).then_inc(s_edges, 16)
            for vec, sl in ((q1, qk1[:, :, 0:H]), (k1, qk1[:, :, H:2 * H])):
                sp.dma_start(sl, vec.rearrange("(k p) h -> p k h", p=P)).then_inc(s_qk, 16)
            for c, vec in enumerate((q2, k2)):
                sp.dma_start(qk2[:, c, :], vec.rearrange("(k p) h -> p (k h)", p=P),
                             allow_slow_non_contiguous=True).then_inc(s_qk, 16)

            def load_w(i):
                big = (W1, W2)[i // R][i % R]
                sp.dma_start(w[:, i % 2], big.rearrange("(k p) f -> p k f", p=P)).then_inc(s_w[i % 2], 16)

            load_w(0)
            load_nodes(sp, g, h, x, s_x)
            load_w(1)
            sp.wait_ge(s_zero, 1)
            for i, table in enumerate(counts):
                flat = table.rearrange("(k p c) o -> k p (c o)", p=P, k=PIECES)
                for k in range(PIECES):
                    sp.dma_start(flat[k], zero).then_inc(s_cleared[i], 16)

            def next_w(i):
                sp.wait_ge(s_wused, i - 1)
                load_w(i)

            next_w(2)
            next_w(3)
            for q in range(TABLES):
                sp.wait_ge(s_scat[q], 16 * tables.count(q))
            tiles = [c.rearrange("(r s p n) o -> (r s) p (n o)", r=R, s=NT, p=P) for c in counts]
            for n in range(R * NT):
                if n >= 2:
                    sp.wait_ge(s_ct, (TABLES - 1) * (n - 1))
                for k in range(TABLES):
                    sp.dma_start(part[:, n % 2, k, :], tiles[k][n]).then_inc(s_part[n % 2], 16)
                if n in (16, 21):
                    next_w(4 + n // 21)

        @block.gpsimd
        def _(pool):
            pool.memset(edges_i[:], R).then_inc(s_clean, 1)
            pool.memset(h[:, NT - 1, :], 0.0).then_inc(s_clean, 1)
            pool.memset(ident[:], 0.0).then_inc(s_const, 1)
            pool.memset(earlier[:], float(2 * P + 1)).then_inc(s_const, 1)
            pool.memset(ones[:], 1.0).then_inc(s_const, 1)
            pool.memset(eps[:], LN_EPS).then_inc(s_const, 1)
            pool.memset(stage[:], 1.0).then_inc(s_const, 1)
            pool.wait_ge(s_const, 2)
            pool.affine_select(out=ident[:], in_=ident[:], compare_op=ALU.not_equal, fill=1.0, base=0,
                               pattern=[[-1, P]], channel_multiplier=1).then_inc(s_const, 1)
            pool.affine_select(out=earlier[:], in_=earlier[:], compare_op=ALU.is_gt, fill=1.0, base=0,
                               pattern=[[-1, P]], channel_multiplier=1).then_inc(s_const, 1)
            pool.wait_ge(s_const, 7)
            pool.wait_ge(s_key, 3)
            pool.sem_inc(s_bcast, 2)
            with pool.Fori(0, EC // 8) as i:
                for b in range(2):
                    pool.wait_ge(s_bcast, i * 2 + b + 1)
                    pool.tensor_tensor(diag[:, b], ident[:].rearrange("p (a e) -> p a e", a=1).broadcast_to([P, 4, P]),
                                       key[:, bass.ds(i * 8 + b * 4, 4)].rearrange("p (a e) -> p a e", e=1)
                                       .broadcast_to([P, 4, P]), ALU.mult).then_inc(s_diag, 1)
            pool.wait_ge(s_index, 2)
            done = [0] * TABLES
            for c, table in enumerate(tables):
                if done[table] == 0:
                    pool.wait_ge(s_cleared[table], 16 * PIECES)
                else:
                    pool.wait_ge(s_scat[table], 16 * done[table])
                done[table] += 1
                pool.indirect_dma_start(out=counts[table],
                                        out_offset=bass.IndirectOffsetOnAxis(ap=key_i[:, c:c + 1], axis=0),
                                        in_=packed_i[:, c:c + 1], in_offset=None, bounds_check=CELLS - 1,
                                        oob_is_err=False, compute_op=ALU.add).then_inc(s_scat[table], 16)

        @block.tensor
        def _(pe):
            hd.start_tensor(pe)
            turns = [0]

            def turn(blocks):
                n = turns[0]
                turns[0] += 1
                if n >= 2:
                    pe.wait_ge(s_turned, n - 1)
                for j, blk in enumerate(blocks):
                    last = pe.transpose(ps_turn[:, n % 2, j * P:(j + 1) * P], blk, ident[:])
                last.then_inc(s_turn, 1)

            def turn_weights(i, group):
                f, half = divmod(group, 2)
                turn([w[:, i % 2, 3 * half + j, f * P:(f + 1) * P] for j in range(3)])

            def logit_weights(i):
                c = 2 * H if i < R else 2
                pe.wait_ge(s_turned, turns[0])
                if i >= 1:
                    pe.wait_ge(s_wqk_out, i + i // R)
                wt = wT if i < R else wT2
                for half in range(2):
                    for f in range(KD):
                        last = pe.matmul(wq_banks[half][0:c, 0:D // 2], qk1[:, f, :] if i < R else qk2[:, :, f],
                                         wt[:, f, half * D // 2:(half + 1) * D // 2], start=(f == 0),
                                         stop=(f == KD - 1))
                    last.then_inc(s_wqT, 1)
                pe.wait_ge(s_wqT_out, 2 * i + 2)
                for kd in range(KD):
                    last = pe.transpose(ps_small[:, kd * c:(kd + 1) * c], wqT[0:c, kd * P:(kd + 1) * P],
                                        ident[0:c, 0:c])
                last.then_inc(s_wqk, 1)

            def compare(m):
                pe.wait_ge(s_diag, m + 1)
                pe.wait_ge(s_same, 4 * m + 4)
                pe.matmul(ps_key[:, m % 2], ones[:], diag[:, m % 2].rearrange("p a e -> p (a e)"),
                          start=True, stop=True).then_inc(s_bcast, 1)

            pe.wait_ge(s_const, 7)
            pe.wait_ge(s_qk, 64)
            def maxima_turned(r):
                pe.wait_ge(s_turned, turns[0])
                for j in range(2):
                    hd.turn_unit(pe, j, r)
                pe.wait_ge(hd.s_km, 6 * (r + 1) + 3)

            def features(r):
                for t in range(NT):
                    n = r * NT + t
                    if n >= 2:
                        pe.wait_ge(s_feat_out, 2 * (n - 1))
                    for half in range(2):
                        for kd in range(KD):
                            last = pe.matmul(ps_feat[:, n % 2, half, 0:D // 2], hT[:, kd, t * P:(t + 1) * P],
                                             w[:, r % 2, kd, half * D // 2:(half + 1) * D // 2],
                                             start=(kd == 0), stop=(kd == KD - 1))
                    last.then_inc(s_feat, 1)
                    if n == R * NT - 4:
                        maxima_turned(0)
                pe.wait_ge(s_feat, (r + 1) * NT)
                pe.sem_inc(s_wused, 1)

            pe.wait_ge(s_w[0], 16)
            for group in range(TURNS_W):
                turn_weights(0, group)
            logit_weights(0)
            for m in range(EC // 4):
                compare(m)
                if m < 2 * NT:
                    t, half = divmod(m, 2)
                    pe.wait_ge(s_h, t + 1)
                    turn([h[:, t, (3 * half + j) * P:(3 * half + j + 1) * P] for j in range(3)])
                elif m < 2 * NT + TURNS_W:
                    pe.wait_ge(s_w[1], 16)
                    turn_weights(1, m - 2 * NT)
            logit_weights(1)
            pe.wait_ge(s_same, EC + 8)
            features(0)
            features(1)
            pe.wait_ge(s_w[0], 32)
            for group in range(TURNS_W):
                turn_weights(2, group)
            logit_weights(2)
            pe.wait_ge(s_wqk_out, R)
            for t in range(NT):
                for kd in range(KD):
                    last = pe.matmul(ps_small[:, t * 2 * H * R:(t + 1) * 2 * H * R], hT[:, kd, t * P:(t + 1) * P],
                                     wqk1[:, kd].rearrange("p r c -> p (r c)"), start=(kd == 0), stop=(kd == KD - 1),
                                     skip_group_check=True)
            last.then_inc(s_wqk, 1)
            features(2)
            for i in range(R, 2 * R):
                pe.wait_ge(s_w[i % 2], 16 * (i // 2 + 1))
                for group in range(TURNS_W):
                    turn_weights(i, group)
                logit_weights(i)
                pe.wait_ge(s_wqk, i + 2)
                pe.sem_inc(s_wused, 1)
                if i != R + 1:
                    maxima_turned(1 + (i - R) // 2)
            for j in range(2):
                hd.turn_rows(pe, j)

        @block.scalar
        def _(act):
            hd.start_scalar(act)
            act.wait_ge(s_const, 7)

            def turned(n, out):
                act.wait_ge(s_turn, n + 1)
                act.copy(out, ps_turn[:, n % 2, 0:3 * P].rearrange("p (k n) -> p k n", k=3)).then_inc(s_turned, 1)

            def weights_turned(i, first):
                if i >= 1:
                    act.wait_ge(s_wqk, i + i // R)
                for group in range(TURNS_W):
                    f, half = divmod(group, 2)
                    turned(first + group, (wT if i < R else wT2)[:, f, half * 3 * P:(half + 1) * 3 * P].rearrange(
                        "p (k n) -> p k n", k=3))
                c = 2 * H if i < R else 2
                for half in range(2):
                    act.wait_ge(s_wqT, 2 * i + half + 1)
                    act.copy(wqT[0:c, half * D // 2:(half + 1) * D // 2], wq_banks[half][0:c, 0:D // 2]
                             ).then_inc(s_wqT_out, 1)

            def features_out(first, last):
                with act.Fori(first, last) as i:
                    for q in range(2):
                        act.wait_ge(s_feat, i * 2 + q + 1)
                        act.wait_ge(s_spill[q], i * 16 + 16)
                        for half in range(2):
                            act.copy(stage[:, q, 2 * half:2 * half + 2, 0:F],
                                     ps_feat[:, q, half, 0:2 * F].rearrange("p (a f) -> p a f", a=2)
                                     ).then_inc(s_feat_out, 1)
                        act.wait_ge(s_feat_out, i * 4 + 2 * q + 2)
                        act.dma_start(feat1[:, bass.ds(i * 2 + q, 1)].rearrange("h n p f -> p (n h) f"),
                                      stage[:, q]).then_inc(s_spill[q], 16)

            weights_turned(0, 0)
            act.wait_ge(s_stat, 3 * NT)
            act.activation(std[:], mv[:, :, 1], ACT.Sqrt, bias=eps[:]).then_inc(s_norm, 1)
            act.wait_ge(s_norm, 3)
            for t in range(NT):
                act.activation(h[:, t, :], h[:, t, :], ACT.Relu, bias=shift[:, t:t + 1],
                               scale=rstd[:, t:t + 1]).then_inc(s_h, 1)
            for t in range(NT):
                for half in range(2):
                    turned(TURNS_W + 2 * t + half, hT[:, 3 * half:3 * half + 3, t * P:(t + 1) * P])
            weights_turned(1, TURNS_W + 2 * NT)
            for q in range(2):
                act.sem_inc(s_spill[q], 16)
            features_out(0, NT)
            weights_turned(2, 2 * TURNS_W + 2 * NT)
            features_out(NT, R * NT // 2)
            for i in range(R, 2 * R):
                weights_turned(i, i * TURNS_W + 2 * NT)
            for j in range(2):
                hd.rows_to_dram(act, j)
            for q in range(2):
                act.wait_ge(s_spill[q], 16 * (R * NT // 2) + 16)

        @block.vector
        def _(dve):
            hd.start_vector(dve)
            dve.memset(zero, 0.0).then_inc(s_zero, 1)
            dve.wait_ge(s_edges, 96)
            dve.tensor_copy(edges_f[:], edges_i[:]).then_inc(s_key, 1)
            dve.wait_ge(s_key, 1)
            dve.scalar_tensor_tensor(out=packed[:], in0=edges_f[:, 2, :], scalar=float(NP), in1=edges_f[:, 0, :],
                                     op0=ALU.mult, op1=ALU.add).then_inc(s_key, 1)
            dve.wait_ge(s_key, 2)
            dve.scalar_tensor_tensor(out=key[:], in0=packed[:], scalar=float(NP), in1=edges_f[:, 1, :],
                                     op0=ALU.mult, op1=ALU.add).then_inc(s_key, 1)
            dve.wait_ge(s_key, 3)
            dve.sem_inc(s_same, 8)

            def small_out(i):
                dve.wait_ge(s_wqk, i + 1 + i // R)
                c, out = (2 * H, wqk1[:, :, i, :]) if i < R else (2, wqk2[:, :, i - R, :])
                dve.tensor_copy(out, ps_small[:, 0:KD * c].rearrange("p (k c) -> p k c", c=c)).then_inc(s_wqk_out, 1)

            dve.wait_ge(s_x, 32)
            layernorm_stats(dve, g, h, stats, mv, s_stat)
            dve.wait_ge(s_norm, 1)
            dve.reciprocal(rstd[:], std[:]).then_inc(s_norm, 1)
            dve.wait_ge(s_norm, 2)
            dve.scalar_tensor_tensor(out=shift[:], in0=mv[:, :, 0], scalar=-1.0, in1=rstd[:],
                                     op0=ALU.mult, op1=ALU.mult).then_inc(s_norm, 1)
            small_out(0)
            for m in range(EC // 4):
                dve.wait_ge(s_bcast, m + 3)
                for a in range(4):
                    c = 4 * m + a
                    dve.wait_ge(s_same, c + 1)
                    dve.scalar_tensor_tensor(out=same[:, c % 8], in0=ps_key[:, m % 2, a * P:(a + 1) * P],
                                             scalar=key[:, c:c + 1], in1=earlier[:],
                                             op0=ALU.is_equal, op1=ALU.mult,
                                             accum_out=packed[:, c:c + 1]).then_inc(s_same, 1)
            dve.wait_ge(s_same, EC + 8)
            dve.tensor_scalar(edges_f[:, 0, :], packed[:], float(2 * P), float(2 ** 23), ALU.is_ge,
                              ALU.mult).then_inc(s_key, 1)
            dve.wait_ge(s_key, 4)
            dve.tensor_tensor(edges_f[:, 1, :], key[:], edges_f[:, 0, :], ALU.add).then_inc(s_key, 1)
            dve.wait_ge(s_key, 5)
            dve.tensor_copy(key_i[:], edges_f[:, 1, :]).then_inc(s_index, 1)
            dve.tensor_copy(packed_i[:], packed[:]).then_inc(s_index, 1)
            small_out(1)
            small_out(2)
            dve.wait_ge(s_wqk, R + 1)
            dve.tensor_copy(kq1[:], ps_small[:, 0:NT * R * 2 * H].rearrange("p (t r c) -> p t r c", t=NT, r=R)
                            ).then_inc(s_wqk_out, 1)
            dve.wait_ge(s_wqk_out, R + 1)
            for r in range(R):
                for s in range(NT):
                    n = r * NT + s
                    dve.wait_ge(s_part[n % 2], 16 * TABLES * (n // 2 + 1))
                    for k in range(1, TABLES):
                        if k > 1:
                            dve.wait_ge(s_ct, (TABLES - 1) * n + k - 1)
                        dve.tensor_tensor(hd.ct[r][:, s, :], part[:, n % 2, 0, :] if k == 1 else hd.ct[r][:, s, :],
                                          part[:, n % 2, k, :], ALU.add).then_inc(s_ct, 1)
                    dve.wait_ge(s_ct, (TABLES - 1) * (n + 1))
                    if n >= 2:
                        dve.wait_ge(hd.s_first[1], n - 1)
                    hd.mask(dve, r, s)
                    dve.wait_ge(hd.s_miss, n + 1)
                    for j in range(2):
                        hd.first_step(dve, j, r, s)
                    if n in (19, 25, 29):
                        small_out(R + (19, 25, 29).index(n))
                for j in range(2):
                    hd.reduce_unit(dve, j, r)
            for j in range(2):
                hd.rows_of_head(dve, j)


def multi_head(nc, g, tag, hd, F, feat, post_setup):
    NT, NP, H, R, ct, kq = g.NT, g.NP, hd.H, hd.R, hd.ct, hd.kq
    rows = hd.rows
    banks = -(-NT // (512 // (F + 1)))
    per_bank = NT // banks
    assert banks * per_bank == NT
    UNIT = NT
    PE0 = 2 * UNIT
    T0 = 2 * UNIT
    turned = R == 1
    direct = [s for s in range(NT) if R > 1 and s % SLOTS == SLOTS - 1]
    ON_POOL = NT - len(direct)
    exps_before = [sum(1 if t in direct else 2 for t in range(s)) for s in range(NT + 1)]
    pool_before = [sum(t not in direct for t in range(s)) for s in range(NT)]
    with ExitStack() as ctx:
        sb = lambda n, s, d=F32: ctx.enter_context(nc.sbuf_tensor(tag + n, s, d))
        sem = lambda n: ctx.enter_context(nc.semaphore(tag + n))
        cf = sb("cf", [P, 2, NP]) if direct else None
        hd.ps_turn = ctx.enter_context(nc.psum_tensor(tag + "ps_turn", [P, 3, 512], F32))
        wt = sb("wt", [P, SLOTS, NP])
        row = sb("row", [P, 2, 2, NP])
        ft = sb("ft", [P, 2, NT, F + 1])
        k08 = sb("k08", [P, NT, R, H])
        k02 = sb("k02", [P, NT, R, H])
        k02n = sb("k02n", [P, NT, R, H])
        rz = sb("rz", [P, 2, banks, per_bank])
        ps_out = ctx.enter_context(nc.psum_tensor(tag + "ps_out", [P, banks, 512], F32))
        if turned:
            ps_outT = ctx.enter_context(nc.psum_tensor(tag + "ps_outT", [F + 1, 3, 512], F32))
            outT = hd.acc[1][0:F + 1]
        s_outT = sem("sumsT_copied")
        s_back = sem("sumsT_turned")
        s_k = sem("k_scaled")
        s_row = sem("row_in")
        s_ft = sem("ft_in")
        s_lg = sem("logit_made")
        s_exp = sem("exp_made")
        s_wt = sem("weight_made")
        s_wtd = sem("weight_direct")
        s_cf = sem("counts_float")
        s_pe = sem("step_summed")
        s_rz = sem("rz_made")
        s_raw = sem("sums_out")
        post = post_setup(ctx, s_raw)
        block = ctx.enter_context(nc.Block())

        def over_heads(eng, body):
            body(0, False, False, True)
            if H > 3:
                with eng.Fori(1, H - 2) as h:
                    body(h, True, True, True)
            body(H - 2, True, True, False)
            body(H - 1, True, False, False)

        @block.sync
        def _(sp):
            for u in range(H * R):
                h, r = divmod(u, R)
                if r == 0:
                    sp.wait_ge(hd.s_rows_out, h * 16 + 32)
                if u >= 2:
                    sp.wait_ge(s_lg, (u + 1) * UNIT)
                sp.dma_start(row[:, u % 2].rearrange("p c n -> p (c n)"),
                             rows[u:u + 1].broadcast_to([P, 2 * NP])).then_inc(s_row, 16)
                if u >= 2:
                    sp.wait_ge(s_pe, (u + 1) * UNIT)
                sp.dma_start(ft[:, u % 2], feat[h, r * NT:(r + 1) * NT].rearrange("s p f -> p s f")
                             ).then_inc(s_ft, 16)
                sp.wait_ge(s_ft, u * 16 + 16)
                sp.wait_ge(s_row, u * 16 + 16)
                if u == 0:
                    post.sync(sp, H)
                if r == 0 and h >= 2:
                    post.store(sp, h - 2)
            post.store(sp, H - 2)
            post.store(sp, H - 1)
            post.finish(sp, H)

        @block.vector
        def _(dve):
            dve.sem_inc(s_lg, T0)
            dve.sem_inc(s_raw, 1)
            scaled_k(dve, kq, H, k08, k02, s_k)
            dve.tensor_scalar(k02n[:], kq[:, :, :, H:2 * H], -SLOPE, None, ALU.mult).then_inc(s_k, 1)
            dve.wait_ge(s_k, 3)

            def sums_out(h):
                if turned:
                    dve.wait_ge(s_back, h + 1)
                else:
                    dve.wait_ge(s_pe, (h + 1) * R * UNIT + PE0)
                v = ps_out[:, :, 0:per_bank * (F + 1)].rearrange("p b (t f) -> p b t f", t=per_bank)
                dve.tensor_scalar(rz[:, 0], v[:, :, :, F], Z_EPS, None, post.guard).then_inc(s_rz, 1)
                dve.wait_ge(s_rz, h * 2 + 1)
                dve.reciprocal(rz[:, 1], rz[:, 0]).then_inc(s_rz, 1)
                post.before_sums(dve, h)
                dve.wait_ge(s_rz, h * 2 + 2)
                dve.tensor_tensor(post.y[:].rearrange("p (b t) f -> p b t f", b=banks), v[:, :, :, 0:F],
                                  rz[:, 1].rearrange("p b (t o) -> p b t o", o=1)
                                  .broadcast_to([P, banks, per_bank, F]), ALU.mult).then_inc(s_raw, 1)

            def body(h, pending_sums, pending_rows, maximum):
                for r in range(R):
                    u = h * R + r

                    def logits(s):
                        n = u * UNIT + s
                        dve.wait_ge(s_pe, n + 1 + PE0 - SLOTS)
                        if s == 0:
                            dve.wait_ge(s_row, u * 16 + 16)
                        slot = u % 2
                        a = row[:, bass.ds(slot, 1), 0, :].rearrange("p o n -> p (o n)")
                        b = row[:, bass.ds(slot, 1), 1, :].rearrange("p o n -> p (o n)")
                        dve.scalar_tensor_tensor(out=wt[:, s % SLOTS], in0=a, scalar=k08[:, s, r, bass.ds(h, 1)],
                                                 in1=b, op0=ALU.add, op1=ALU.max).then_inc(s_lg, 1)

                    logits(0)
                    for s in range(NT):
                        if s + 1 < NT:
                            logits(s + 1)
                        if s == 0 and (r > 0 and maximum or r == 0 and pending_rows):
                            hd.reduce_unit(dve, h + 2 if r > 0 else h + 1, (r - 1) % R)
                        if maximum:
                            n = hd.later_unit(h + 2, r) * NT + s
                            if not hd.all_miss:
                                dve.wait_ge(hd.s_later, n - 1) if s >= 2 or r > 0 else None
                                hd.mask(dve, r, s)
                                dve.wait_ge(hd.s_miss, (R + r) * NT + h * UNIT * R + s + 1)
                            if s == 0:
                                dve.wait_ge(hd.s_turn, hd.unit(h + 2, r) * 3)
                            hd.later_step(dve, h + 2, r, s)
                        if pending_rows and r == 0 and s < hd.ROW_PARTS - 1:
                            hd.rows_of_head(dve, h + 1, [s])
                        if pending_rows and r == 0 and s == hd.ROW_PARTS - 2:
                            hd.rows_of_head(dve, h + 1, [s + 1])
                        if s in direct:
                            dve.wait_ge(s_exp, u * exps_before[NT] + exps_before[s + 1])
                            dve.scalar_tensor_tensor(out=wt[:, s % SLOTS], in0=wt[:, s % SLOTS], scalar=1.0,
                                                     in1=ct[r][:, s, :], op0=ALU.min, op1=ALU.mult).then_inc(s_wtd, 1)
                        if r == 0 and s == (5 if turned else 2) and pending_sums:
                            sums_out(h - 1)
                        if r == R - 1 and s == NT - 1 and pending_sums:
                            post.vector(dve, h - 1)

            over_heads(dve, body)
            sums_out(H - 1)
            post.vector(dve, H - 1)

        @block.scalar
        def _(act):
            act.wait_ge(s_k, 3)

            def sumsT_out(h):
                act.wait_ge(s_pe, (h + 1) * UNIT + PE0)
                act.wait_ge(s_back, h)
                for i, (t0, nt) in enumerate(GROUPS):
                    act.copy(outT[:, t0 * P:(t0 + nt) * P], ps_outT[:, i, 0:nt * P]).then_inc(s_outT, 1)

            def body(h, pending_sums, pending_rows, maximum):
                for r in range(R):
                    for s in range(NT):
                        n = (h * R + r) * UNIT + s
                        if turned and s == 2 and pending_sums:
                            sumsT_out(h - 1)
                        if s in direct:
                            act.wait_ge(s_lg, n + 1 + T0)
                            act.activation(wt[:, s % SLOTS], wt[:, s % SLOTS], ACT.Exp,
                                           bias=k02[:, s, r, bass.ds(h, 1)]).then_inc(s_exp, 1)
                        else:
                            if cf is not None:
                                j = pool_before[s]
                                act.wait_ge(s_wt, (h * R + r) * ON_POOL + j - 1 + ON_POOL)
                                act.copy(cf[:, j % 2], ct[r][:, s, :]).then_inc(s_cf, 1)
                            act.wait_ge(s_lg, n + 1 + T0)
                            act.activation(wt[:, s % SLOTS], wt[:, s % SLOTS], ACT.Relu, scale=-1.0,
                                           bias=k02n[:, s, r, bass.ds(h, 1)]).then_inc(s_exp, 1)
                            act.wait_ge(s_exp, (h * R + r) * exps_before[NT] + exps_before[s] + 1)
                            act.activation(wt[:, s % SLOTS], wt[:, s % SLOTS], ACT.Exp, scale=-1.0).then_inc(s_exp, 1)
                        if r == 0 and s == 5 and pending_rows:
                            hd.rows_to_dram(act, h + 1)
                        if r == R - 1 and s == NT // 2 and pending_sums:
                            post.scalar(act, h - 1)

            over_heads(act, body)
            if turned:
                sumsT_out(H - 1)
            post.scalar(act, H - 1)
            act.wait_ge(hd.s_rows_out, 16 * H + 16)

        @block.tensor
        def _(pe):
            pe.sem_inc(s_pe, PE0)
            pe.sem_inc(s_outT, 3)

            def turn_back(h):
                pe.wait_ge(s_outT, h * 3 + 6)
                pe.wait_ge(s_raw, h + 1)
                for t in range(NT):
                    b, j = divmod(t, per_bank)
                    last = pe.transpose(ps_out[:, b, j * (F + 1):(j + 1) * (F + 1)], outT[:, t * P:(t + 1) * P],
                                        hd.ident[0:F + 1, 0:F + 1])
                last.then_inc(s_back, 1)

            def body(h, pending_sums, pending_rows, maximum, slot=None):
                for r in range(R):
                    u = h * R + r
                    for s in range(NT):
                        if s == TURN_STEP and maximum:
                            hd.turn_unit(pe, h + 2, r)
                        if s in direct:
                            pe.wait_ge(s_wtd, u * len(direct) + s // SLOTS + 1)
                        else:
                            pe.wait_ge(s_wt, u * ON_POOL + pool_before[s] + 1 + ON_POOL)
                        if turned:
                            if s == 0:
                                pe.wait_ge(s_ft, u * 16 + 16)
                                pe.wait_ge(s_outT, h * 3 + 3)
                            for i, (t0, nt) in enumerate(GROUPS):
                                last = pe.matmul(ps_outT[:, i, 0:nt * P], ft[:, slot, s, :],
                                                 wt[:, s % SLOTS, t0 * P:(t0 + nt) * P], start=(s == 0),
                                                 stop=(s == NT - 1), skip_group_check=True)
                            last.then_inc(s_pe, 1)
                            if s == 3 and pending_rows:
                                hd.turn_rows(pe, h + 1)
                            if s == 1 and pending_sums:
                                turn_back(h - 1)
                            continue
                        if s == 0:
                            pe.wait_ge(s_ft, u * 16 + 16)
                            if r == 0:
                                pe.wait_ge(s_raw, h + 1)
                        for t in range(NT):
                            b, j = divmod(t, per_bank)
                            last = pe.matmul(ps_out[:, b, j * (F + 1):(j + 1) * (F + 1)],
                                             wt[:, s % SLOTS, t * P:(t + 1) * P],
                                             ft[:, bass.ds(u % 2, 1), s, :].rearrange("p o f -> p (o f)"),
                                             start=(r == 0 and s == 0 and j == 0),
                                             stop=(r == R - 1 and s == NT - 1), skip_group_check=True)
                        last.then_inc(s_pe, 1)
                        if r == 0 and s == 3 and pending_rows:
                            hd.turn_rows(pe, h + 1)

            if turned:
                body(0, False, False, True, 0)
                with pe.Fori(0, (H - 4) // 2) as i:
                    body(i * 2 + 1, True, True, True, 1)
                    body(i * 2 + 2, True, True, True, 0)
                body(H - 3, True, True, True, 1)
                body(H - 2, True, True, False, 0)
                body(H - 1, True, False, False, 1)
                turn_back(H - 1)
            else:
                over_heads(pe, body)

        @block.gpsimd
        def _(pool):
            post.start_pool(pool)
            pool.sem_inc(s_wt, ON_POOL)
            for h in range(H):
                for r in range(R):
                    u = h * R + r
                    for s in range(NT):
                        if s not in direct:
                            counts = ct[r][:, s, :]
                            if cf is not None:
                                counts = cf[:, pool_before[s] % 2]
                                pool.wait_ge(s_cf, u * ON_POOL + pool_before[s] + 1)
                            pool.wait_ge(s_exp, u * exps_before[NT] + exps_before[s + 1])
                            pool.tensor_tensor(wt[:, s % SLOTS], wt[:, s % SLOTS], counts, ALU.mult
                                               ).then_inc(s_wt, 1)
                        if r == 0 and s == (6 if turned else NT // 2) and h >= 1:
                            post.pool(pool, h - 1)
            post.pool(pool, H - 1)


def relational_post(nc, g, b1, h2):
    H, F, NT = 4, g.D // 4, g.NT

    def setup(ctx, s_raw):
        sb = lambda n, s, d=F32: ctx.enter_context(nc.sbuf_tensor("r1" + n, s, d))
        sem = lambda n: ctx.enter_context(nc.semaphore("r1" + n))
        bias = sb("bias", [P, g.D])
        y = sb("y", [P, NT, F])
        e = sb("e", [P, NT, F])
        s_b = sem("bias_in")
        s_y = sem("y")
        s_e = sem("elu_exp")
        s_h = sem("elu")
        s_out = sem("h2_out")

        class Post:
            guard = ALU.add

            def sync(self, sp, H):
                sp.dma_start(bias[:], b1.rearrange("(o d) -> o d", o=1).broadcast_to([P, g.D])).then_inc(s_b, 16)
                sp.sem_inc(s_out, 16)

            def before_sums(self, dve, h):
                dve.wait_ge(s_out, h * 16 + 16)

            def scalar(self, act, h):
                act.wait_ge(s_y, h + 1)
                act.activation(e[:], y[:], ACT.Relu, scale=-1.0).then_inc(s_e, 1)
                act.wait_ge(s_e, h * 3 + 1)
                act.activation(e[:], e[:], ACT.Exp, scale=-1.0).then_inc(s_e, 1)
                act.activation(y[:], y[:], ACT.Relu).then_inc(s_e, 1)

            def vector(self, dve, h):
                dve.wait_ge(s_e, h * 3 + 3)
                dve.scalar_tensor_tensor(out=y[:], in0=e[:], scalar=-1.0, in1=y[:], op0=ALU.add,
                                         op1=ALU.add).then_inc(s_h, 1)

            def start_pool(self, pool):
                pool.wait_ge(s_b, 16)

            def pool(self, pool, h):
                bh = bias[:, h * F:(h + 1) * F].rearrange("p (o f) -> p o f", o=1).broadcast_to([P, NT, F])
                pool.wait_ge(s_raw, h + 2)
                pool.tensor_tensor(y[:], y[:], bh, ALU.add).then_inc(s_y, 1)

            def store(self, sp, h):
                sp.wait_ge(s_h, h + 1)
                sp.dma_start(h2[:, :, h * F:(h + 1) * F], y[:]).then_inc(s_out, 16)

            def finish(self, sp, H):
                sp.wait_ge(s_out, 16 * H + 16)

        post = Post()
        post.y = y
        return post

    return setup


def final_post(nc, g, x1, res, out):
    H, F, NT = 12, g.D // 12, g.NT

    def setup(ctx, s_raw):
        sb = lambda n, s, d=F32: ctx.enter_context(nc.sbuf_tensor("g1" + n, s, d))
        sem = lambda n: ctx.enter_context(nc.semaphore("g1" + n))
        y = sb("y", [P, NT, F])
        s_y = sem("y")
        s_h = sem("summed")
        s_out = sem("out")
        full = (NT - 1) * P

        class Post:
            guard = ALU.max

            def sync(self, sp, H):
                sp.sem_inc(s_out, 32)

            def before_sums(self, dve, h):
                dve.wait_ge(s_out, h * 32 + 32)

            def scalar(self, act, h):
                pass

            def vector(self, dve, h):
                dve.wait_ge(s_y, h + 1)
                dve.scalar_tensor_tensor(out=y[:], in0=y[:], scalar=0.0, in1=x1[:, :, bass.ds(h * F, F)],
                                         op0=ALU.max, op1=ALU.add).then_inc(s_h, 1)

            def start_pool(self, pool):
                pass

            def pool(self, pool, h):
                pool.wait_ge(s_raw, h + 2)
                pool.tensor_tensor(y[:], y[:], res[:, :, h * F:(h + 1) * F], ALU.add).then_inc(s_y, 1)

            def store(self, sp, h):
                sp.wait_ge(s_h, h + 1)
                sp.dma_start(out[0:full, h * F:(h + 1) * F].rearrange("(t p) d -> p t d", p=P),
                             y[:, 0:NT - 1, :]).then_inc(s_out, 16)
                sp.dma_start(out[full:g.N, h * F:(h + 1) * F], y[0:g.LAST, NT - 1, :]).then_inc(s_out, 16)

            def finish(self, sp, H):
                sp.wait_ge(s_out, 32 * H + 32)

        post = Post()
        post.y = y
        return post

    return setup


def second_logits(nc, g, ct, h2d, hh, hl, kq2, wqk2, ident, rows):
    NT, NP, KD, R, D = g.NT, g.NP, g.KD, g.R, g.D
    with ExitStack() as ctx:
        sb = lambda n, s, d=F32: ctx.enter_context(nc.sbuf_tensor("l2" + n, s, d))
        sem = lambda n: ctx.enter_context(nc.semaphore("l2" + n))
        hd = Heads(nc, ctx, g, "l2", 1, R, ct, kq2, ident, rows)
        hd.ps_turn = ctx.enter_context(nc.psum_tensor("l2ps_turn", [P, 3, 512], F32))
        h2 = sb("h2", [P, NT, D])
        h2T = sb("h2T", [P, KD, NP])
        ps_h = ctx.enter_context(nc.psum_tensor("l2ps_h", [P, 2, 512], F32))
        ps_kq = ctx.enter_context(nc.psum_tensor("l2ps_kq", [P, 512], F32))
        kT = hd.acc[1]
        chunk_banks = [hd.ps_turn[:, i] for i in range(3)]
        s_in = [sem(f"in{i}") for i in range(NT // 2)]
        s_hT = sem("hT")
        s_hT_out = sem("hT_out")
        s_kT = sem("kT")
        s_kT_out = sem("kT_out")
        s_kq = sem("kq")
        s_kq_out = sem("kq_out")
        s_hh = sem("hh")
        s_hl = sem("hl")
        block = ctx.enter_context(nc.Block())

        @block.sync
        def _(sp):
            for i in range(NT // 2):
                sp.dma_start(h2[:, 2 * i:2 * i + 2, :], h2d[:, 2 * i:2 * i + 2, :]).then_inc(s_in[i], 16)

        @block.gpsimd
        def _(pool):
            for t in range(NT):
                pool.wait_ge(s_hh, t + 1)
                pool.tensor_tensor(hl[:, t, :], h2[:, t, :], hh[:, t, :], ALU.subtract).then_inc(s_hl, 1)

        @block.tensor
        def _(pe):
            hd.start_tensor(pe)
            for n in range(2 * NT):
                t, half = divmod(n, 2)
                if n % 4 == 0:
                    pe.wait_ge(s_in[n // 4], 16)
                if n >= 2:
                    pe.wait_ge(s_hT_out, n - 1)
                for j in range(3):
                    kd = 3 * half + j
                    last = pe.transpose(ps_h[:, n % 2, j * P:(j + 1) * P], h2[:, t, kd * P:(kd + 1) * P], ident[:])
                last.then_inc(s_hT, 1)
                for i, (t0, nt) in enumerate(GROUPS):
                    if n == min(2 * (t0 + nt) + 1, 2 * NT - 1):
                        pe.wait_ge(s_hT_out, 2 * (t0 + nt))
                        logits_by_chunk(pe, lambda kd: wqk2[:, kd].rearrange("p r c -> p (r c)"), h2T, chunk_banks,
                                        i, 2 * R, s_kT)
            logits_back(pe, hd, kT, ps_kq, 2 * R, s_kT_out, s_kq)
            for r in range(R):
                hd.turn_unit(pe, 0, r)
            hd.turn_rows(pe, 0)

        @block.scalar
        def _(act):
            hd.start_scalar(act)
            for n in range(2 * NT):
                t, half = divmod(n, 2)
                act.wait_ge(s_hT, n + 1)
                act.copy(h2T[:, 3 * half:3 * half + 3, t * P:(t + 1) * P],
                         ps_h[:, n % 2, 0:3 * P].rearrange("p (k n) -> p k n", k=3)).then_inc(s_hT_out, 1)
                for i, (t0, nt) in enumerate(GROUPS):
                    if n == min(2 * (t0 + nt) + 3, 2 * NT - 1):
                        act.wait_ge(s_kT, i + 1)
                        act.copy(kT[0:2 * R, t0 * P:(t0 + nt) * P], chunk_banks[i][0:2 * R, 0:nt * P]
                                 ).then_inc(s_kT_out, 1)
            for t in range(NT):
                act.copy(hh[:, t, :], h2[:, t, :]).then_inc(s_hh, 1)
            hd.rows_to_dram(act, 0)
            act.wait_ge(hd.s_rows_out, 32)

        @block.vector
        def _(dve):
            hd.start_vector(dve)
            dve.wait_ge(s_kq, 3)
            dve.tensor_copy(kq2[:], ps_kq[:, 0:NT * 2 * R].rearrange("p (t r c) -> p t r c", t=NT, r=R)
                            ).then_inc(s_kq_out, 1)
            dve.wait_ge(s_kq_out, 1)
            for r in range(R):
                for s in range(NT):
                    hd.mask(dve, r, s)
                    dve.wait_ge(hd.s_miss, r * NT + s + 1)
                    hd.first_step(dve, 0, r, s)
                    if s == 3 and r > 0:
                        hd.reduce_unit(dve, 0, r - 1)
            hd.reduce_unit(dve, 0, R - 1)
            hd.rows_of_head(dve, 0)


def second_layer(nc, g, ct, hh, hl, kq2, rows, W2, b2, x, x1, mv):
    NT, NP, KD, R, D = g.NT, g.NP, g.KD, g.R, g.D
    TG = 2
    W = TG * P
    NG = NT // TG
    RING = 5
    full = (NT - 1) * P
    with ExitStack() as ctx:
        sb = lambda n, s, d=F32: ctx.enter_context(nc.sbuf_tensor("m2" + n, s, d))
        sem = lambda n: ctx.enter_context(nc.semaphore("m2" + n))
        w = sb("w", [P, R, KD, D])
        row = sb("row", [P, 2 * R, W])
        wt = sb("wt", [P, RING, W])
        wh = sb("wh", [P, RING, W], F16)
        wl = sb("wl", [P, RING, W], F16)
        k08 = sb("k08", [P, NT, R, 1])
        k02 = sb("k02", [P, NT, R, 1])
        gT = sb("gT", [P, R, KD, W])
        zsum = sb("zsum", [P, W])
        ones = sb("ones", [P, 1])
        none = sb("none", [P, 1])
        rz = sb("rz", [P, 2])
        bias = sb("bias", [P, D])
        xt = sb("xt", [P, 2, D])
        stats = sb("stats", [P, 2, 6])
        ps_g = ctx.enter_context(nc.psum_tensor("m2ps_g", [P, 2, 3, 512], F32))
        ps_o = ctx.enter_context(nc.psum_tensor("m2ps_o", [P, 2, 512], F32))
        o_banks = [ps_o, ps_g[:, 1, 0:2]]
        s_k = sem("k")
        s_one = sem("one")
        s_w = sem("w")
        s_b = sem("b")
        s_row = sem("row")
        s_x = [sem("x0"), sem("x1")]
        s_lg = sem("lg")
        s_exp = sem("exp")
        s_wt = sem("wt")
        s_hi = sem("hi")
        s_lo = sem("lo")
        s_pe = sem("pe")
        s_z = sem("z")
        s_g = sem("g")
        s_o = sem("o")
        s_rz = sem("rz")
        s_o_out = sem("o_out")
        s_stat = sem("stat")
        s_sum = sem("sum_rel")
        s_st = [sem("st0"), sem("st1")]
        block = ctx.enter_context(nc.Block())
        U = R * NT

        @block.sync
        def _(sp):
            rv = rows.rearrange("r (c n) -> (r c) n", c=2)

            def load_rows(gr):
                sp.wait_ge(s_lg, (gr + 1) * U)
                sp.dma_start(row[:],
                             rv[:, bass.ds(gr * W, W)].rearrange("(o c) n -> o c n", o=1)
                             .broadcast_to([P, 2 * R, W])).then_inc(s_row, 16)
                sp.wait_ge(s_row, (gr + 1) * 16)

            load_rows(0)
            sp.dma_start(bias[:], b2.rearrange("(o d) -> o d", o=1).broadcast_to([P, D])).then_inc(s_b, 16)
            for r in range(R):
                sp.dma_start(w[:, r], W2[r].rearrange("(k p) f -> p k f", p=P)).then_inc(s_w, 16)
            sp.wait_ge(s_one, 3)
            for gr in range(NG):
                if gr + 1 < NG:
                    load_rows(gr + 1)
                for j in range(TG):
                    t = gr * TG + j
                    if gr >= 1:
                        sp.wait_ge(s_st[j], 16 * gr)
                        sp.wait_ge(s_stat, 3 * (t - TG + 1))
                    if t < NT - 1:
                        sp.dma_start(xt[:, j, :], x[t * P:(t + 1) * P, :]).then_inc(s_x[j], 16)
                    else:
                        sp.wait_ge(s_o_out, 3)
                        sp.dma_start(xt[0:g.LAST, j, :], x[full:g.N, :]).then_inc(s_x[j], 16)
                if gr >= 0:
                    for j in range(TG):
                        t = gr * TG + j
                        sp.wait_ge(s_o_out, 3 * (t + 1))
                        sp.dma_start(x1[:, t, :], xt[:, j, :]).then_inc(s_st[j], 16)
            for j in range(TG):
                sp.wait_ge(s_st[j], 16 * NG)

        @block.gpsimd
        def _(pool):
            pool.memset(ones[:], 1.0).then_inc(s_one, 1)
            pool.memset(none[:], 0.0).then_inc(s_one, 1)
            pool.memset(xt[:], 0.0).then_inc(s_one, 1)
            pool.sem_inc(s_z, RING)
            pool.wait_ge(s_one, 3)
            with pool.Fori(0, NG) as gr:
                for r in range(R):
                    for s in range(NT):
                        n = gr * U + r * NT + s
                        pool.wait_ge(s_wt, n + 1)
                        if r == 0 and s == 0:
                            pool.wait_ge(s_o, gr * TG + 1)
                            pool.tensor_tensor(zsum[:], wt[:, s % RING], none[:].broadcast_to([P, W]), ALU.add).then_inc(s_z, 1)
                        else:
                            pool.wait_ge(s_z, n + RING)
                            pool.tensor_tensor(zsum[:], zsum[:], wt[:, s % RING], ALU.add).then_inc(s_z, 1)

        @block.vector
        def _(dve):
            dve.sem_inc(s_lg, U)
            dve.sem_inc(s_lo, RING)
            scaled_k(dve, kq2, 1, k08, k02, s_k)
            dve.wait_ge(s_k, 2)
            dve.wait_ge(s_b, 16)

            def steps(gr):
                dve.wait_ge(s_row, gr * 16 + 16)

                def logits(m):
                    n = gr * U + m
                    r, s = divmod(m, NT)
                    dve.wait_ge(s_hi, n + 1)
                    dve.wait_ge(s_lo, n + 1)
                    dve.wait_ge(s_z, n + 1)
                    dve.scalar_tensor_tensor(out=wt[:, s % RING], in0=row[:, 2 * r, :], scalar=k08[:, s, r, :],
                                             in1=row[:, 2 * r + 1, :], op0=ALU.add,
                                             op1=ALU.max).then_inc(s_lg, 1)

                def weights(m):
                    n = gr * U + m
                    r, s = divmod(m, NT)
                    dve.wait_ge(s_exp, n + 1)
                    dve.scalar_tensor_tensor(out=wt[:, s % RING], in0=wt[:, s % RING], scalar=1.0,
                                             in1=ct[r][:, s, bass.ds(gr * W, W)], op0=ALU.min,
                                             op1=ALU.mult).then_inc(s_wt, 1)

                def low(m):
                    n = gr * U + m
                    dve.wait_ge(s_hi, n + 1 + RING)
                    dve.wait_ge(s_pe, n + 1)
                    dve.tensor_tensor(wl[:, m % RING], wt[:, m % RING], wh[:, m % RING], ALU.subtract
                                      ).then_inc(s_lo, 1)

                for part in (logits, weights, low):
                    for m in range(RING):
                        part(m)
                if gr >= 1:
                    outputs(gr - 1)
                for m in range(RING, U + 4):
                    if m < U:
                        logits(m)
                    if RING <= m - 2 < U:
                        weights(m - 2)
                    if RING <= m - 4:
                        low(m - 4)

            def outputs(gr):
                for j in range(TG):
                    t = gr * TG + j
                    dve.wait_ge(s_o, t + 2)
                    dve.wait_ge(s_stat, 3 * t) if t else None
                    dve.tensor_scalar(rz[:, 0:1], o_banks[j][:, 1, D // 2:D // 2 + 1], Z_EPS, None, ALU.add).then_inc(s_rz, 1)
                    dve.wait_ge(s_rz, 2 * t + 1)
                    dve.reciprocal(rz[:, 1:2], rz[:, 0:1]).then_inc(s_rz, 1)
                    dve.wait_ge(s_x[j], 16 * (gr + 1))
                    dve.tensor_tensor(xt[:, j, :], xt[:, j, :], bias[:], ALU.add).then_inc(s_o_out, 1)
                    dve.wait_ge(s_rz, 2 * t + 2)
                    dve.wait_ge(s_o_out, 3 * t + 1)
                    for half in range(2):
                        c = slice(half * D // 2, (half + 1) * D // 2)
                        dve.scalar_tensor_tensor(out=xt[:, j, c], in0=o_banks[j][:, half, 0:D // 2], scalar=rz[:, 1:2],
                                                 in1=xt[:, j, c], op0=ALU.mult, op1=ALU.add).then_inc(s_o_out, 1)
                    for half in range(2):
                        dve.wait_ge(s_o_out, 3 * t + 2 + half)
                        dve.bn_stats(stats[:, half, :], xt[:, j, half * D // 2:(half + 1) * D // 2]).then_inc(s_stat, 1)
                    dve.wait_ge(s_stat, 3 * t + 2)
                    dve.bn_aggr(mv[:, t, :], stats[:]).then_inc(s_stat, 1)

            def sum_relations(gr):
                c = slice(gr * W, (gr + 1) * W)
                for r in range(R - 1):
                    if r == 0:
                        dve.wait_ge(s_wt, (gr + 1) * U)
                    else:
                        dve.wait_ge(s_sum, (R - 1) * gr + r)
                    dve.tensor_tensor(ct[R - 1][:, :, c], ct[R - 1][:, :, c], ct[r][:, :, c], ALU.add
                                      ).then_inc(s_sum, 1)

            for gr in range(NG):
                steps(gr)
                sum_relations(gr)
            outputs(NG - 1)

        @block.scalar
        def _(act):
            act.wait_ge(s_k, 2)

            def evac(gr, r):
                act.wait_ge(s_pe, RING + gr * U + (r + 1) * NT)
                for b in range(3):
                    act.copy(gT[:, r, 2 * b:2 * b + 2, :],
                             ps_g[:, r % 2, b, 0:2 * W].rearrange("p (k n) -> p k n", k=2)).then_inc(s_g, 1)

            act.sem_inc(s_hi, RING)
            for gr in range(NG):
                def exponential(m):
                    r, s = divmod(m, NT)
                    act.wait_ge(s_lg, gr * U + m + 1 + U)
                    act.activation(wt[:, s % RING], wt[:, s % RING], ACT.Exp, bias=k02[:, s, r, :]).then_inc(s_exp, 1)

                def high(m):
                    act.wait_ge(s_wt, gr * U + m + 1)
                    act.wait_ge(s_pe, gr * U + m + 1)
                    act.copy(wh[:, m % RING], wt[:, m % RING]).then_inc(s_hi, 1)

                for part in (exponential, high):
                    for m in range(RING):
                        part(m)
                for m in range(RING, U + 2):
                    r, s = divmod(m, NT)
                    if m < U:
                        exponential(m)
                    if RING <= m - 2:
                        high(m - 2)
                    if s == 6 and 0 < r < R:
                        evac(gr, r - 1)
                evac(gr, R - 1)

        @block.tensor
        def _(pe):
            pe.sem_inc(s_pe, RING)
            pe.sem_inc(s_o, 1)
            for gr in range(NG):
                for r in range(R):
                    u = gr * R + r
                    for s in range(NT):
                        pe.wait_ge(s_lo, gr * U + r * NT + s + 1 + RING)
                        if s == 0 and u >= 2:
                            pe.wait_ge(s_g, 3 * u if r == 0 else 3 * (u - 1))
                        if s == 0 and r == 1 and gr >= 1:
                            pe.wait_ge(s_o_out, 3 * TG * gr)
                        for f in range(KD):
                            for i, (a, b) in enumerate(((hh, wh), (hh, wl), (hl, wh))):
                                last = pe.matmul(ps_g[:, r % 2, f // 2, (f % 2) * W:(f % 2 + 1) * W],
                                                 a[:, s, f * P:(f + 1) * P], b[:, s % RING],
                                                 start=(s == 0 and f % 2 == 0 and i == 0),
                                                 stop=(s == NT - 1 and i == 2), skip_group_check=True)
                        last.then_inc(s_pe, 1)
                pe.wait_ge(s_w, 16 * R)
                pe.wait_ge(s_one, 3)
                for j in range(TG):
                    t = gr * TG + j
                    if t >= 2:
                        pe.wait_ge(s_o_out, 3 * (t - 1))
                    for half in range(2):
                        for i in range(R * KD):
                            r, kd = divmod(i, KD)
                            if j == 0 and half == 0 and kd == 0:
                                pe.wait_ge(s_g, 3 * (R * gr + r + 1))
                            last = pe.matmul(o_banks[j][:, half, 0:D // 2], gT[:, r, kd, j * P:(j + 1) * P],
                                             w[:, r, kd, half * D // 2:(half + 1) * D // 2], start=(i == 0),
                                             stop=(i == R * KD - 1), skip_group_check=True)
                    pe.wait_ge(s_z, RING + (gr + 1) * U)
                    pe.matmul(o_banks[j][:, 1, D // 2:D // 2 + 1], zsum[:, j * P:(j + 1) * P], ones[:], start=False,
                              stop=True, skip_group_check=True).then_inc(s_o, 1)


def third_tables(nc, g, ct, total, hd, x1d, x1, mv, res, kq3, feat3, Wg, al, ar, Wres, ident):
    NT, NP, KD, D = g.NT, g.NP, g.KD, g.D
    H, F = 12, D // 12
    with ExitStack() as ctx:
        sb = lambda n, s, d=F32: ctx.enter_context(nc.sbuf_tensor("t3" + n, s, d))
        sem = lambda n: ctx.enter_context(nc.semaphore("t3" + n))
        h = res
        hT = sb("hT", [P, KD, NP])
        std = sb("std", [P, NT])
        rstd = sb("rstd", [P, NT])
        shift = sb("shift", [P, NT])
        eps = sb("eps", [P, 1])
        wd = sb("wd", [F, 2, 2, F])
        att = sb("att", [2 * H, F])
        attT = sb("attT", [F, 2 * H])
        wbd = sb("wbd", [P, 2, P])
        wa = sb("wa", [P, 2 * H])
        wabd = sb("wabd", [P, KD, 2 * H])
        stage = sb("stage", [P, 2, H, F + 1])
        ps_turn = ctx.enter_context(nc.psum_tensor("t3ps_turn", [P, 3, 512], F32))
        hd.ps_turn = ps_turn
        ps_f = ctx.enter_context(nc.psum_tensor("t3ps_f", [P, 2, 2, 512], F32))
        kT = hd.acc[1]
        chunk_banks = [ps_f[:, i // 2, i % 2] for i in range(3)]
        ps_s = ctx.enter_context(nc.psum_tensor("t3ps_s", [P, 512], F32))
        s_const = sem("const")
        s_x = [sem(f"x{i}") for i in range(NT // 2)]
        s_wd = sem("wd")
        s_norm = sem("norm")
        s_total = sem("total")
        s_h = sem("h_made")
        s_turn = sem("turn")
        s_turned = sem("turned")
        s_prep = sem("prep")
        s_prep_out = sem("prep_out")
        s_f = sem("f")
        s_f_out = sem("f_out")
        s_kT = sem("kT")
        s_kT_out = sem("kT_out")
        s_kq = sem("kq")
        s_spill = [sem("spill0"), sem("spill1")]
        block = ctx.enter_context(nc.Block())

        @block.sync
        def _(sp):
            for i in range(NT // 2):
                sp.dma_start(x1[:, 2 * i:2 * i + 2, :], x1d[:, 2 * i:2 * i + 2, :]).then_inc(s_x[i], 16)
            for i, m in enumerate((Wg, Wres)):
                for c in range(2):
                    sp.dma_start(wd[:, i, c, :], m).then_inc(s_wd, 16)
            for i, m in enumerate((al, ar)):
                sp.dma_start(att[i * H:(i + 1) * H, :], m.rearrange("o h f -> (o h) f")).then_inc(s_wd, 16)

        @block.gpsimd
        def _(pool):
            pool.memset(eps[:], LN_EPS).then_inc(s_const, 1)
            pool.memset(wbd[:], 0.0).then_inc(s_const, 1)
            pool.memset(wabd[:], 0.0).then_inc(s_const, 1)
            pool.memset(stage[:], 1.0).then_inc(s_const, 1)

        @block.tensor
        def _(pe):
            hd.start_tensor(pe)
            pe.wait_ge(s_wd, 96)
            for i in range(2):
                last = pe.transpose(ps_s[:, i * F:(i + 1) * F], wd[:, i].rearrange("o c d -> o (c d)"), ident[0:F, 0:F])
            last = pe.transpose(ps_s[0:F, P:P + 2 * H], att[:], ident[0:2 * H, 0:2 * H])
            last.then_inc(s_prep, 1)
            pe.wait_ge(s_prep_out, 5)
            pe.matmul(ps_s[:, 0:2 * H], wd[:, 0].rearrange("o c d -> o (c d)"), attT[:], start=True,
                      stop=True).then_inc(s_prep, 1)
            for n in range(2 * NT):
                t, half = divmod(n, 2)
                pe.wait_ge(s_h, t + 1)
                if n >= 2:
                    pe.wait_ge(s_turned, n - 1)
                for j in range(3):
                    kd = 3 * half + j
                    last = pe.transpose(ps_turn[:, n % 2, j * P:(j + 1) * P], h[:, t, kd * P:(kd + 1) * P], ident[:])
                last.then_inc(s_turn, 1)
                for i, (t0, nt) in enumerate(GROUPS):
                    if n == min(2 * (t0 + nt) + 1, 2 * NT - 1):
                        pe.wait_ge(s_turned, 2 * (t0 + nt))
                        pe.wait_ge(s_prep_out, 6 + 2 * KD)
                        logits_by_chunk(pe, lambda kd: wabd[:, kd, :], hT, chunk_banks, i, 2 * H, s_kT)
            logits_back(pe, hd, kT, ps_s, 2 * H, s_kT_out, s_kq)
            for n in range(2 * NT):
                i, t = divmod(n, NT)
                if n >= 2:
                    pe.wait_ge(s_f_out, 2 * (n - 1))
                for kd in range(KD):
                    b, j = divmod(kd, 3)
                    last = pe.matmul(ps_f[:, n % 2, b, j * P:(j + 1) * P], hT[:, kd, t * P:(t + 1) * P], wbd[:, i, :],
                                     start=(j == 0), stop=True, skip_group_check=True)
                last.then_inc(s_f, 1)
                if n == 2 * NT - 6:
                    for j in range(2):
                        hd.turn_unit(pe, j, 0)
                if n == 2 * NT - 3:
                    hd.turn_rows(pe, 0)
            hd.turn_rows(pe, 1)

        @block.vector
        def _(dve):
            hd.start_vector(dve)
            dve.wait_ge(s_norm, 1)
            dve.reciprocal(rstd[:], std[:]).then_inc(s_norm, 1)
            dve.wait_ge(s_norm, 2)
            dve.scalar_tensor_tensor(out=shift[:], in0=mv[:, :, 0], scalar=-1.0, in1=rstd[:],
                                     op0=ALU.mult, op1=ALU.mult).then_inc(s_norm, 1)
            for s in range(NT):
                dve.tensor_copy(total[:, s, :], ct[:, s, :]).then_inc(s_total, 1)
            dve.wait_ge(s_prep, 1)
            dve.wait_ge(s_const, 4)
            for i in range(2):
                for c in range(2):
                    dve.tensor_copy(wbd[c * F:(c + 1) * F, i, c * F:(c + 1) * F],
                                    ps_s[c * F:(c + 1) * F, i * F:(i + 1) * F]).then_inc(s_prep_out, 1)
            dve.tensor_copy(attT[:], ps_s[0:F, P:P + 2 * H]).then_inc(s_prep_out, 1)
            dve.wait_ge(s_prep, 2)
            dve.tensor_copy(wa[:], ps_s[:, 0:2 * H]).then_inc(s_prep_out, 1)
            dve.wait_ge(s_prep_out, 6)
            for kd in range(KD):
                for c in range(2):
                    hh = 2 * kd + c
                    p = slice(c * F, (c + 1) * F)
                    dve.tensor_copy(wabd[p, kd, hh:hh + H + 1:H], wa[p, hh:hh + H + 1:H]).then_inc(s_prep_out, 1)
            for s in range(NT):
                dve.wait_ge(s_total, s + 1)
                hd.mask(dve, 0, s)
            dve.wait_ge(s_kq, 3)
            v = ps_s[:, 0:NT * 2 * H].rearrange("p (t c) -> p t c", t=NT)
            dve.tensor_copy(kq3[:, :, 0, H:2 * H], v[:, :, 0:H]).then_inc(s_prep_out, 1)
            dve.tensor_copy(kq3[:, :, 0, 0:H], v[:, :, H:2 * H]).then_inc(s_prep_out, 1)
            dve.wait_ge(s_prep_out, 8 + 2 * KD)
            dve.wait_ge(hd.s_miss, NT)
            for s in range(NT):
                for j in range(2):
                    hd.first_step(dve, j, 0, s)
            for j in range(2):
                hd.reduce_unit(dve, j, 0)
            for j in range(2):
                hd.rows_of_head(dve, j)

        @block.scalar
        def _(act):
            hd.start_scalar(act)
            act.wait_ge(s_const, 1)
            act.activation(std[:], mv[:, :, 1], ACT.Sqrt, bias=eps[:]).then_inc(s_norm, 1)
            act.wait_ge(s_const, 4)
            act.wait_ge(s_norm, 3)
            act.wait_ge(s_total, NT)
            for t in range(NT):
                act.wait_ge(s_x[t // 2], 16)
                act.activation(h[:, t, :], x1[:, t, :], ACT.Relu, bias=shift[:, t:t + 1],
                               scale=rstd[:, t:t + 1]).then_inc(s_h, 1)
            for n in range(2 * NT):
                t, half = divmod(n, 2)
                act.wait_ge(s_turn, n + 1)
                act.copy(hT[:, 3 * half:3 * half + 3, t * P:(t + 1) * P],
                         ps_turn[:, n % 2, 0:3 * P].rearrange("p (k n) -> p k n", k=3)).then_inc(s_turned, 1)
                for i, (t0, nt) in enumerate(GROUPS):
                    if n == min(2 * (t0 + nt) + 3, 2 * NT - 1):
                        act.wait_ge(s_kT, i + 1)
                        act.copy(kT[0:2 * H, t0 * P:(t0 + nt) * P], chunk_banks[i][0:2 * H, 0:nt * P]
                                 ).then_inc(s_kT_out, 1)
            for n in range(2 * NT):
                i, t = divmod(n, NT)
                act.wait_ge(s_f, n + 1)
                if i == 0 and t >= 2:
                    act.wait_ge(s_spill[t % 2], 16 * (t // 2))
                for b in range(2):
                    v = ps_f[:, n % 2, b, 0:3 * P]
                    if i == 0:
                        act.copy(stage[:, t % 2, 6 * b:6 * b + 6, 0:F],
                                 v.rearrange("p (a f) -> p a f", f=F)).then_inc(s_f_out, 1)
                    else:
                        act.copy(res[:, t, b * 3 * P:(b + 1) * 3 * P], v).then_inc(s_f_out, 1)
                if i == 0:
                    act.wait_ge(s_f_out, 2 * (n + 1))
                    act.dma_start(feat3[:, t].rearrange("h p f -> p h f"), stage[:, t % 2]).then_inc(s_spill[t % 2], 16)
                if n == 2 * NT - 2:
                    hd.rows_to_dram(act, 0)
            hd.rows_to_dram(act, 1)
            for q in range(2):
                act.wait_ge(s_spill[q], 16 * NT // 2)


def gnn_kernel(nc, x, src, dst, etype, W1, q1, k1, b1, W2, q2, k2, b2, Wg, al, ar, Wres, out):
    g = Graph(x, src)
    NT, NP, R, D = g.NT, g.NP, g.R, g.D
    H1, F1, H3, F3 = 4, D // 4, 12, D // 12
    dram = lambda n, s, d=F32: nc.dram_tensor(n, s, d, kind="Internal").ap()
    counts = [dram(f"counts{i}", [R * NP * NP, 1], U16) for i in range(TABLES)]
    feat1 = dram("feat1", [H1, R * NT, P, F1 + 1])
    feat3 = dram("feat3", [H3, NT, P, F3 + 1])
    rows1 = dram("rows1", [H1 * R, 2 * NP])
    rows2 = dram("rows2", [R, 2 * NP])
    rows3 = dram("rows3", [H3, 2 * NP])
    h2d = dram("h2d", [P, NT, D])
    x1d = dram("x1d", [P, NT, D])
    with ExitStack() as ctx:
        sb = lambda c, n, s, d=F32: c.enter_context(nc.sbuf_tensor(n, s, d))
        ident = sb(ctx, "ident", [P, P])
        ct_all = sb(ctx, "ct_all", [P, R * NT * NP], U16)
        ct = [ct_all[:, r * NT * NP:(r + 1) * NT * NP].rearrange("p (t n) -> p t n", t=NT) for r in range(R)]
        mv1 = sb(ctx, "mv1", [P, NT, 2])
        with ExitStack() as inner:
            wqk2 = sb(inner, "wqk2", [P, g.KD, R, 2])
            with ExitStack() as first:
                kq1 = sb(first, "kq1", [P, NT, R, 2 * H1])
                hd = Heads(nc, first, g, "h1", H1, R, ct, kq1, ident, rows1)
                tables_and_counts(nc, g, x, src, dst, etype, W1, q1, k1, W2, q2, k2, ident, hd, kq1, wqk2, feat1,
                                  counts, ct_all)
                multi_head(nc, g, "h1", hd, F1, feat1, relational_post(nc, g, b1, h2d))
            kq2 = sb(inner, "kq2", [P, NT, R, 2])
            hh = sb(inner, "hh", [P, NT, D], F16)
            hl = sb(inner, "hl", [P, NT, D], F16)
            second_logits(nc, g, ct, h2d, hh, hl, kq2, wqk2, ident, rows2)
            second_layer(nc, g, ct, hh, hl, kq2, rows2, W2, b2, x, x1d, mv1)
        total = sb(ctx, "total", [P, NT, NP])
        kq3 = sb(ctx, "kq3", [P, NT, 1, 2 * H3])
        spare = ct_all[:].bitcast(F32)
        x1 = spare[:, 0:NT * D].rearrange("p (t d) -> p t d", t=NT)
        res = spare[:, NT * D:2 * NT * D].rearrange("p (t d) -> p t d", t=NT)
        space = spare[:, 2 * NT * D:2 * NT * D + 3 * NP].rearrange("p (a n) -> p a n", a=3)
        hd = Heads(nc, ctx, g, "h3", H3, 1, [total], kq3, ident, rows3, space)
        third_tables(nc, g, ct[R - 1], total, hd, x1d, x1, mv1, res, kq3, feat3, Wg, al, ar, Wres, ident)
        multi_head(nc, g, "h3", hd, F3, feat3, final_post(nc, g, x1, res, out))


_INS = ['x', 'src', 'dst', 'edge_type_3', 'L0_gnn_W1', 'L0_gnn_q1', 'L0_gnn_k1', 'L0_gnn_b1', 'L0_gnn_W2', 'L0_gnn_q2',
        'L0_gnn_k2', 'L0_gnn_b2', 'L1_gnn_W', 'L1_gnn_attn_l', 'L1_gnn_attn_r', 'L1_gnn_W_res']


def kernel(**inputs):
    import numpy as _np
    import concourse.bacc as _bacc
    from concourse import mybir as _mybir
    from concourse.bass_utils import run_bass_kernel_spmd as _run

    nc = _bacc.Bacc("TRN2", target_bir_lowering=False, num_devices=1)
    arrays, args = {}, []
    for name in _INS:
        a = _np.ascontiguousarray(inputs[name])
        arrays[f"in_{name}_dram"] = a
        args.append(nc.dram_tensor(f"in_{name}_dram", a.shape, _mybir.dt.from_np(a.dtype), kind="ExternalInput").ap())
    out = nc.dram_tensor("out_0_dram", tuple(inputs['x'].shape), _mybir.dt.float32, kind="ExternalOutput").ap()
    gnn_kernel(nc, *args, out)
    r = _run(nc, [arrays], core_ids=[0])
    return r.results[0]["out_0_dram"]
```
